# Optimizing a Trainium2 kernel written in Bass

```python
import numpy as np
import jax
import jax.numpy as jnp

def _softmax(x, axis=-1):
    return jax.nn.softmax(x, axis=axis)

def _gelu(x):
    return jax.nn.gelu(x, approximate=True)

def _silu(x):
    return jax.nn.silu(x)

def _sigmoid(x):
    return jax.nn.sigmoid(x)

def _layernorm(x, axis=-1, eps=1e-05):
    m = jnp.mean(x, axis=axis, keepdims=True)
    v = jnp.var(x, axis=axis, keepdims=True)
    return (x - m) / jnp.sqrt(v + eps)

def _scatter_add(tgt, idx, src, axis=0):
    return tgt.at[idx].add(src)

def _segment_sum(src, seg, n):
    return jax.ops.segment_sum(src, seg, n)
kernel_name = 'mk_adaln_d1_jaxref_r8_1b6c1e'

def setup_inputs(seed: int=0):
    np.random.seed(seed)
    _w = jnp.asarray

    def _L0_attn_setup():
        import jax, jax.numpy as jnp
        import numpy as np
        D_MODEL = 128
        EXPAND = 2
        D_INNER = EXPAND * D_MODEL
        D_STATE = 16
        DT_RANK = (D_MODEL + 15) // 16
        EPS = 1e-05
        FP_ITERS = 8
        STEP = 0.99
        B_SZ, L_SEQ = (2, 256)

        def _shift1(y):
            return jnp.pad(y, ((0, 0), (1, 0), (0, 0)))[:, :-1, :]

        def _selective_scan(u, delta, A, Bm, Cm, D):

            def step(h, inp):
                dt_t, u_t, b_t, c_t = inp
                h = jnp.exp(dt_t[:, :, None] * A) * h + (dt_t * u_t)[:, :, None] * b_t[:, None, :]
                y = jnp.einsum('bdn,bn->bd', h, c_t) + D * u_t
                return (h, y)
            b, l, d = u.shape
            h0 = jnp.zeros((b, d, A.shape[1]), u.dtype)
            xs = tuple((jnp.moveaxis(a, 1, 0) for a in (delta, u, Bm, Cm)))
            _, ys = jax.lax.scan(step, h0, xs)
            return jnp.moveaxis(ys, 0, 1)
        key = jax.random.key(seed)
        ks = jax.random.split(key, 12)
        f32 = jnp.float32
        hidden_states = jax.random.normal(ks[0], (B_SZ, L_SEQ, D_MODEL), f32)
        W_in = jax.random.normal(ks[1], (2 * D_INNER, D_MODEL), f32) * D_MODEL ** (-0.5)
        W_x = jax.random.normal(ks[2], (DT_RANK + 2 * D_STATE, D_INNER), f32) * D_INNER ** (-0.5)
        W_dt = jax.random.uniform(ks[3], (D_INNER, DT_RANK), f32, -DT_RANK ** (-0.5), DT_RANK ** (-0.5))
        dt = jnp.exp(jax.random.uniform(ks[4], (D_INNER,), f32) * (np.log(0.1) - np.log(0.001)) + np.log(0.001))
        dt = jnp.clip(dt, 0.0001)
        b_dt = dt + jnp.log(-jnp.expm1(-dt))
        A_log = jnp.log(jnp.tile(jnp.arange(1, D_STATE + 1, dtype=f32)[None, :], (D_INNER, 1)))
        W_bc = jax.random.normal(ks[5], (2 * D_STATE, D_INNER), f32) * D_INNER ** (-0.5)
        W_zy = jax.random.normal(ks[6], (D_INNER, D_INNER), f32) * D_INNER ** (-0.5)
        W_mix = jax.random.normal(ks[7], (D_INNER, D_INNER), f32) * D_INNER ** (-0.5)
        D = jnp.ones((D_INNER,), f32)
        ln_gamma = jnp.ones((D_INNER,), f32)
        ln_beta = jnp.zeros((D_INNER,), f32)
        W_out = jax.random.normal(ks[8], (D_MODEL, D_INNER), f32) * D_INNER ** (-0.5)
        return dict(hidden_states=hidden_states, W_in=W_in, W_x=W_x, W_dt=W_dt, b_dt=b_dt, A_log=A_log, W_bc=W_bc, W_zy=W_zy, W_mix=W_mix, D=D, ln_gamma=ln_gamma, ln_beta=ln_beta, W_out=W_out)
    _L0_attn_in = _L0_attn_setup()

    def _L0_ffn_setup():
        import jax, jax.numpy as jnp
        import numpy as np
        D = 128
        E = 12
        HS = 2 * D
        HR = 3 * D
        TAU = 1.5

        def _geglu(h):
            a, g = jnp.split(h, 2, axis=-1)
            return a * jax.nn.gelu(g, approximate=False)
        key = jax.random.key(seed)
        ks = jax.random.split(key, 12)

        def xavier(k, shape):
            fan_in, fan_out = (shape[-2], shape[-1])
            lim = jnp.sqrt(6.0 / (fan_in + fan_out))
            return jax.random.uniform(k, shape, jnp.float32, -lim, lim)
        x = jax.random.normal(ks[0], (2, 128, D), jnp.float32)
        Ws1 = xavier(ks[1], (D, 2 * HS))
        bs1 = jnp.zeros((2 * HS,), jnp.float32)
        Ws2 = xavier(ks[2], (HS, D))
        bs2 = jnp.zeros((D,), jnp.float32)
        We1 = xavier(ks[3], (E, D, 2 * HR))
        be1 = jnp.zeros((E, 2 * HR), jnp.float32)
        We2 = xavier(ks[4], (E, HR, D))
        be2 = jnp.zeros((E, D), jnp.float32)
        Wr = xavier(ks[5], (D, E))
        br = jnp.zeros((E,), jnp.float32)
        return {'x': x, 'Ws1': Ws1, 'bs1': bs1, 'Ws2': Ws2, 'bs2': bs2, 'We1': We1, 'be1': be1, 'We2': We2, 'be2': be2, 'Wr': Wr, 'br': br}
    _L0_ffn_in = _L0_ffn_setup()
    _L0_c = _w((lambda *s: np.random.randn(*s).astype(np.float32) * 0.05)(2, 128))
    _L0_wmod = _w((lambda *s: np.random.randn(*s).astype(np.float32) * 0.05)(128, 6 * 128) * 128 ** (-0.5))
    _d = {'L0_attn_hidden_states': _L0_attn_in['hidden_states'], 'L0_attn_W_in': _L0_attn_in['W_in'], 'L0_attn_W_x': _L0_attn_in['W_x'], 'L0_attn_W_dt': _L0_attn_in['W_dt'], 'L0_attn_b_dt': _L0_attn_in['b_dt'], 'L0_attn_A_log': _L0_attn_in['A_log'], 'L0_attn_W_bc': _L0_attn_in['W_bc'], 'L0_attn_W_zy': _L0_attn_in['W_zy'], 'L0_attn_W_mix': _L0_attn_in['W_mix'], 'L0_attn_D': _L0_attn_in['D'], 'L0_attn_ln_gamma': _L0_attn_in['ln_gamma'], 'L0_attn_ln_beta': _L0_attn_in['ln_beta'], 'L0_attn_W_out': _L0_attn_in['W_out'], 'L0_ffn_Ws1': _L0_ffn_in['Ws1'], 'L0_ffn_bs1': _L0_ffn_in['bs1'], 'L0_ffn_Ws2': _L0_ffn_in['Ws2'], 'L0_ffn_bs2': _L0_ffn_in['bs2'], 'L0_ffn_We1': _L0_ffn_in['We1'], 'L0_ffn_be1': _L0_ffn_in['be1'], 'L0_ffn_We2': _L0_ffn_in['We2'], 'L0_ffn_be2': _L0_ffn_in['be2'], 'L0_ffn_Wr': _L0_ffn_in['Wr'], 'L0_ffn_br': _L0_ffn_in['br'], 'L0_c': _L0_c, 'L0_wmod': _L0_wmod}
    _x0 = _d['L0_attn_hidden_states']
    _d['L0_attn_hidden_states'] = jax.random.normal(jax.random.fold_in(jax.random.key(seed), 1), (2, 1024, 128), dtype=_x0.dtype)
    del _x0
    return _d

def reference(L0_attn_hidden_states, L0_attn_W_in, L0_attn_W_x, L0_attn_W_dt, L0_attn_b_dt, L0_attn_A_log, L0_attn_W_bc, L0_attn_W_zy, L0_attn_W_mix, L0_attn_D, L0_attn_ln_gamma, L0_attn_ln_beta, L0_attn_W_out, L0_ffn_Ws1, L0_ffn_bs1, L0_ffn_Ws2, L0_ffn_bs2, L0_ffn_We1, L0_ffn_be1, L0_ffn_We2, L0_ffn_be2, L0_ffn_Wr, L0_ffn_br, L0_c, L0_wmod):

    def _L0_attn_ref(hidden_states, W_in, W_x, W_dt, b_dt, A_log, W_bc, W_zy, W_mix, D, ln_gamma, ln_beta, W_out):
        import jax, jax.numpy as jnp
        import numpy as np
        D_MODEL = 128
        EXPAND = 2
        D_INNER = EXPAND * D_MODEL
        D_STATE = 16
        DT_RANK = (D_MODEL + 15) // 16
        EPS = 1e-05
        FP_ITERS = 8
        STEP = 0.99
        B_SZ, L_SEQ = (2, 256)

        def _shift1(y):
            return jnp.pad(y, ((0, 0), (1, 0), (0, 0)))[:, :-1, :]

        def _selective_scan(u, delta, A, Bm, Cm, D):

            def step(h, inp):
                dt_t, u_t, b_t, c_t = inp
                h = jnp.exp(dt_t[:, :, None] * A) * h + (dt_t * u_t)[:, :, None] * b_t[:, None, :]
                y = jnp.einsum('bdn,bn->bd', h, c_t) + D * u_t
                return (h, y)
            b, l, d = u.shape
            h0 = jnp.zeros((b, d, A.shape[1]), u.dtype)
            xs = tuple((jnp.moveaxis(a, 1, 0) for a in (delta, u, Bm, Cm)))
            _, ys = jax.lax.scan(step, h0, xs)
            return jnp.moveaxis(ys, 0, 1)
        xz = hidden_states @ W_in.T
        x, z = (xz[..., :D_INNER], xz[..., D_INNER:])
        x_dbl = x @ W_x.T
        dt_low = x_dbl[..., :DT_RANK]
        B0 = x_dbl[..., DT_RANK:DT_RANK + D_STATE]
        C0 = x_dbl[..., DT_RANK + D_STATE:]
        delta = jax.nn.softplus(dt_low @ W_dt.T + b_dt)
        A = -jnp.exp(A_log)

        def layer_norm(y):
            m = jnp.mean(y, -1, keepdims=True)
            v = jnp.var(y, -1, keepdims=True)
            return ln_gamma * (y - m) * jax.lax.rsqrt(v + EPS) + ln_beta

        def bc_normalize(v):
            n = jnp.linalg.norm(v, axis=-1, keepdims=True)
            return v / jnp.maximum(n, EPS)

        def fp_step(y_prev):
            x_tilde = (x - y_prev) @ W_mix.T + y_prev
            bc = _shift1(y_prev) @ W_bc.T
            Bt = bc_normalize(B0 + bc[..., :D_STATE])
            Ct = bc_normalize(C0 + bc[..., D_STATE:])
            y = _selective_scan(x_tilde, delta, A, Bt, Ct, D)
            return layer_norm(y)
        y0 = jnp.zeros_like(x)
        y_star = jax.lax.fori_loop(0, FP_ITERS, lambda i, y: y + STEP * (fp_step(y) - y), y0)
        y_star = jax.lax.stop_gradient(y_star)
        y = fp_step(y_star)
        z2 = z + _shift1(y) @ W_zy.T
        return jax.nn.silu(z2) * y @ W_out.T

    def _L0_ffn_ref(x, Ws1, bs1, Ws2, bs2, We1, be1, We2, be2, Wr, br):
        import jax, jax.numpy as jnp
        import numpy as np
        D = 128
        E = 12
        HS = 2 * D
        HR = 3 * D
        TAU = 1.5

        def _geglu(h):
            a, g = jnp.split(h, 2, axis=-1)
            return a * jax.nn.gelu(g, approximate=False)
        B, T, Dm = x.shape
        xf = x.reshape(-1, Dm)
        ys = _geglu(xf @ Ws1 + bs1) @ Ws2 + bs2
        logits = (xf @ Wr + br) / TAU
        top_val, top_idx = jax.lax.top_k(logits, 2)
        top_w = jax.nn.softmax(top_val, axis=-1)
        onehot = jax.nn.one_hot(top_idx, E, dtype=x.dtype)
        w = jnp.einsum('nke,nk->ne', onehot, top_w)
        h = jnp.einsum('nd,edh->enh', xf, We1) + be1[:, None, :]
        act = _geglu(h)
        yE = jnp.einsum('enh,ehd->end', act, We2) + be2[:, None, :]
        yr = jnp.einsum('end,ne->nd', yE, w)
        return (ys + yr).reshape(B, T, Dm)
    x = L0_attn_hidden_states
    mod = (_silu(L0_c) @ L0_wmod).reshape(L0_c.shape[0], 6, 1, -1)
    sa, ca, ga, sb, cb, gb = (mod[:, 0], mod[:, 1], mod[:, 2], mod[:, 3], mod[:, 4], mod[:, 5])
    ga = (2 * (ga >= 0) - 1) * jnp.maximum(jnp.abs(ga), 0.25)
    gb = (2 * (gb >= 0) - 1) * jnp.maximum(jnp.abs(gb), 0.25)
    h = _layernorm(x, axis=-1) * (1 + ca) + sa
    x = x + ga * _L0_attn_ref(h, L0_attn_W_in, L0_attn_W_x, L0_attn_W_dt, L0_attn_b_dt, L0_attn_A_log, L0_attn_W_bc, L0_attn_W_zy, L0_attn_W_mix, L0_attn_D, L0_attn_ln_gamma, L0_attn_ln_beta, L0_attn_W_out)
    h = _layernorm(x, axis=-1) * (1 + cb) + sb
    x = x + gb * _L0_ffn_ref(h, L0_ffn_Ws1, L0_ffn_bs1, L0_ffn_Ws2, L0_ffn_bs2, L0_ffn_We1, L0_ffn_be1, L0_ffn_We2, L0_ffn_be2, L0_ffn_Wr, L0_ffn_br)
    return x

_drawn_inputs = setup_inputs


def setup_inputs(seed=0):
    import zlib

    import numpy as np

    out = dict(_drawn_inputs(seed))
    spreads = {'L0_attn_D': (1.0, 0.2),
     'L0_attn_ln_gamma': (1.0, 0.2),
     'L0_attn_ln_beta': (0.0, 0.1),
     'L0_ffn_bs1': (0.0, 0.543),
     'L0_ffn_bs2': (0.0, 0.348),
     'L0_ffn_be1': (0.0, 0.8),
     'L0_ffn_be2': (0.0, 0.466),
     'L0_ffn_br': (0.0, 0.58)}
    factors = {'L0_attn_W_x': 3.708,
     'L0_attn_W_dt': 7.807,
     'L0_attn_b_dt': 5.722,
     'L0_attn_A_log': 5.575,
     'L0_attn_W_bc': 3.875}
    for name, (base, spread) in spreads.items():
        noise = np.random.default_rng([zlib.crc32(name.encode()), seed]).standard_normal(out[name].shape)
        drawn = base * np.exp(spread * noise) if base else spread * noise
        out[name] = jnp.asarray(drawn.astype(out[name].dtype))
    for name, factor in factors.items():
        out[name] = (out[name] * factor).astype(out[name].dtype)
    return out
```

```python
import concourse.bass as bass
from concourse import mybir
from concourse.alu_op_type import AluOpType as ALU
from contextlib import ExitStack
import numpy as np


F32 = mybir.dt.float32
U32 = mybir.dt.uint32
ACT = mybir.ActivationFunctionType
AX = mybir.AxisListType

NB, L, DM = 2, 1024, 128
DI, NS, RK = 256, 16, 8
T = 256
NC = L // T
NT = T // 128
NTT = NB * NT
EV = 9
STEP = 0.99
EPS = 1e-5
NTILE = DI * NS // 128
NG = 8
UC = EV * NB
XW = DI + 2 * NS
NE, HR, HS = 12, 384, 256
TAU = 1.5
TOK = NB * T


P_BACK, P_FORTH, P_MIX, P_REP = ((1, 1), (2, 1), (4, 0), (6, 1))
A_SPLIT = (5, 6, 8, 2, 4)
PLACE = dict(zip(("D_STATS", "D_NORM", "D_UPDATE", "D_NORMS", "D_INPUTS"), (3, 4, 6, 8, 9)))


def log1p_coefficients(degree):
    k = np.arange(degree + 1)
    at = 0.5 + 0.5 * np.cos(np.pi * (k + 0.5) / (degree + 1))
    fit = np.polynomial.chebyshev.Chebyshev.fit(at, np.log1p(at) / at, degree, domain=[0, 1])
    return [float(x) for x in fit.convert(kind=np.polynomial.polynomial.Polynomial).coef]


def adaln_block_kernel(nc, hidden, WinT, WxT, Wdt9, AlogS, WbcT, WzyT, WmixT, chanT, WoutT,
                       Ws1, bs1T, Ws2, bs2T, We1, be1T, We2, be2, Wr, br, cT, wmod, consts, out):
    ctx = ExitStack()
    with ctx:
        def sb(name, shape, dt=F32):
            return ctx.enter_context(nc.sbuf_tensor(name, shape, dt))

        def ps(name, shape):
            return ctx.enter_context(nc.psum_tensor(name, shape, F32))

        def sem(name):
            return ctx.enter_context(nc.semaphore(name))

        ident = sb("ident", [128, 128])
        sel = sb("sel", [128, 32])
        iota = sb("iota", [128, NE])
        winT = sb("winT", [DM, 2 * DI])
        wxdt = sb("wxdt", [128, 2, RK])
        wxm = sb("wxm", [128, 2, XW])
        imix = sb("imix", [128, 2, DI])
        wbc = sb("wbc", [128, 2, 2 * NS])
        wzy = sb("wzy", [128, 2, DI])
        wout = sb("wout", [128, 2, DM])
        wdt9 = sb("wdt9", [RK + 1, DI])
        Aneg = sb("Aneg", [128, NTILE])
        chan = sb("chan", [128, 2, 2])
        damp = sb("damp", [128, 2, 2])
        Dbc = sb("Dbc", [128, DI])
        silc = sb("silc", [128, NB])
        modT = sb("modT", [128, 6, NB])
        modsg = sb("modsg", [128, 2, 6 * NB])
        wr = sb("wr", [DM, NE])
        brow = sb("brow", [1, NE])
        ones = sb("ones", [1, 128])
        be2s = sb("be2s", [NE, DM])
        bs1s = sb("bs1s", [128, 2 * HS // 128])
        bs2s = sb("bs2s", [128, 1])
        be1s = sb("be1s", [128, NE, 2 * HR // 128])
        X = sb("X", [128, NTT, DM])
        nx = sb("nx", [128, NTT, DM])
        hT = sb("hT", [128, TOK])
        xT = sb("xT", [128, 2, TOK])
        dlow = sb("dlow", [RK + 1, TOK])
        delta = sb("delta", [128, NTT, DI])
        xm = sb("xm", [128, NTT, XW])
        decay = sb("decay", [128, NTILE, NB, T])
        yT = sb("yT", [128, NB, 2, T + 1])
        ylast = sb("ylast", [128, EV + 1, NB, 2])
        hcar = sb("hcar", [128, EV, NB, NTILE])
        v = sb("v", [128, NB, NT, DI])
        xD = sb("xD", [128, NB, NT, DI])
        bcs = sb("bcs", [128, NT, 2, NS])
        sq = sb("sq", [128, NT, 2, NS])
        ss = sb("ss", [128, NT, 2])
        sdb = sb("sdb", [128, NT, 2])
        rn = sb("rn", [128, NT, 2])
        Bn = sb("Bn", [128, NB, NT, NS])
        U = sb("U", [128, 4, NT, 8, 128])
        cexp = sb("cexp", [128, NT, NS, 32])
        crep = sb("crep", [128, NB, 4, T])
        hring = sb("hring", [128, 4, 4, T])
        gring = sb("gring", [128, 4, 4, T])
        yTs = sb("yTs", [128, 2, T])
        st = sb("st", [128, NTT, 6])
        mv = sb("mv", [128, NTT, 2])
        sd = sb("sd", [128, NTT])
        rs = sb("rs", [128, NTT])
        nrm = sb("nrm", [128, NT, DI])
        gy = sb("gy", [128, 2, T])
        xmid = sb("xmid", [128, NC, NTT, DM])
        ups = ps("ups", [128, 4, 512])
        yps = ps("yps", [128, 2, 512])
        mm = ps("mm", [128, 2, 512])

        w_in = sem("w_in"); silu_c = sem("silu_c"); mod_mm = sem("mod_mm"); mod_sb = sem("mod_sb")
        gates = sem("gates"); setup_dve = sem("setup_dve"); a_exp = sem("a_exp"); a_neg = sem("a_neg")
        setup_pool = sem("setup_pool")
        x_in = sem("x_in"); ln1_stat = sem("ln1_stat"); ln1_agg = sem("ln1_agg"); ln1_sd = sem("ln1_sd")
        ln1_rs = sem("ln1_rs"); ln1_n = sem("ln1_n"); ln1_T = sem("ln1_T"); h_T = sem("h_T")
        x_mm = sem("x_mm"); x_T = sem("x_T"); dl_mm = sem("dl_mm"); dl_sb = sem("dl_sb")
        dt_mm = sem("dt_mm"); xm_mm = sem("xm_mm"); xm_sb = sem("xm_sb"); dt_abs = sem("dt_abs")
        dt_exp = sem("dt_exp"); dt_relu = sem("dt_relu"); poly = sem("poly"); delta_ok = sem("delta_ok")
        drep_p = sem("drep_p"); drep_a = sem("drep_a"); dbank = sem("dbank"); decay_ok = sem("decay_ok")
        y_zero = sem("y_zero")
        mix_mm = sem("mix_mm"); bc_mm = sem("bc_mm"); bc_ok = sem("bc_ok"); m_step = sem("m_step"); bc_sd = sem("bc_sd")
        rn_ok = sem("rn_ok"); v_ok = sem("v_ok"); bn_ok = sem("bn_ok"); xd_ok = sem("xd_ok")
        cexp_ok = sem("cexp_ok"); crep_mm = sem("crep_mm"); crep_ok = sem("crep_ok")
        quarter = sem("quarter"); u_ok = sem("u_ok"); scanned = sem("scanned"); carried = sem("carried")
        g_ok = sem("g_ok"); summed = sem("summed"); y_ev = sem("y_ev"); y_t = sem("y_t")
        l_stat = sem("l_stat"); l_agg = sem("l_agg"); l_sd = sem("l_sd"); l_rs = sem("l_rs")
        l_n = sem("l_n"); n_T = sem("n_T"); gy_ok = sem("gy_ok"); y_head = sem("y_head"); y_new = sem("y_new")
        y_tail = sem("y_tail")
        z_mm = sem("z_mm"); z_silu = sem("z_silu"); s_ok = sem("s_ok"); o_mm = sem("o_mm")
        o_sc = sem("o_sc"); o_t = sem("o_t"); x_mid = sem("x_mid")
        fw_in = sem("fw_in"); f_stat = sem("f_stat"); f_agg = sem("f_agg"); f_sd = sem("f_sd")
        f_rs = sem("f_rs"); f_n = sem("f_n"); f_T = sem("f_T"); f_h = sem("f_h"); r_mm = sem("r_mm")
        r_l = sem("r_l"); r_top = sem("r_top"); r_idx = sem("r_idx"); r_dif = sem("r_dif")
        r_e = sem("r_e"); r_p = sem("r_p"); r_w = sem("r_w"); w_T = sem("w_T"); w_Ts = sem("w_Ts")
        wb_mm = sem("wb_mm"); wb_sb = sem("wb_sb"); ag_mm = sem("ag_mm"); gelu = sem("gelu")
        geglu = sem("geglu"); act_ok = sem("act_ok"); down = sem("down"); f_mm = sem("f_mm")
        f_sc = sem("f_sc"); f_t = sem("f_t"); x_out = sem("x_out"); stored = sem("stored")

        def alone(eng):
            eng.nop(nofuse=True)

        flat = decay[:, :, :, :].rearrange("p a b t -> p (a b t)")
        we1 = flat[:, 0:NE * 2 * HR].rearrange("p (e f) -> p e f", e=NE)
        o1 = NE * 2 * HR
        we2 = flat[:, o1:o1 + NE * HR].rearrange("p (e k f) -> p e k f", e=NE, k=3)
        o2 = o1 + NE * HR
        ws1 = flat[:, o2:o2 + 2 * HS]
        ws2 = flat[:, o2 + 2 * HS:o2 + 3 * HS].rearrange("p (k f) -> p k f", k=2)
        uflat = U[:, :, :, :, :].rearrange("p q t d n -> p (q t d n)")
        drep = uflat.rearrange("p (x k n d) -> p x k n d", x=8, k=8, n=4)
        hflat = hring[:, :, :, :].rearrange("p s j t -> p (s j t)")
        gflat = gring[:, :, :, :].rearrange("p s j t -> p (s j t)")
        sT = gflat[:, 0:2 * TOK].rearrange("p (k t) -> p k t", k=2)
        wmods = hflat[:, 0:6 * DM]
        dabs, dexp_, drelu, dpoly = (hflat[:, 1024 * k:1024 * (k + 1)] for k in range(4))
        NW = 14 + 2 + 2 + 2

        def geg(e):
            return hflat[:, (e % 2) * 1536:(e % 2) * 1536 + 1536].rearrange("p (k t) -> p k t", k=3)

        def actw(e):
            return gflat[:, (e % 2) * 1536:(e % 2) * 1536 + 1536].rearrange("p (k t) -> p k t", k=3)

        gel = uflat[:, 0:3 * TOK].rearrange("p (k t) -> p k t", k=3)
        shg = uflat[:, 3 * TOK:5 * TOK].rearrange("p (k t) -> p k t", k=2)
        wbs = uflat[:, 5 * TOK:7 * TOK].rearrange("p (s t) -> p s t", s=2)
        rt = uflat[:, 7 * TOK:8 * TOK]
        lg = rt[:, 0:48].rearrange("p (x e) -> p x e", x=4)
        top = rt[:, 48:80].rearrange("p (x e) -> p x e", x=4)
        idx = rt[:, 80:112].rearrange("p (x e) -> p x e", x=4)
        idf = rt[:, 112:144].rearrange("p (x e) -> p x e", x=4)
        dif = rt[:, 144:148]; er = rt[:, 148:152]; den = rt[:, 152:156]
        p1 = rt[:, 156:160]; p2 = rt[:, 160:164]
        oh = rt[:, 164:212].rearrange("p (x e) -> p x e", x=4)
        wt = rt[:, 212:260].rearrange("p (x e) -> p x e", x=4)
        wTs = nx[0:NE, 0:4, :].rearrange("p x t -> p (x t)")

        def abank(n):
            return ups[:, n % 3, :]

        def gbank(n):
            return (ups[:, 3, :], yps[:, 0, :], yps[:, 1, :])[n % 3]

        block = ctx.enter_context(nc.Block())

        @block.sync
        def _(sp):
            def load(dst, src, s=w_in):
                sp.dma_start(dst, src).then_inc(s, 16)

            with nc.allow_non_contiguous_dma(reason="one-off weight loads with short rows"):
                load(ident[:, :], consts[:, 0:128])
                load(sel[:, :], consts[:, 128:160])
                load(iota[:, :], consts[:, 160:160 + NE])
                load(silc[:, :], cT)
                load(wmods, wmod)
                load(Aneg[:, :], AlogS)
                load(winT[:, :], WinT)
                load(wxdt[:, :, :], WxT[:, 0:RK].rearrange("(k p) m -> p k m", p=128))
                load(wxm[:, :, 0:DI], WmixT.rearrange("(k p) m -> p k m", p=128))
                load(wxm[:, :, DI:XW], WxT[:, RK:RK + 2 * NS].rearrange("(k p) m -> p k m", p=128))
                load(wbc[:, :, :], WbcT.rearrange("(k p) m -> p k m", p=128))
                load(wzy[:, :, :], WzyT.rearrange("(k p) m -> p k m", p=128))
                load(wout[:, :, :], WoutT.rearrange("(k p) m -> p k m", p=128))
                load(wdt9[:, :], Wdt9)
                load(chan[:, :, 0:1], chanT[0:2 * 128, 0:1].rearrange("(k p) m -> p k m", p=128))
                load(chan[:, :, 1:2], chanT[0:2 * 128, 1:2].rearrange("(k p) m -> p k m", p=128))
                load(Dbc[:, :], chanT[:, 2:3].rearrange("d o -> o d").to_broadcast([128, DI]))
                load(wr[:, :], Wr)
                load(brow[:, :], br)
                load(be2s[:, :], be2)
                load(bs1s[:, :], bs1T, fw_in)
                load(bs2s[:, :], bs2T, fw_in)
                load(be1s[:, :, :], be1T.rearrange("p (e k) -> p e k", e=NE), fw_in)
            with sp.Fori(0, NC) as c:
                sp.wait_ge(x_mid, c + 1)
                for b in range(NB):
                    sp.dma_start(X[:, b * NT:(b + 1) * NT, :],
                                 hidden[b, bass.ds(c * T, T), :].rearrange("(u p) d -> p u d", p=128)).then_inc(x_in, 16)
            sp.wait_ge(scanned, NC * UC * 16)
            for e in range(NE):
                load(we1[:, e, :], We1[e, :, :], fw_in)
                load(we2[:, e, :, :], We2[e, :, :].rearrange("(k p) m -> p k m", p=128), fw_in)
            load(ws1, Ws1, fw_in)
            load(ws2, Ws2.rearrange("(k p) m -> p k m", p=128), fw_in)
            with sp.Fori(0, NC) as c:
                sp.wait_ge(x_out, c + 2)
                for b in range(NB):
                    sp.dma_start(out[b, bass.ds(c * T, T), :].rearrange("(u p) d -> p u d", p=128),
                                 xmid[:, bass.ds(c, 1), b * NT:(b + 1) * NT, :].rearrange("p o k d -> p (o k) d")).then_inc(stored, 16)
            sp.wait_ge(stored, NC * NB * 16)

        NFW = 3 + 2 * NE + 2

        @block.gpsimd
        def _(pool):
            nc.gpsimd.memset(dlow[:, :], 1.0)
            nc.gpsimd.memset(ylast[:, :, :, :], 0.0)
            nc.gpsimd.memset(hcar[:, :, :, :], 0.0)
            nc.gpsimd.memset(ones[:, :], 1.0).then_inc(setup_pool, 1)

            def multiply(u, b, first=False):
                for g in range(NG):
                    q = g // 2
                    if g == 0:
                        pool.wait_ge(crep_ok, u * 2 + 2)
                    pool.wait_ge(scanned, u * 16 + 2 * g + 2)
                    if not (first and g < 4):
                        pool.wait_ge(summed, u * 8 + g - 3)
                    nc.gpsimd.tensor_tensor(
                        gring[:, g % 4, :, :], hring[:, g % 4, :, :],
                        crep[:, b, q:q + 1, :].to_broadcast([128, 4, T]), ALU.mult).then_inc(g_ok, 1)

            with pool.Fori(0, NC) as c:
                pool.wait_ge(x_mid, c + 1)
                alone(pool)
                nc.gpsimd.memset(yT[:, :, :, :], 0.0).then_inc(y_zero, 1)
                pool.wait_ge(delta_ok, c + 1)
                alone(pool)
                for k in range(2):
                    nc.gpsimd.tensor_copy(
                        drep[:, k, :, :, :],
                        delta[:, k, :].rearrange("p (k o d) -> p k o d", k=8, o=1).to_broadcast([128, 8, 4, 32])
                    ).then_inc(drep_p, 1)
                multiply(c * UC, 0, first=True)
                with pool.Fori(0, EV - 1) as i:
                    u = c * UC + i * 2
                    multiply(u + 1, 1)
                    multiply(u + 2, 0)
                multiply(c * UC + UC - 1, 1)

            with pool.Fori(0, NC) as c:
                for e in range(NE):
                    n = e + 1
                    pool.wait_ge(wb_sb, c * NE + e + 1)
                    pool.wait_ge(geglu, c * (3 * NE + 2) + 3 * e + 3)
                    if e >= 2:
                        pool.wait_ge(down, c * (NE + 1) + e - 1)
                    nc.gpsimd.tensor_tensor(
                        actw(e), geg(e),
                        wbs[:, e % 2, :].rearrange("p (o t) -> p o t", o=1).to_broadcast([128, 3, TOK]),
                        ALU.mult).then_inc(act_ok, 1)

        @block.scalar
        def _(act):
            A = nc.scalar.activation
            act.wait_ge(w_in, 16 * NW)
            A(silc[:, :], silc[:, :], ACT.Silu).then_inc(silu_c, 1)
            A(Aneg[:, :], Aneg[:, :], ACT.Exp).then_inc(a_exp, 1)

            def v_times_b(vu, b, h, first=False):
                q = h // 2
                if h == 0:
                    act.wait_ge(bn_ok, vu + 1)
                    act.wait_ge(v_ok, vu + 1)
                if not first and h % 2 == 0:
                    act.wait_ge(u_ok, vu * 16 + 4 * q - 12)
                for n in (2 * (h % 2), 2 * (h % 2) + 1):
                    for tt in range(NT):
                        last = A(U[:, q, tt, :, 32 * n:32 * n + 32],
                                 v[:, b, tt, :].rearrange("p (k d) -> p k d", k=8),
                                 ACT.Copy, scale=Bn[:, b, tt, 4 * q + n:4 * q + n + 1])
                if h % 2:
                    last.then_inc(quarter, 1)

            def form(vu, b, first=False):
                act.wait_ge(bc_ok, vu + 1)
                A(sdb[:, :, :], ss[:, :, :], ACT.Sqrt).then_inc(bc_sd, 1)
                act.wait_ge(rn_ok, vu + 1)
                for tt in range(NT):
                    A(cexp[:, tt, :, :], bcs[:, tt, 1, :].rearrange("p (n o) -> p n o", o=1).to_broadcast([128, NS, 32]),
                      ACT.Copy, scale=rn[:, tt, 1:2]).then_inc(cexp_ok, 1)
                for h in range(A_SPLIT[3]):
                    v_times_b(vu, b, h, first)
                act.wait_ge(crep_mm, vu + 1)
                for k in range(2):
                    A(crep[:, b, 2 * k:2 * k + 2, :].rearrange("p q t -> p (q t)"), mm[:, k, :],
                      ACT.Copy).then_inc(crep_ok, 1)
                for h in range(A_SPLIT[3], A_SPLIT[4]):
                    v_times_b(vu, b, h, first)

            def slot(u, b, norm=True, last=False, nxt=True, first=False):
                w, o = u - 1, 1 - b
                if norm:
                    for blk in range(2):
                        act.wait_ge(summed, w * 8 + 7 + blk)
                        A(yTs[:, blk, :], yps[:, blk, 0:T], ACT.Copy).then_inc(y_ev, 1)
                for h in range(A_SPLIT[4], A_SPLIT[0]):
                    v_times_b(u, b, h, first)
                if norm:
                    act.wait_ge(l_agg, w * 2 + 2)
                    A(sd[:, 0:NT], mv[:, 0:NT, 1], ACT.Sqrt, bias=EPS).then_inc(l_sd, 1)
                for h in range(A_SPLIT[0], A_SPLIT[1]):
                    v_times_b(u, b, h, first)
                if norm:
                    evac_norm(w, o, last)
                for h in range(A_SPLIT[1], 8):
                    v_times_b(u, b, h, first)
                if nxt:
                    form(u + 1, o)

            def evac_norm(w, b, last=False):
                act.wait_ge(n_T, w + 1)
                for blk in range(2):
                    src = mm[:, 1, blk * T:(blk + 1) * T]
                    if last:
                        A(yT[:, b, blk, 1:T + 1], src, ACT.Identity, bias=chan[:, blk, 1:2],
                          scale=chan[:, blk, 0:1]).then_inc(gy_ok, 1)
                    else:
                        A(gy[:, blk, :], src, ACT.Identity, bias=damp[:, blk, 1:2],
                          scale=damp[:, blk, 0:1]).then_inc(gy_ok, 1)

            with act.Fori(0, NC) as c:
                act.wait_ge(ln1_agg, c * NTT + NTT)
                A(sd[:, :], mv[:, :, 1], ACT.Sqrt, bias=EPS).then_inc(ln1_sd, 1)
                for k in range(2):
                    act.wait_ge(x_mm, c * 2 + k + 1)
                    A(xT[:, k, :], ups[:, k, :], ACT.Copy).then_inc(x_T, 1)
                act.wait_ge(setup_pool, 1)
                act.wait_ge(dl_mm, c + 1)
                A(dlow[0:RK, :], mm[0:RK, 1, :], ACT.Copy).then_inc(dl_sb, 1)
                act.wait_ge(dt_mm, c + 1)
                A(dabs, ups[:, 2:4, :].rearrange("p k t -> p (k t)"), ACT.Abs).then_inc(dt_abs, 1)
                act.wait_ge(dt_abs, c + 1)
                A(dexp_, dabs, ACT.Exp, scale=-1.0).then_inc(dt_exp, 1)
                A(drelu, ups[:, 2:4, :].rearrange("p k t -> p (k t)"), ACT.Relu).then_inc(dt_relu, 1)
                act.wait_ge(xm_mm, c + 1)
                A(xm[:, 0:2, :], mm[:, :, 0:XW], ACT.Copy).then_inc(xm_sb, 1)
                A(xm[:, 2:4, :], yps[:, :, 0:XW], ACT.Copy).then_inc(xm_sb, 1)
                act.wait_ge(delta_ok, c + 1)
                for k in range(2, 4):
                    A(drep[:, k, :, :, :],
                      delta[:, k, :].rearrange("p (k o d) -> p k o d", k=8, o=1).to_broadcast([128, 8, 4, 32]),
                      ACT.Copy).then_inc(drep_a, 1)
                act.wait_ge(a_neg, 1)
                for k in range(8):
                    act.wait_ge(dbank, c * 8 + k + 1)
                    for q in range(4):
                        tile = (2 * q + k // 4) * 4 + k % 4
                        last = A(decay[:, tile, :, :].rearrange("p b t -> p (b t)"), ups[:, k % 4, :], ACT.Exp,
                                 scale=Aneg[:, tile:tile + 1])
                    last.then_inc(decay_ok, 1)
                form(c * UC, 0, first=True)
                slot(c * UC, 0, norm=False, first=True)
                with act.Fori(0, EV - 1) as i:
                    u = c * UC + i * 2
                    slot(u + 1, 1)
                    slot(u + 2, 0)
                w = c * UC + UC - 2
                slot(w + 1, 1, last=True, nxt=False)
                for blk in range(2):
                    act.wait_ge(summed, (w + 1) * 8 + 7 + blk)
                    A(yTs[:, blk, :], yps[:, blk, 0:T], ACT.Copy).then_inc(y_ev, 1)
                act.wait_ge(l_agg, (w + 1) * 2 + 2)
                A(sd[:, 0:NT], mv[:, 0:NT, 1], ACT.Sqrt, bias=EPS).then_inc(l_sd, 1)
                evac_norm(w + 1, 1, last=True)
                for m in range(2):
                    act.wait_ge(z_mm, c * 2 + m + 1)
                    A(sT[:, m, :], ups[:, m, :], ACT.Silu).then_inc(z_silu, 1)

            act.wait_ge(fw_in, 16 * NFW)
            with act.Fori(0, NC) as c:
                act.wait_ge(f_agg, c * NTT + NTT)
                A(sd[:, :], mv[:, :, 1], ACT.Sqrt, bias=EPS).then_inc(f_sd, 1)
                act.wait_ge(r_dif, c + 1)
                A(er, dif, ACT.Exp).then_inc(r_e, 1)
                act.wait_ge(w_T, c + 1)
                A(wTs, mm[0:NE, 1, :], ACT.Copy).then_inc(w_Ts, 1)
                for e in range(NE + 1):
                    if e < NE:
                        act.wait_ge(wb_mm, c * NE + e + 1)
                        if e >= 2:
                            act.wait_ge(act_ok, c * NE + e - 1)
                        A(wbs[:, e % 2, :], mm[:, 1, :], ACT.Copy).then_inc(wb_sb, 1)
                    for k in range(3 if e < NE else 2):
                        n = 3 * e + k
                        act.wait_ge(ag_mm, c * (3 * NE + 2) + n + 1)
                        if n >= 3:
                            act.wait_ge(geglu, c * (3 * NE + 2) + n - 2)
                        bias = be1s[:, e, 3 + k:4 + k] if e < NE else bs1s[:, 2 + k:3 + k]
                        A(gel[:, k, :], gbank(n), ACT.Gelu, bias=bias).then_inc(gelu, 1)

        @block.vector
        def _(dve):
            V = nc.vector
            dve.wait_ge(w_in, 16 * NW)
            V.tensor_scalar(imix[:, :, :], wxm[:, :, 0:DI], -1.0, None, ALU.mult).then_inc(setup_dve, 1)
            dve.wait_ge(setup_dve, 1)
            for k in range(2):
                V.tensor_tensor(imix[:, k, 128 * k:128 * k + 128], imix[:, k, 128 * k:128 * k + 128], ident[:, :],
                                ALU.add).then_inc(setup_dve, 1)
            V.tensor_scalar(damp[:, :, :], chan[:, :, :], STEP, None, ALU.mult).then_inc(setup_dve, 1)
            dve.sem_inc(x_mid, 1)
            dve.sem_inc(x_out, 1)
            dve.wait_ge(a_exp, 1)
            V.tensor_scalar(Aneg[:, :], Aneg[:, :], -1.0, None, ALU.mult).then_inc(a_neg, 1)
            dve.wait_ge(mod_mm, 1)
            V.tensor_copy(modT[:, :, :].rearrange("p k b -> p (k b)"), mm[:, 0, 0:6 * NB]).then_inc(mod_sb, 1)
            dve.wait_ge(mod_sb, 1)
            sgn, mag = modsg[:, 0, :], modsg[:, 1, :]
            flatm = modT[:, :, :].rearrange("p k b -> p (k b)")
            V.tensor_scalar(sgn, flatm, 0.0, 2.0, ALU.is_ge, ALU.mult).then_inc(gates, 1)
            V.tensor_scalar(mag, flatm, -1.0, None, ALU.mult).then_inc(gates, 1)
            dve.wait_ge(gates, 2)
            V.tensor_scalar(sgn, sgn, -1.0, None, ALU.add).then_inc(gates, 1)
            V.tensor_tensor(mag, mag, flatm, ALU.max).then_inc(gates, 1)
            dve.wait_ge(gates, 4)
            V.tensor_scalar(mag, mag, 0.25, None, ALU.max).then_inc(gates, 1)
            dve.wait_ge(gates, 5)
            V.tensor_tensor(mag, mag, sgn, ALU.mult).then_inc(gates, 1)
            dve.wait_ge(gates, 6)
            for k in (2, 5):
                V.tensor_copy(modT[:, k, :], mag[:, NB * k:NB * k + NB]).then_inc(gates, 1)
            for k in (1, 4):
                V.tensor_scalar(modT[:, k, :], modT[:, k, :], 1.0, None, ALU.add).then_inc(gates, 1)
            dve.wait_ge(gates, 10)

            def norms(vu, b):
                dve.wait_ge(bc_mm, vu + 1)
                V.tensor_copy(bcs[:, :, :, :].rearrange("p t k n -> p (t k n)"), mm[:, 1, 0:NT * 2 * NS]).then_inc(m_step, 1)
                dve.wait_ge(m_step, vu * 3 + 1)
                V.tensor_tensor(sq[:, :, :, :], bcs[:, :, :, :], bcs[:, :, :, :], ALU.mult).then_inc(m_step, 1)
                dve.wait_ge(m_step, vu * 3 + 2)
                V.tensor_reduce(ss[:, :, :], sq[:, :, :, :], AX.X, ALU.add).then_inc(m_step, 1)
                dve.wait_ge(m_step, vu * 3 + 3)
                V.tensor_scalar(ss[:, :, :], ss[:, :, :], EPS * EPS, None, ALU.max).then_inc(bc_ok, 1)

            def inputs(vu, b):
                row = slice(b * NT, (b + 1) * NT)
                dve.wait_ge(bc_sd, vu + 1)
                V.reciprocal(rn[:, :, :], sdb[:, :, :]).then_inc(rn_ok, 1)
                dve.wait_ge(rn_ok, vu + 1)
                V.tensor_tensor(Bn[:, b, :, :], bcs[:, :, 0, :], rn[:, :, 0:1].to_broadcast([128, NT, NS]),
                                ALU.mult).then_inc(bn_ok, 1)
                dve.wait_ge(mix_mm, vu + 1)
                V.tensor_tensor(v[:, b, :, :], mm[:, 0, :].rearrange("p (t d) -> p t d", t=NT), delta[:, row, :], ALU.mult).then_inc(v_ok, 1)
                V.tensor_tensor(xD[:, b, :, :], mm[:, 0, :].rearrange("p (t d) -> p t d", t=NT),
                                Dbc[:, :].rearrange("p (o d) -> p o d", o=1).to_broadcast([128, NT, DI]),
                                ALU.mult).then_inc(xd_ok, 1)

            def stats(w):
                dve.wait_ge(y_t, w + 1)
                for tt in range(NT):
                    V.bn_stats(st[:, tt, :], mm[:, 0, tt * DI:(tt + 1) * DI]).then_inc(l_stat, 1)
                for tt in range(NT):
                    dve.wait_ge(l_stat, w * 2 + 1 + tt)
                    alone(dve)
                    V.bn_aggr(mv[:, tt, :], st[:, tt, :]).then_inc(l_agg, 1)

            def normalise(w):
                dve.wait_ge(l_sd, w + 1)
                V.reciprocal(rs[:, 0:NT], sd[:, 0:NT]).then_inc(l_rs, 1)
                dve.wait_ge(l_rs, w + 1)
                for tt in range(NT):
                    V.tensor_scalar(nrm[:, tt, :], mm[:, 0, tt * DI:(tt + 1) * DI], mv[:, tt, 0:1], rs[:, tt:tt + 1],
                                    ALU.subtract, ALU.mult).then_inc(l_n, 1)

            def update(w, b, i, last=False):
                V.tensor_scalar(yT[:, b, :, 0], ylast[:, i + 1, b, :] if last else ylast[:, bass.ds(i + 1, 1), b, :].rearrange("p o k -> p (o k)"), 1.0, None, ALU.mult).then_inc(y_head, 1)
                dve.wait_ge(gy_ok, w * 2 + 2)
                if last:
                    dve.wait_ge(y_head, w + 1)
                    V.tensor_scalar(ylast[:, i + 1, b, :], yT[:, b, :, T], 1.0, None, ALU.mult).then_inc(y_tail, 1)
                else:
                    V.scalar_tensor_tensor(yT[:, b, :, 1:T + 1], yT[:, b, :, 1:T + 1], 1.0 - STEP, gy[:, :, :],
                                           ALU.mult, ALU.add).then_inc(y_new, 1)

            def keep(w, b, i, nth):
                dve.wait_ge(y_new, nth)
                V.tensor_scalar(ylast[:, bass.ds(i + 1, 1), b, :].rearrange("p o k -> p (o k)"), yT[:, b, :, T], 1.0, None, ALU.mult).then_inc(y_tail, 1)

            def at(**steps):
                return {PLACE[k]: f for k, f in steps.items()}

            def scans(u, b, i, static, first=False, after=None):
                def car(t0, t1):
                    if static:
                        return hcar[:, i, b, t0:t1]
                    return hcar[:, bass.ds(i, 1), b, t0:t1].rearrange("p o k -> p (o k)")

                def carry(g):
                    dve.wait_ge(scanned, u * 16 + 2 * g + 2)
                    V.tensor_scalar(car(4 * g, 4 * g + 4), hring[:, g % 4, :, T - 1], 1.0, None, ALU.mult).then_inc(carried, 1)

                for g in range(NG):
                    for k in range(2):
                        dve.wait_ge(u_ok, u * 16 + 2 * g + k + 1)
                        if k == 0 and not (first and g < 4):
                            dve.wait_ge(g_ok, u * 8 + g - 3)
                        for j in (2 * k, 2 * k + 1):
                            tile = 4 * g + j
                            last = V.tensor_tensor_scan(
                                hring[:, g % 4, j, :], decay[:, tile, b, :],
                                ups[:, (2 * g + k) % 4, (j % 2) * T:(j % 2 + 1) * T],
                                car(tile, tile + 1), ALU.mult, ALU.add)
                        last.then_inc(scanned, 1)
                        if k == 0:
                            if g >= 1:
                                carry(g - 1)
                            if after and 2 * g in after:
                                after[2 * g]()
                    if after and 2 * g + 1 in after:
                        after[2 * g + 1]()
                carry(NG - 1)

            with dve.Fori(0, NC) as c:
                dve.wait_ge(x_in, c * 32 + 32)
                for k in range(NTT):
                    V.bn_stats(st[:, k, :], X[:, k, :]).then_inc(ln1_stat, 1)
                for k in range(NTT):
                    dve.wait_ge(ln1_stat, c * NTT + k + 1)
                    alone(dve)
                    V.bn_aggr(mv[:, k, :], st[:, k, :]).then_inc(ln1_agg, 1)
                dve.wait_ge(ln1_sd, c + 1)
                V.reciprocal(rs[:, :], sd[:, :]).then_inc(ln1_rs, 1)
                dve.wait_ge(ln1_rs, c + 1)
                for k in range(NTT):
                    V.tensor_scalar(nx[:, k, :], X[:, k, :], mv[:, k, 0:1], rs[:, k:k + 1],
                                    ALU.subtract, ALU.mult).then_inc(ln1_n, 1)
                dve.wait_ge(ln1_T, c + 1)
                for b in range(NB):
                    V.tensor_scalar(hT[:, b * T:(b + 1) * T], mm[:, 0, b * T:(b + 1) * T], modT[:, 1, b:b + 1],
                                    modT[:, 0, b:b + 1], ALU.mult, ALU.add).then_inc(h_T, 1)
                coef = log1p_coefficients(9)
                dve.wait_ge(dt_exp, c + 1)
                V.tensor_scalar(dpoly, dexp_, coef[-1], None, ALU.mult).then_inc(poly, 1)
                for k, a in enumerate(coef[-2::-1]):
                    dve.wait_ge(poly, c * 10 + k + 1)
                    V.scalar_tensor_tensor(dpoly, dpoly, a, dexp_, ALU.add, ALU.mult).then_inc(poly, 1)
                dve.wait_ge(poly, c * 10 + 10)
                dve.wait_ge(dt_relu, c + 1)
                V.tensor_tensor(delta[:, :, :].rearrange("p k d -> p (k d)"), dpoly, drelu, ALU.add).then_inc(delta_ok, 1)
                dve.wait_ge(decay_ok, c * 8 + 8)
                norms(c * UC, 0)
                inputs(c * UC, 0)
                scans(c * UC, 0, 0, True, first=True, after=at(D_NORMS=lambda: norms(c * UC + 1, 1), D_INPUTS=lambda: inputs(c * UC + 1, 1)))
                with dve.Fori(0, EV - 1) as i:
                    u = c * UC + i * 2
                    n = c * (UC - 2) + i * 2

                    def upd(w, b, nth):
                        def go():
                            update(w, b, i)
                            keep(w, b, i, nth)
                        return go

                    scans(u + 1, 1, i, False, after=at(
                        D_STATS=lambda: stats(u), D_NORM=lambda: normalise(u), D_UPDATE=upd(u, 0, n + 1),
                        D_NORMS=lambda: norms(u + 2, 0), D_INPUTS=lambda: inputs(u + 2, 0)))
                    scans(u + 2, 0, i + 1, False, after=at(
                        D_STATS=lambda: stats(u + 1), D_NORM=lambda: normalise(u + 1), D_UPDATE=upd(u + 1, 1, n + 2),
                        D_NORMS=lambda: norms(u + 3, 1), D_INPUTS=lambda: inputs(u + 3, 1)))
                w = c * UC + UC - 2
                scans(w + 1, 1, EV - 1, True, after=at(
                    D_STATS=lambda: stats(w), D_NORM=lambda: normalise(w),
                    D_UPDATE=lambda: update(w, 0, EV - 1, last=True)))
                stats(w + 1)
                normalise(w + 1)
                update(w + 1, 1, EV - 1, last=True)
                dve.wait_ge(z_silu, c * 2 + 2)
                V.tensor_tensor(sT[:, :, :].rearrange("p k (b t) -> p k b t", b=NB),
                                sT[:, :, :].rearrange("p k (b t) -> p k b t", b=NB),
                                yT[:, :, :, 1:T + 1].rearrange("p b k t -> p k b t"), ALU.mult).then_inc(s_ok, 1)
                dve.wait_ge(o_mm, c + 1)
                for b in range(NB):
                    V.tensor_scalar(xT[:, 0, b * T:(b + 1) * T], ups[:, 2, b * T:(b + 1) * T], modT[:, 2, b:b + 1],
                                    None, ALU.mult).then_inc(o_sc, 1)
                dve.wait_ge(o_t, c + 1)
                V.tensor_tensor(xmid[:, bass.ds(c, 1), :, :].rearrange("p o k d -> p (o k d)"),
                                ups[:, 3, :], X[:, :, :].rearrange("p k d -> p (k d)"), ALU.add).then_inc(x_mid, 1)

            with dve.Fori(0, NC) as c:
                xc = xmid[:, bass.ds(c, 1), :, :].rearrange("p o k d -> p (o k) d")
                dve.wait_ge(x_mid, NC + 1)
                for k in range(NTT):
                    V.bn_stats(st[:, k, :], xc[:, k, :]).then_inc(f_stat, 1)
                for k in range(NTT):
                    dve.wait_ge(f_stat, c * NTT + k + 1)
                    alone(dve)
                    V.bn_aggr(mv[:, k, :], st[:, k, :]).then_inc(f_agg, 1)
                dve.wait_ge(f_sd, c + 1)
                V.reciprocal(rs[:, :], sd[:, :]).then_inc(f_rs, 1)
                dve.wait_ge(f_rs, c + 1)
                for k in range(NTT):
                    V.tensor_scalar(nrm[:, :, :].rearrange("p a (x d) -> p (a x) d", d=DM)[:, k, :], xc[:, k, :],
                                    mv[:, k, 0:1], rs[:, k:k + 1],
                                    ALU.subtract, ALU.mult).then_inc(f_n, 1)
                dve.wait_ge(f_T, c + 1)
                for b in range(NB):
                    V.tensor_scalar(hT[:, b * T:(b + 1) * T], mm[:, 0, b * T:(b + 1) * T], modT[:, 4, b:b + 1],
                                    modT[:, 3, b:b + 1], ALU.mult, ALU.add).then_inc(f_h, 1)
                dve.wait_ge(r_mm, c + 1)
                V.tensor_scalar(lg, mm[:, 1, 0:4 * NE].rearrange("p (x e) -> p x e", x=4), 1.0 / TAU, None,
                                ALU.mult).then_inc(r_l, 1)
                dve.wait_ge(r_l, c + 1)
                alone(dve)
                for k in range(NTT):
                    V.max(top[:, k, :], lg[:, k, :]).then_inc(r_top, 1)
                dve.wait_ge(r_top, c * NTT + NTT)
                alone(dve)
                for k in range(NTT):
                    V.max_index(idx[:, k, :].bitcast(U32), top[:, k, :], lg[:, k, :]).then_inc(r_idx, 1)
                V.tensor_tensor(dif, top[:, :, 1], top[:, :, 0], ALU.subtract).then_inc(r_dif, 1)
                dve.wait_ge(r_idx, c * NTT + NTT)
                V.tensor_copy(idf, idx.bitcast(U32)).then_inc(r_p, 1)
                dve.wait_ge(r_e, c + 1)
                V.tensor_scalar(den, er, 1.0, None, ALU.add).then_inc(r_p, 1)
                dve.wait_ge(r_p, c * 4 + 2)
                V.reciprocal(p1, den).then_inc(r_p, 1)
                dve.wait_ge(r_p, c * 4 + 3)
                V.tensor_tensor(p2, er, p1, ALU.mult).then_inc(r_p, 1)
                dve.wait_ge(r_p, c * 4 + 4)
                for k in range(NTT):
                    V.tensor_scalar(wt[:, k, :], iota[:, :], idf[:, k, 0:1], p1[:, k:k + 1], ALU.is_equal,
                                    ALU.mult).then_inc(r_w, 1)
                    V.tensor_scalar(oh[:, k, :], iota[:, :], idf[:, k, 1:2], p2[:, k:k + 1], ALU.is_equal,
                                    ALU.mult).then_inc(r_w, 1)
                dve.wait_ge(r_w, c * 9 + 8)
                V.tensor_tensor(wt, wt, oh, ALU.add).then_inc(r_w, 1)
                for e in range(NE + 1):
                    for k in range(3 if e < NE else 2):
                        n = 3 * e + k
                        dve.wait_ge(gelu, c * (3 * NE + 2) + n + 1)
                        if e >= 2 and e < NE and k == 0:
                            dve.wait_ge(act_ok, c * NE + e - 1)
                        bias = be1s[:, e, k:k + 1] if e < NE else bs1s[:, k:k + 1]
                        dst = geg(e)[:, k, :] if e < NE else shg[:, k, :]
                        V.scalar_tensor_tensor(dst, abank(n), bias, gel[:, k, :], ALU.add, ALU.mult).then_inc(geglu, 1)
                dve.wait_ge(f_mm, c + 1)
                for b in range(NB):
                    V.tensor_scalar(xT[:, 0, b * T:(b + 1) * T], mm[:, 0, b * T:(b + 1) * T], bs2s[:, 0:1],
                                    modT[:, 5, b:b + 1], ALU.add, ALU.mult).then_inc(f_sc, 1)
                dve.wait_ge(f_t, c + 1)
                xo = xmid[:, bass.ds(c, 1), :, :].rearrange("p o k d -> p (o k d)")
                V.tensor_tensor(xo, mm[:, 1, :], xo, ALU.add).then_inc(x_out, 1)

        @block.tensor
        def _(pe):
            MM = nc.tensor.matmul
            TR = nc.tensor.transpose
            pe.wait_ge(w_in, 16 * NW)
            pe.wait_ge(silu_c, 1)
            for k in range(6):
                last = MM(mm[:, 0, NB * k:NB * k + NB], wmods[:, DM * k:DM * k + DM], silc[:, :], start=True, stop=True)
            last.then_inc(mod_mm, 1)

            def mix_x(b):
                for tt in range(NT):
                    MM(mm[:, 0, tt * DI:(tt + 1) * DI], ident[:, :], xm[:, b * NT + tt, 0:DI], start=(tt == 0),
                       stop=False, skip_group_check=True)

            def mix_bc(b):
                for tt in range(NT):
                    MM(mm[:, 1, 2 * NS * tt:2 * NS * (tt + 1)], ident[:, :], xm[:, b * NT + tt, DI:XW],
                       start=(tt == 0), stop=False, skip_group_check=True)

            def mix_y(vu, b):
                for tt in range(NT):
                    for k in range(2):
                        last = MM(mm[:, 1, 2 * NS * tt:2 * NS * (tt + 1)], yT[:, b, k, 128 * tt:128 * tt + 128],
                                  wbc[:, k, :], start=False, stop=(k == 1), skip_group_check=True)
                last.then_inc(bc_mm, 1)
                for tt in range(NT):
                    for k in range(2):
                        last = MM(mm[:, 0, tt * DI:(tt + 1) * DI], yT[:, b, k, 1 + 128 * tt:129 + 128 * tt],
                                  imix[:, k, :], start=False, stop=(k == 1), skip_group_check=True)
                last.then_inc(mix_mm, 1)

            def mix(vu, b):
                mix_x(b)
                mix_bc(b)
                mix_y(vu, b)

            def rep_c(vu, b):
                pe.wait_ge(cexp_ok, vu * 2 + 2)
                pe.wait_ge(v_ok, vu + 1)
                pe.wait_ge(xd_ok, vu + 1)
                for q in range(4):
                    for tt in range(NT):
                        last = TR(mm[:, q // 2, (q % 2) * T + 128 * tt:(q % 2) * T + 128 * tt + 128],
                                  cexp[:, tt, 4 * q:4 * q + 4, :].rearrange("p n d -> p (n d)"), ident[:, :])
                last.then_inc(crep_mm, 1)

            def start_y(u, b, first=False):
                if not first:
                    pe.wait_ge(y_ev, u * 2)
                pe.wait_ge(xd_ok, u + 1)
                for blk in range(2):
                    for tt in range(NT):
                        MM(yps[:, blk, 128 * tt:128 * tt + 128], xD[:, b, tt, 128 * blk:128 * blk + 128], ident[:, :],
                           start=(tt == 0), stop=False, skip_group_check=True)

            def reduce(u, g):
                pe.wait_ge(g_ok, u * 8 + g + 1)
                for j in range(4):
                    last = MM(yps[32 * j:32 * j + 32, g % 2, 0:T], sel[:, :], gring[:, g % 4, j, :],
                              start=False, stop=(g // 2 == 3), skip_group_check=True)
                last.then_inc(summed, 1)

            def inputs(u, g, first=False):
                q, blk = g // 2, g % 2
                for k in range(2):
                    if k == 0 and blk == 0:
                        pe.wait_ge(quarter, u * 4 + q + 1)
                    if not (first and g < 2):
                        pe.wait_ge(scanned, u * 16 + 2 * g + k - 3)
                    for j in (2 * k, 2 * k + 1):
                        for tt in range(NT):
                            last = TR(ups[:, (2 * g + k) % 4, (j % 2) * T + 128 * tt:(j % 2) * T + 128 * tt + 128],
                                      U[:, q, tt, 4 * blk + j, :], ident[:, :])
                    last.then_inc(u_ok, 1)

            def back_y(w):
                pe.wait_ge(y_ev, w * 2 + 2)
                for tt in range(NT):
                    for blk in range(2):
                        last = TR(mm[:, 0, tt * DI + 128 * blk:tt * DI + 128 * blk + 128],
                                  yTs[:, blk, 128 * tt:128 * tt + 128], ident[:, :])
                last.then_inc(y_t, 1)

            def forth_n(w):
                pe.wait_ge(l_n, w * 2 + 2)
                for blk in range(2):
                    for tt in range(NT):
                        last = TR(mm[:, 1, blk * T + 128 * tt:blk * T + 128 * tt + 128],
                                  nrm[:, tt, 128 * blk:128 * blk + 128], ident[:, :])
                last.then_inc(n_T, 1)

            def slot(u, b, after, first=False, prev=True):
                for g in range(NG):
                    inputs(u, g, first)
                    for f in after.get((g, 0), ()):
                        f()
                    if g < 2:
                        if prev:
                            reduce(u - 1, 6 + g)
                    else:
                        if g == 2:
                            start_y(u, b, first)
                        reduce(u, g - 2)
                    for f in after.get((g, 1), ()):
                        f()

            with pe.Fori(0, NC) as c:
                pe.wait_ge(ln1_n, c * NTT + NTT)
                pe.wait_ge(gates, 10)
                for k in range(NTT):
                    last = TR(mm[:, 0, 128 * k:128 * k + 128], nx[:, k, :], ident[:, :])
                last.then_inc(ln1_T, 1)
                pe.wait_ge(h_T, c * 2 + 2)
                for k in range(2):
                    MM(ups[:, k, :], winT[:, 128 * k:128 * k + 128], hT[:, :], start=True, stop=True).then_inc(x_mm, 1)
                pe.wait_ge(x_T, c * 2 + 2)
                for k in range(2):
                    last = MM(mm[0:RK, 1, :], wxdt[:, k, :], xT[:, k, :], start=(k == 0), stop=(k == 1))
                last.then_inc(dl_mm, 1)
                pe.wait_ge(dl_sb, c + 1)
                for k in range(NTT):
                    last = MM(ups[:, 2 + k // 2, (k % 2) * DI:(k % 2 + 1) * DI], dlow[:, 128 * k:128 * k + 128],
                              wdt9[:, :], start=True, stop=True)
                last.then_inc(dt_mm, 1)
                for k in range(NTT):
                    dst = mm[:, k, 0:XW] if k < 2 else yps[:, k - 2, 0:XW]
                    for m in range(2):
                        last = MM(dst, xT[:, m, 128 * k:128 * k + 128], wxm[:, m, :], start=(m == 0), stop=(m == 1))
                last.then_inc(xm_mm, 1)
                pe.wait_ge(drep_p, c * 2 + 2)
                pe.wait_ge(drep_a, c * 2 + 2)
                pe.wait_ge(dt_relu, c + 1)
                for k in range(8):
                    if k >= 4:
                        pe.wait_ge(decay_ok, c * 8 + k - 3)
                    for x in range(NTT):
                        last = TR(ups[:, k % 4, 128 * x:128 * x + 128],
                                  drep[:, x, k, :, :].rearrange("p n d -> p (n d)"), ident[:, :])
                    last.then_inc(dbank, 1)
                pe.wait_ge(y_zero, c + 1)
                pe.wait_ge(xm_sb, c * 2 + 2)
                pe.wait_ge(setup_dve, 4)
                mix(c * UC, 0)
                rep_c(c * UC, 0)
                pe.wait_ge(decay_ok, c * 8 + 8)

                def mix1():
                    pe.wait_ge(crep_ok, c * UC * 2 + 2)
                    mix(c * UC + 1, 1)
                slot(c * UC, 0, {(4, 1): [mix1], P_REP: [lambda: rep_c(c * UC + 1, 1)]}, first=True, prev=False)
                with pe.Fori(0, EV - 1) as i:
                    u = c * UC + i * 2
                    n = c * (UC - 2) + i * 2

                    def chain(w, b, nth):
                        def back():
                            pe.wait_ge(crep_ok, w * 2 + 4)
                            back_y(w)

                        def forth():
                            forth_n(w)
                            mix_x(b)

                        def again():
                            pe.wait_ge(gy_ok, w * 2 + 2)
                            mix_bc(b)
                            pe.wait_ge(y_new, nth)
                            pe.wait_ge(y_head, w + 1)
                            mix_y(w + 2, b)
                        return {P_BACK: [back], P_FORTH: [forth], P_MIX: [again], P_REP: [lambda: rep_c(w + 2, b)]}

                    slot(u + 1, 1, chain(u, 0, n + 1))
                    slot(u + 2, 0, chain(u + 1, 1, n + 2))
                w = c * UC + UC - 2

                def back_last():
                    pe.wait_ge(crep_ok, w * 2 + 4)
                    back_y(w)
                slot(w + 1, 1, {P_BACK: [back_last], P_FORTH: [lambda: forth_n(w)]})
                reduce(w + 1, 6)
                reduce(w + 1, 7)
                pe.wait_ge(gy_ok, w * 2 + 2)
                back_y(w + 1)
                forth_n(w + 1)
                pe.wait_ge(gy_ok, w * 2 + 4)
                pe.wait_ge(y_head, w + 2)
                for m in range(2):
                    MM(ups[:, m, :], winT[:, DI + 128 * m:DI + 128 * m + 128], hT[:, :], start=True, stop=False)
                    for b in range(NB):
                        for k in range(2):
                            last = MM(ups[:, m, b * T:(b + 1) * T], wzy[:, k, 128 * m:128 * m + 128], yT[:, b, k, 0:T],
                                      start=False, stop=(b == 1 and k == 1))
                    last.then_inc(z_mm, 1)
                pe.wait_ge(s_ok, c + 1)
                for m in range(2):
                    last = MM(ups[:, 2, :], wout[:, m, :], sT[:, m, :], start=(m == 0), stop=(m == 1))
                last.then_inc(o_mm, 1)
                pe.wait_ge(o_sc, c * 2 + 2)
                for k in range(NTT):
                    last = TR(ups[:, 3, 128 * k:128 * k + 128], xT[:, 0, 128 * k:128 * k + 128], ident[:, :])
                last.then_inc(o_t, 1)

            pe.wait_ge(fw_in, 16 * NFW)
            pe.wait_ge(setup_pool, 1)
            pe.wait_ge(x_mid, NC + 1)
            nrmx = nrm[:, :, :].rearrange("p a (x d) -> p (a x) d", d=DM)
            with pe.Fori(0, NC) as c:
                pe.wait_ge(f_n, c * NTT + NTT)
                for k in range(NTT):
                    last = TR(mm[:, 0, 128 * k:128 * k + 128], nrmx[:, k, :], ident[:, :])
                last.then_inc(f_T, 1)
                pe.wait_ge(f_h, c * 2 + 2)
                pe.wait_ge(x_out, c + 1)
                for k in range(NTT):
                    MM(mm[:, 1, NE * k:NE * k + NE], hT[:, 128 * k:128 * k + 128], wr[:, :], start=True, stop=False)
                    last = MM(mm[:, 1, NE * k:NE * k + NE], ones[:, :], brow[:, :], start=False, stop=True)
                last.then_inc(r_mm, 1)
                pe.wait_ge(r_w, c * 9 + 9)
                for k in range(NTT):
                    last = TR(mm[0:NE, 1, 128 * k:128 * k + 128], wt[:, k, :], ident[:, :])
                last.then_inc(w_T, 1)
                pe.wait_ge(w_Ts, c + 1)
                MM(mm[:, 0, :], be2s[:, :], wTs, start=True, stop=False, skip_group_check=True)
                NN = 3 * NE + 2

                def up(e):
                    for k in range(3 if e < NE else 2):
                        n = 3 * e + k
                        if n >= 3:
                            pe.wait_ge(geglu, c * NN + n - 2)
                        wa = we1[:, e, 128 * k:128 * k + 128] if e < NE else ws1[:, 128 * k:128 * k + 128]
                        wg = we1[:, e, HR + 128 * k:HR + 128 * k + 128] if e < NE else \
                            ws1[:, HS + 128 * k:HS + 128 * k + 128]
                        MM(abank(n), wa, hT[:, :], start=True, stop=True)
                        MM(gbank(n), wg, hT[:, :], start=True, stop=True).then_inc(ag_mm, 1)

                def dn(e):
                    if e < NE:
                        pe.wait_ge(act_ok, c * NE + e + 1)
                        for k in range(3):
                            last = MM(mm[:, 0, :], we2[:, e, k, :], actw(e)[:, k, :], start=False, stop=False,
                                      skip_group_check=True)
                    else:
                        pe.wait_ge(geglu, c * NN + NN)
                        for k in range(2):
                            last = MM(mm[:, 0, :], ws2[:, k, :], shg[:, k, :], start=False, stop=(k == 1),
                                      skip_group_check=True)
                    last.then_inc(down, 1)
                    if e == NE:
                        return last

                for e in range(NE + 1):
                    if e < NE:
                        if e >= 1:
                            pe.wait_ge(wb_sb, c * NE + e)
                        for k in range(NTT):
                            last = TR(mm[:, 1, 128 * k:128 * k + 128], wt[:, k, e:e + 1].to_broadcast([128, 128]),
                                      ident[:, :])
                        last.then_inc(wb_mm, 1)
                    up(e)
                    if e >= 1:
                        dn(e - 1)
                dn(NE)
                pe.wait_ge(down, c * (NE + 1) + NE + 1)
                pe.sem_inc(f_mm, 1)
                pe.wait_ge(f_sc, c * 2 + 2)
                for k in range(NTT):
                    last = TR(mm[:, 1, 128 * k:128 * k + 128], xT[:, 0, 128 * k:128 * k + 128], ident[:, :])
                last.then_inc(f_t, 1)


_SHAPE = (NB, L, DM)


def kernel(**inputs):
    import numpy as _np
    import concourse.bacc as _bacc
    from concourse import mybir as _mybir
    from concourse.bass_utils import run_bass_kernel_spmd as _run

    a = {k[3:]: _np.asarray(x) for k, x in inputs.items()}
    eye = _np.eye(128, dtype=_np.float32)
    consts = _np.concatenate([eye, _np.tile(_np.eye(32, dtype=_np.float32), (4, 1)),
                              _np.tile(_np.arange(NE, dtype=_np.float32), (128, 1))], axis=1)
    lay = dict(
        hidden=a["attn_hidden_states"], WinT=a["attn_W_in"].T, WxT=a["attn_W_x"].T,
        Wdt9=_np.concatenate([a["attn_W_dt"].T, a["attn_b_dt"][None, :]], axis=0),
        AlogS=a["attn_A_log"].reshape(2, 4, 32, 4, 4).transpose(4, 2, 3, 0, 1).reshape(128, NTILE),
        WbcT=a["attn_W_bc"].T, WzyT=a["attn_W_zy"].T, WmixT=a["attn_W_mix"].T,
        chanT=_np.stack([a["attn_ln_gamma"], a["attn_ln_beta"], a["attn_D"]], axis=1),
        WoutT=a["attn_W_out"].T,
        Ws1=a["ffn_Ws1"], bs1T=a["ffn_bs1"].reshape(-1, 128).T, Ws2=a["ffn_Ws2"], bs2T=a["ffn_bs2"][:, None],
        We1=a["ffn_We1"], be1T=a["ffn_be1"].reshape(-1, 128).T, We2=a["ffn_We2"], be2=a["ffn_be2"],
        Wr=a["ffn_Wr"], br=a["ffn_br"][None, :], cT=a["c"].T, wmod=a["wmod"], consts=consts)
    nc = _bacc.Bacc("TRN2", target_bir_lowering=False, num_devices=1)
    arrays, args = {}, []
    for name, x in lay.items():
        x = _np.ascontiguousarray(x)
        arrays[f"in_{name}"] = x
        args.append(nc.dram_tensor(f"in_{name}", x.shape, _mybir.dt.from_np(x.dtype), kind="ExternalInput").ap())
    args.append(nc.dram_tensor("out_0", _SHAPE, _mybir.dt.float32, kind="ExternalOutput").ap())
    adaln_block_kernel(nc, *args)
    r = _run(nc, [arrays], core_ids=[0])
    return r.results[0]["out_0"]
```

```python
import concourse.bass as bass
from concourse import mybir
from concourse.alu_op_type import AluOpType as ALU
from contextlib import ExitStack
import numpy as np


F32 = mybir.dt.float32
U32 = mybir.dt.uint32
ACT = mybir.ActivationFunctionType
AX = mybir.AxisListType

NB, L, DM = 2, 1024, 128
DI, NS, RK = 256, 16, 8
T = 256
NC = L // T
NT = T // 128
NTT = NB * NT
EV = 9
STEP = 0.99
EPS = 1e-5
NTILE = DI * NS // 128
NG = 8
UC = EV * NB
XW = DI + 2 * NS
NE, HR, HS = 12, 384, 256
TAU = 1.5
TOK = NB * T


P_BACK, P_FORTH, P_MIX, P_REP = ((1, 1), (3, 0), (4, 0), (6, 1))
A_SPLIT = (5, 6, 8, 2, 4)
PLACE = dict(zip(("D_STATS", "D_NORM", "D_UPDATE", "D_NORMS", "D_INPUTS"), (3, 4, 6, 8, 9)))


S_STATS, S_NORM, S_UPDATE, S_SILU = 4, 5, 7, 10


def log1p_coefficients(degree):
    k = np.arange(degree + 1)
    at = 0.5 + 0.5 * np.cos(np.pi * (k + 0.5) / (degree + 1))
    fit = np.polynomial.chebyshev.Chebyshev.fit(at, np.log1p(at) / at, degree, domain=[0, 1])
    return [float(x) for x in fit.convert(kind=np.polynomial.polynomial.Polynomial).coef]


def adaln_block_kernel(nc, hidden, WinT, WxT, Wdt9, AlogS, WbcT, WzyT, WmixT, chanT, WoutT,
                       Ws1, bs1T, Ws2, bs2T, We1, be1T, We2, be2, Wr, br, cT, wmod, consts, out):
    ctx = ExitStack()
    with ctx:
        def sb(name, shape, dt=F32):
            return ctx.enter_context(nc.sbuf_tensor(name, shape, dt))

        def ps(name, shape):
            return ctx.enter_context(nc.psum_tensor(name, shape, F32))

        def sem(name):
            return ctx.enter_context(nc.semaphore(name))

        ident = sb("ident", [128, 128])
        sel = sb("sel", [128, 32])
        iota = sb("iota", [128, NE])
        winT = sb("winT", [DM, 2 * DI])
        wxdt = sb("wxdt", [128, 2, RK])
        wxm = sb("wxm", [128, 2, XW])
        imix = sb("imix", [128, 2, DI])
        wbc = sb("wbc", [128, 2, 2 * NS])
        wzy = sb("wzy", [128, 2, DI])
        wout = sb("wout", [128, 2, DM])
        wdt9 = sb("wdt9", [RK + 1, DI])
        Aneg = sb("Aneg", [128, NTILE])
        chan = sb("chan", [128, 2, 2])
        damp = sb("damp", [128, 2, 2])
        Dbc = sb("Dbc", [128, DI])
        silc = sb("silc", [128, NB])
        modT = sb("modT", [128, 6, NB])
        modsg = sb("modsg", [128, 2, 6 * NB])
        wr = sb("wr", [DM, NE])
        brow = sb("brow", [1, NE])
        ones = sb("ones", [1, 128])
        be2s = sb("be2s", [NE, DM])
        bs1s = sb("bs1s", [128, 2 * HS // 128])
        bs2s = sb("bs2s", [128, 1])
        be1s = sb("be1s", [128, NE, 2 * HR // 128])
        nx = sb("nx", [128, NTT, DM])
        hT = sb("hT", [128, TOK])
        hTn = sb("hTn", [128, TOK])
        st1 = sb("st1", [128, NTT, 6])
        mv1 = sb("mv1", [128, NTT, 2])
        sd1 = sb("sd1", [128, NTT])
        rs1 = sb("rs1", [128, NTT])
        xT = sb("xT", [128, 2, TOK])
        dlow = sb("dlow", [RK + 1, TOK])
        delta = sb("delta", [128, NTT, DI])
        xm = sb("xm", [128, NTT, XW])
        decay = sb("decay", [128, NTILE, NB, T])
        yT = sb("yT", [128, NB, 2, T + 1])
        ylast = sb("ylast", [128, EV + 1, NB, 2])
        hcar = sb("hcar", [128, EV, NB, NTILE])
        v = sb("v", [128, NB, NT, DI])
        xD = sb("xD", [128, NB, NT, DI])
        bcs = sb("bcs", [128, NT, 2, NS])
        sq = sb("sq", [128, NT, 2, NS])
        ss = sb("ss", [128, NT, 2])
        sdb = sb("sdb", [128, NT, 2])
        rn = sb("rn", [128, NT, 2])
        Bn = sb("Bn", [128, NB, NT, NS])
        U = sb("U", [128, 4, NT, 8, 128])
        cexp = sb("cexp", [128, NT, NS, 32])
        crep = sb("crep", [128, NB, 4, T])
        hring = sb("hring", [128, 4, 4, T])
        gring = sb("gring", [128, 4, 4, T])
        yTs = sb("yTs", [128, 2, T])
        st = sb("st", [128, NTT, 6])
        mv = sb("mv", [128, NTT, 2])
        sd = sb("sd", [128, NTT])
        rs = sb("rs", [128, NTT])
        nrm = sb("nrm", [128, NT, DI])
        gy = sb("gy", [128, 2, T])
        xmid = sb("xmid", [128, NC, NTT, DM])
        ups = ps("ups", [128, 4, 512])
        yps = ps("yps", [128, 2, 512])
        mm = ps("mm", [128, 2, 512])

        w_in = sem("w_in"); silu_c = sem("silu_c"); mod_mm = sem("mod_mm"); mod_sb = sem("mod_sb")
        gates = sem("gates"); setup_dve = sem("setup_dve"); a_exp = sem("a_exp"); a_neg = sem("a_neg")
        setup_pool = sem("setup_pool")
        x_in = sem("x_in"); ln1_stat = sem("ln1_stat"); ln1_agg = sem("ln1_agg"); ln1_sd = sem("ln1_sd")
        ln1_rs = sem("ln1_rs"); ln1_n = sem("ln1_n"); ln1_T = sem("ln1_T"); h_T = sem("h_T")
        x_mm = sem("x_mm"); x_T = sem("x_T"); dl_mm = sem("dl_mm"); dl_sb = sem("dl_sb")
        dt_mm = sem("dt_mm"); xm_mm = sem("xm_mm"); xm_sb = sem("xm_sb"); dt_abs = sem("dt_abs")
        dt_exp = sem("dt_exp"); dt_relu = sem("dt_relu"); poly = sem("poly"); delta_ok = sem("delta_ok")
        drep_d = sem("drep_d"); drep_a = sem("drep_a"); dbank = sem("dbank"); decay_ok = sem("decay_ok")
        y_zero = sem("y_zero"); h_kept = sem("h_kept")
        mix_mm = sem("mix_mm"); bc_mm = sem("bc_mm"); bc_ok = sem("bc_ok"); m_step = sem("m_step"); bc_sd = sem("bc_sd")
        rn_ok = sem("rn_ok"); v_ok = sem("v_ok"); bn_ok = sem("bn_ok"); xd_ok = sem("xd_ok")
        cexp_ok = sem("cexp_ok"); crep_mm = sem("crep_mm"); crep_ok = sem("crep_ok")
        quarter = sem("quarter"); quarter_d = sem("quarter_d"); quarter_p = sem("quarter_p")
        u_ok = sem("u_ok"); scanned = sem("scanned"); carried = sem("carried")
        g_ok = sem("g_ok"); summed = sem("summed"); y_ev = sem("y_ev"); y_t = sem("y_t")
        l_stat = sem("l_stat"); l_agg = sem("l_agg"); l_sd = sem("l_sd"); l_rs = sem("l_rs")
        l_n = sem("l_n"); n_T = sem("n_T"); gy_ok = sem("gy_ok"); y_head = sem("y_head"); y_new = sem("y_new")
        y_tail = sem("y_tail")
        z_mm = sem("z_mm"); z_silu = sem("z_silu"); s_ok = sem("s_ok"); o_mm = sem("o_mm")
        o_sc = sem("o_sc"); o_t = sem("o_t"); x_mid = sem("x_mid")
        fw_in = sem("fw_in"); f_stat = sem("f_stat"); f_agg = sem("f_agg"); f_sd = sem("f_sd")
        f_rs = sem("f_rs"); f_n = sem("f_n"); f_T = sem("f_T"); f_h = sem("f_h"); r_mm = sem("r_mm")
        r_l = sem("r_l"); r_top = sem("r_top"); r_idx = sem("r_idx"); r_dif = sem("r_dif")
        r_e = sem("r_e"); r_p = sem("r_p"); r_w = sem("r_w"); w_T = sem("w_T"); w_Ts = sem("w_Ts")
        wb_mm = sem("wb_mm"); wb_sb = sem("wb_sb"); ag_mm = sem("ag_mm"); gelu = sem("gelu")
        geglu = sem("geglu"); act_ok = sem("act_ok"); down = sem("down"); f_mm = sem("f_mm")
        f_sc = sem("f_sc"); f_t = sem("f_t"); x_out = sem("x_out"); stored = sem("stored")

        def alone(eng):
            eng.nop(nofuse=True)

        def v_b_at_once(eng, b, q, tt):
            return eng.tensor_tensor(
                U[:, q, tt, :, :].rearrange("p k (n d) -> p k n d", n=4),
                v[:, b, tt, :].rearrange("p (k o d) -> p k o d", k=8, o=1).to_broadcast([128, 8, 4, 32]),
                Bn[:, b, tt, 4 * q:4 * q + 4].rearrange("p (o n m) -> p o n m", o=1, m=1).to_broadcast([128, 8, 4, 32]),
                ALU.mult)

        flat = decay[:, :, :, :].rearrange("p a b t -> p (a b t)")
        we1 = flat[:, 0:NE * 2 * HR].rearrange("p (e f) -> p e f", e=NE)
        o1 = NE * 2 * HR
        we2 = flat[:, o1:o1 + NE * HR].rearrange("p (e k f) -> p e k f", e=NE, k=3)
        o2 = o1 + NE * HR
        ws1 = flat[:, o2:o2 + 2 * HS]
        ws2 = flat[:, o2 + 2 * HS:o2 + 3 * HS].rearrange("p (k f) -> p k f", k=2)
        uflat = U[:, :, :, :, :].rearrange("p q t d n -> p (q t d n)")
        hflat = hring[:, :, :, :].rearrange("p s j t -> p (s j t)")
        gflat = gring[:, :, :, :].rearrange("p s j t -> p (s j t)")

        def drep(x):
            flat_x = (xT[:, :, :].rearrange("p k t -> p (k t)"), crep[:, 1, :, :].rearrange("p q t -> p (q t)"),
                      U[:, 3, 0, :, :].rearrange("p k d -> p (k d)"), U[:, 3, 1, :, :].rearrange("p k d -> p (k d)"))[x]
            return flat_x.rearrange("p (k n d) -> p k n d", k=8, n=4)

        sT = crep[:, 0, :, :].rearrange("p (k x) t -> p k (x t)", k=2)
        wmods = hflat[:, 0:6 * DM]
        dabs, dexp_, drelu, dpoly = (uflat[:, 1024 * k:1024 * (k + 1)] for k in range(4))
        NW = 14 + 2 + 2 + 2 + NB

        def geg(e):
            return hflat[:, (e % 2) * 1536:(e % 2) * 1536 + 1536].rearrange("p (k t) -> p k t", k=3)

        def actw(e):
            return gflat[:, (e % 2) * 1536:(e % 2) * 1536 + 1536].rearrange("p (k t) -> p k t", k=3)

        gel = uflat[:, 0:3 * TOK].rearrange("p (k t) -> p k t", k=3)
        shg = uflat[:, 3 * TOK:5 * TOK].rearrange("p (k t) -> p k t", k=2)
        wbs = uflat[:, 5 * TOK:7 * TOK].rearrange("p (s t) -> p s t", s=2)
        rt = uflat[:, 7 * TOK:8 * TOK]
        lg = rt[:, 0:48].rearrange("p (x e) -> p x e", x=4)
        top = rt[:, 48:80].rearrange("p (x e) -> p x e", x=4)
        idx = rt[:, 80:112].rearrange("p (x e) -> p x e", x=4)
        idf = rt[:, 112:144].rearrange("p (x e) -> p x e", x=4)
        dif = rt[:, 144:148]; er = rt[:, 148:152]; den = rt[:, 152:156]
        p1 = rt[:, 156:160]; p2 = rt[:, 160:164]
        oh = rt[:, 164:212].rearrange("p (x e) -> p x e", x=4)
        wt = rt[:, 212:260].rearrange("p (x e) -> p x e", x=4)
        wTs = nx[0:NE, 0:4, :].rearrange("p x t -> p (x t)")

        gated = nrm[:, :, :].rearrange("p a d -> p (a d)")

        def abank(n):
            return ups[:, n % 3, :]

        def gbank(n):
            return (ups[:, 3, :], yps[:, 0, :], yps[:, 1, :])[n % 3]

        block = ctx.enter_context(nc.Block())

        @block.sync
        def _(sp):
            def load(dst, src, s=w_in):
                sp.dma_start(dst, src).then_inc(s, 16)

            with nc.allow_non_contiguous_dma(reason="one-off weight loads with short rows"):
                load(ident[:, :], consts[:, 0:128])
                load(sel[:, :], consts[:, 128:160])
                load(iota[:, :], consts[:, 160:160 + NE])
                load(silc[:, :], cT)
                load(wmods, wmod)
                for c in range(NC):
                    for b in range(NB):
                        load(xmid[:, c, b * NT:(b + 1) * NT, :],
                             hidden[b, c * T:(c + 1) * T, :].rearrange("(u p) d -> p u d", p=128), w_in if c == 0 else x_in)
                load(Aneg[:, :], AlogS)
                load(winT[:, :], WinT)
                load(wxdt[:, :, :], WxT[:, 0:RK].rearrange("(k p) m -> p k m", p=128))
                load(wxm[:, :, 0:DI], WmixT.rearrange("(k p) m -> p k m", p=128))
                load(wxm[:, :, DI:XW], WxT[:, RK:RK + 2 * NS].rearrange("(k p) m -> p k m", p=128))
                load(wbc[:, :, :], WbcT.rearrange("(k p) m -> p k m", p=128))
                load(wzy[:, :, :], WzyT.rearrange("(k p) m -> p k m", p=128))
                load(wout[:, :, :], WoutT.rearrange("(k p) m -> p k m", p=128))
                load(wdt9[:, :], Wdt9)
                load(chan[:, :, 0:1], chanT[0:2 * 128, 0:1].rearrange("(k p) m -> p k m", p=128))
                load(chan[:, :, 1:2], chanT[0:2 * 128, 1:2].rearrange("(k p) m -> p k m", p=128))
                load(Dbc[:, :], chanT[:, 2:3].rearrange("d o -> o d").to_broadcast([128, DI]))
                load(wr[:, :], Wr)
                load(brow[:, :], br)
                load(be2s[:, :], be2)
                load(bs1s[:, :], bs1T, fw_in)
                load(bs2s[:, :], bs2T, fw_in)
                load(be1s[:, :, :], be1T.rearrange("p (e k) -> p e k", e=NE), fw_in)
            sp.wait_ge(scanned, NC * UC * 16)
            for e in range(NE):
                load(we1[:, e, :], We1[e, :, :], fw_in)
                load(we2[:, e, :, :], We2[e, :, :].rearrange("(k p) m -> p k m", p=128), fw_in)
            load(ws1, Ws1, fw_in)
            load(ws2, Ws2.rearrange("(k p) m -> p k m", p=128), fw_in)
            with sp.Fori(0, NC) as c:
                sp.wait_ge(x_out, c + 2)
                for b in range(NB):
                    sp.dma_start(out[b, bass.ds(c * T, T), :].rearrange("(u p) d -> p u d", p=128),
                                 xmid[:, bass.ds(c, 1), b * NT:(b + 1) * NT, :].rearrange("p o k d -> p (o k) d")).then_inc(stored, 16)
            sp.wait_ge(stored, NC * NB * 16)

        NFW = 3 + 2 * NE + 2

        @block.gpsimd
        def _(pool):
            nc.gpsimd.memset(dlow[:, :], 1.0)
            nc.gpsimd.memset(ylast[:, :, :, :], 0.0)
            nc.gpsimd.memset(hcar[:, :, :, :], 0.0)
            nc.gpsimd.memset(ones[:, :], 1.0).then_inc(setup_pool, 1)

            def multiply(u, b, first=None):
                for g in range(NG):
                    q = g // 2
                    if first is not None and g == 2:
                        pool.wait_ge(x_mid, first + 1)
                        alone(pool)
                        nc.gpsimd.memset(yT[:, :, :, :], 0.0).then_inc(y_zero, 1)
                    if g == 0:
                        pool.wait_ge(crep_ok, u * 2 + 2)
                    pool.wait_ge(scanned, u * 16 + 2 * g + 2)
                    if not (first is not None and g < 4):
                        pool.wait_ge(summed, u * 8 + g - 3)
                    nc.gpsimd.tensor_tensor(
                        gring[:, g % 4, :, :], hring[:, g % 4, :, :],
                        crep[:, b, q:q + 1, :].to_broadcast([128, 4, T]), ALU.mult).then_inc(g_ok, 1)

            with pool.Fori(0, NC) as c:
                pool.wait_ge(bn_ok, c * UC + 1)
                pool.wait_ge(v_ok, c * UC + 1)
                for q in (1, 2):
                    for tt in range(NT):
                        last = v_b_at_once(nc.gpsimd, 0, q, tt)
                    last.then_inc(quarter_p, 1)
                multiply(c * UC, 0, first=c)
                with pool.Fori(0, EV - 1) as i:
                    u = c * UC + i * 2
                    multiply(u + 1, 1)
                    multiply(u + 2, 0)
                multiply(c * UC + UC - 1, 1)

            with pool.Fori(0, NC) as c:
                for e in range(NE):
                    n = e + 1
                    pool.wait_ge(wb_sb, c * NE + e + 1)
                    pool.wait_ge(geglu, c * (3 * NE + 2) + 3 * e + 3)
                    if e >= 2:
                        pool.wait_ge(down, c * (NE + 1) + e - 1)
                    nc.gpsimd.tensor_tensor(
                        actw(e), geg(e),
                        wbs[:, e % 2, :].rearrange("p (o t) -> p o t", o=1).to_broadcast([128, 3, TOK]),
                        ALU.mult).then_inc(act_ok, 1)

        @block.scalar
        def _(act):
            A = nc.scalar.activation
            act.wait_ge(w_in, 16 * NW)
            A(silc[:, :], silc[:, :], ACT.Silu).then_inc(silu_c, 1)
            A(Aneg[:, :], Aneg[:, :], ACT.Exp).then_inc(a_exp, 1)

            def v_times_b(vu, b, h):
                q = h // 2
                if h == 0:
                    act.wait_ge(bn_ok, vu + 1)
                    act.wait_ge(v_ok, vu + 1)
                if h % 2 == 0:
                    act.wait_ge(u_ok, vu * 16 + 4 * q - 12)
                for n in (2 * (h % 2), 2 * (h % 2) + 1):
                    for tt in range(NT):
                        last = A(U[:, q, tt, :, 32 * n:32 * n + 32],
                                 v[:, b, tt, :].rearrange("p (k d) -> p k d", k=8),
                                 ACT.Copy, scale=Bn[:, b, tt, 4 * q + n:4 * q + n + 1])
                if h % 2:
                    last.then_inc(quarter, 1)

            def c_tiles(vu):
                act.wait_ge(bc_ok, vu + 1)
                A(sdb[:, :, :], ss[:, :, :], ACT.Sqrt).then_inc(bc_sd, 1)
                act.wait_ge(rn_ok, vu + 1)
                for tt in range(NT):
                    A(cexp[:, tt, :, :], bcs[:, tt, 1, :].rearrange("p (n o) -> p n o", o=1).to_broadcast([128, NS, 32]),
                      ACT.Copy, scale=rn[:, tt, 1:2]).then_inc(cexp_ok, 1)

            def c_out(vu, b):
                act.wait_ge(crep_mm, vu + 1)
                for k in range(2):
                    A(crep[:, b, 2 * k:2 * k + 2, :].rearrange("p q t -> p (q t)"), mm[:, k, :],
                      ACT.Copy).then_inc(crep_ok, 1)

            def form(vu, b):
                c_tiles(vu)
                for h in range(A_SPLIT[3]):
                    v_times_b(vu, b, h)
                c_out(vu, b)
                for h in range(A_SPLIT[3], A_SPLIT[4]):
                    v_times_b(vu, b, h)

            def decays(c, n):
                act.wait_ge(dbank, c * 16 + n + 1)
                k = n % 8
                src = ups[:, n % 4, :] if n < 8 else mm[:, n % 2, :]
                for q in ((0, 1) if n < 8 else (2, 3)):
                    tile = (2 * q + k // 4) * 4 + k % 4
                    last = A(decay[:, tile, :, :].rearrange("p b t -> p (b t)"), src, ACT.Exp,
                             scale=Aneg[:, tile:tile + 1])
                last.then_inc(decay_ok, 1)

            def slot(u, b, last=False, nxt=True, ahead=None):
                w, o = u - 1, 1 - b
                for blk in range(2):
                    act.wait_ge(summed, w * 8 + 7 + blk)
                    A(yTs[:, blk, :], yps[:, blk, 0:T], ACT.Copy).then_inc(y_ev, 1)
                for h in range(A_SPLIT[4], A_SPLIT[0]):
                    v_times_b(u, b, h)
                act.wait_ge(l_agg, w * 2 + 2)
                A(sd[:, 0:NT], mv[:, 0:NT, 1], ACT.Sqrt, bias=EPS).then_inc(l_sd, 1)
                for h in range(A_SPLIT[0], A_SPLIT[1]):
                    v_times_b(u, b, h)
                evac_norm(w, o, last)
                for h in range(A_SPLIT[1], 8):
                    v_times_b(u, b, h)
                if nxt:
                    form(u + 1, o)
                if ahead:
                    ahead()

            def evac_norm(w, b, last=False):
                act.wait_ge(n_T, w + 1)
                for blk in range(2):
                    src = mm[:, 1, blk * T:(blk + 1) * T]
                    if last:
                        A(yT[:, b, blk, 1:T + 1], src, ACT.Identity, bias=chan[:, blk, 1:2],
                          scale=chan[:, blk, 0:1]).then_inc(gy_ok, 1)
                    else:
                        A(gy[:, blk, :], src, ACT.Identity, bias=damp[:, blk, 1:2],
                          scale=damp[:, blk, 0:1]).then_inc(gy_ok, 1)

            def norm_in(c):
                act.wait_ge(ln1_agg, c * NTT + NTT)
                A(sd1[:, :], mv1[:, :, 1], ACT.Sqrt, bias=EPS).then_inc(ln1_sd, 1)

            def delta_in(c):
                for k in range(2):
                    act.wait_ge(x_mm, c * 2 + k + 1)
                    A(xT[:, k, :], mm[:, k, :], ACT.Copy).then_inc(x_T, 1)
                act.wait_ge(dl_mm, c + 1)
                A(dlow[0:RK, :], mm[0:RK, 1, :], ACT.Copy).then_inc(dl_sb, 1)
                act.wait_ge(dt_mm, c + 1)
                A(dabs, mm[:, :, :].rearrange("p k t -> p (k t)"), ACT.Abs).then_inc(dt_abs, 1)
                A(drelu, mm[:, :, :].rearrange("p k t -> p (k t)"), ACT.Relu).then_inc(dt_relu, 1)
                act.wait_ge(dt_abs, c + 1)
                A(dexp_, dabs, ACT.Exp, scale=-1.0).then_inc(dt_exp, 1)

            def xm_out(c):
                act.wait_ge(xm_mm, c + 1)
                for k in range(2):
                    A(xm[:, 2 * k:2 * k + 2, :], ups[:, 2 * k:2 * k + 2, 0:XW], ACT.Copy).then_inc(xm_sb, 1)

            def decay_start(c):
                act.wait_ge(delta_ok, c + 1)
                for k in range(2, 4):
                    A(drep(k), delta[:, k, :].rearrange("p (k o d) -> p k o d", k=8, o=1).to_broadcast([128, 8, 4, 32]),
                      ACT.Copy).then_inc(drep_a, 1)
                for n in range(8):
                    decays(c, n)

            def chunk(c, more):
                c_out(c * UC, 0)
                for n in range(8, 16):
                    decays(c, n)
                act.wait_ge(v_ok, c * UC + 1)
                act.wait_ge(bn_ok, c * UC + 1)
                for n in range(4):
                    for tt in range(NT):
                        last = A(U[:, 3, tt, :, 32 * n:32 * n + 32], v[:, 0, tt, :].rearrange("p (k d) -> p k d", k=8),
                                 ACT.Copy, scale=Bn[:, 0, tt, 12 + n:13 + n])
                last.then_inc(quarter, 4)
                form(c * UC + 1, 1)
                with act.Fori(0, EV - 1) as i:
                    u = c * UC + i * 2
                    slot(u + 1, 1)
                    slot(u + 2, 0)
                w = c * UC + UC - 2
                if more:
                    norm_in(c + 1)

                def ahead():
                    act.wait_ge(u_ok, (w + 1) * 16 + 8)
                    delta_in(c + 1)
                slot(w + 1, 1, last=True, nxt=False, ahead=ahead if more else None)
                for blk in range(2):
                    act.wait_ge(summed, (w + 1) * 8 + 7 + blk)
                    A(yTs[:, blk, :], yps[:, blk, 0:T], ACT.Copy).then_inc(y_ev, 1)
                if more:
                    xm_out(c + 1)
                act.wait_ge(l_agg, (w + 1) * 2 + 2)
                A(sd[:, 0:NT], mv[:, 0:NT, 1], ACT.Sqrt, bias=EPS).then_inc(l_sd, 1)
                evac_norm(w + 1, 1, last=True)
                if more:
                    c_tiles((c + 1) * UC)
                for m in range(2):
                    act.wait_ge(z_mm, c * 2 + m + 1)
                    A(sT[:, m, :], yps[:, m, :], ACT.Silu).then_inc(z_silu, 1)
                if more:
                    decay_start(c + 1)

            norm_in(0)
            act.wait_ge(setup_pool, 1)
            delta_in(0)
            xm_out(0)
            c_tiles(0)
            act.wait_ge(a_neg, 1)
            decay_start(0)
            with act.Fori(0, NC - 1) as c:
                chunk(c, True)
            chunk(NC - 1, False)

            act.wait_ge(fw_in, 16 * NFW)
            with act.Fori(0, NC) as c:
                act.wait_ge(f_agg, c * NTT + NTT)
                A(sd[:, :], mv[:, :, 1], ACT.Sqrt, bias=EPS).then_inc(f_sd, 1)
                act.wait_ge(r_dif, c + 1)
                A(er, dif, ACT.Exp).then_inc(r_e, 1)
                act.wait_ge(w_T, c + 1)
                A(wTs, mm[0:NE, 1, :], ACT.Copy).then_inc(w_Ts, 1)
                for e in range(NE + 1):
                    if e < NE:
                        act.wait_ge(wb_mm, c * NE + e + 1)
                        if e >= 2:
                            act.wait_ge(act_ok, c * NE + e - 1)
                        A(wbs[:, e % 2, :], mm[:, 1, :], ACT.Copy).then_inc(wb_sb, 1)
                    for k in range(3 if e < NE else 2):
                        n = 3 * e + k
                        act.wait_ge(ag_mm, c * (3 * NE + 2) + n + 1)
                        if n >= 3:
                            act.wait_ge(geglu, c * (3 * NE + 2) + n - 2)
                        bias = be1s[:, e, 3 + k:4 + k] if e < NE else bs1s[:, 2 + k:3 + k]
                        A(gel[:, k, :], gbank(n), ACT.Gelu, bias=bias).then_inc(gelu, 1)

        @block.vector
        def _(dve):
            V = nc.vector
            dve.wait_ge(w_in, 16 * NW)
            V.tensor_scalar(imix[:, :, :], wxm[:, :, 0:DI], -1.0, None, ALU.mult).then_inc(setup_dve, 1)
            dve.wait_ge(setup_dve, 1)
            for k in range(2):
                V.tensor_tensor(imix[:, k, 128 * k:128 * k + 128], imix[:, k, 128 * k:128 * k + 128], ident[:, :],
                                ALU.add).then_inc(setup_dve, 1)
            V.tensor_scalar(damp[:, :, :], chan[:, :, :], STEP, None, ALU.mult).then_inc(setup_dve, 1)
            dve.sem_inc(x_mid, 1)
            dve.sem_inc(x_out, 1)
            dve.wait_ge(a_exp, 1)
            V.tensor_scalar(Aneg[:, :], Aneg[:, :], -1.0, None, ALU.mult).then_inc(a_neg, 1)
            dve.wait_ge(mod_mm, 1)
            V.tensor_copy(modT[:, :, :].rearrange("p k b -> p (k b)"), mm[:, 0, 0:6 * NB]).then_inc(mod_sb, 1)
            dve.wait_ge(mod_sb, 1)
            sgn, mag = modsg[:, 0, :], modsg[:, 1, :]
            flatm = modT[:, :, :].rearrange("p k b -> p (k b)")
            V.tensor_scalar(sgn, flatm, 0.0, 2.0, ALU.is_ge, ALU.mult).then_inc(gates, 1)
            V.tensor_scalar(mag, flatm, -1.0, None, ALU.mult).then_inc(gates, 1)
            dve.wait_ge(gates, 2)
            V.tensor_scalar(sgn, sgn, -1.0, None, ALU.add).then_inc(gates, 1)
            V.tensor_tensor(mag, mag, flatm, ALU.max).then_inc(gates, 1)
            dve.wait_ge(gates, 4)
            V.tensor_scalar(mag, mag, 0.25, None, ALU.max).then_inc(gates, 1)
            dve.wait_ge(gates, 5)
            V.tensor_tensor(mag, mag, sgn, ALU.mult).then_inc(gates, 1)
            dve.wait_ge(gates, 6)
            for k in (2, 5):
                V.tensor_copy(modT[:, k, :], mag[:, NB * k:NB * k + NB]).then_inc(gates, 1)
            for k in (1, 4):
                V.tensor_scalar(modT[:, k, :], modT[:, k, :], 1.0, None, ALU.add).then_inc(gates, 1)
            dve.wait_ge(gates, 10)

            def norms(vu, b, nth):
                dve.wait_ge(bc_mm, nth)
                V.tensor_copy(bcs[:, :, :, :].rearrange("p t k n -> p (t k n)"), mm[:, 1, 0:NT * 2 * NS]).then_inc(m_step, 1)
                norms_from(vu)

            def norms_0(c):
                dve.wait_ge(xm_sb, c * 2 + 1)
                V.tensor_copy(bcs[:, :, :, :].rearrange("p t k n -> p t (k n)"), xm[:, 0:NT, DI:XW]).then_inc(m_step, 1)
                norms_from(c * UC)

            def norms_from(vu):
                dve.wait_ge(m_step, vu * 3 + 1)
                V.tensor_tensor(sq[:, :, :, :], bcs[:, :, :, :], bcs[:, :, :, :], ALU.mult).then_inc(m_step, 1)
                dve.wait_ge(m_step, vu * 3 + 2)
                V.tensor_reduce(ss[:, :, :], sq[:, :, :, :], AX.X, ALU.add).then_inc(m_step, 1)
                dve.wait_ge(m_step, vu * 3 + 3)
                V.tensor_scalar(ss[:, :, :], ss[:, :, :], EPS * EPS, None, ALU.max).then_inc(bc_ok, 1)

            def inverse(vu, b):
                dve.wait_ge(bc_sd, vu + 1)
                V.reciprocal(rn[:, :, :], sdb[:, :, :]).then_inc(rn_ok, 1)
                dve.wait_ge(rn_ok, vu + 1)
                V.tensor_tensor(Bn[:, b, :, :], bcs[:, :, 0, :], rn[:, :, 0:1].to_broadcast([128, NT, NS]),
                                ALU.mult).then_inc(bn_ok, 1)

            def v_in(xt, b):
                row = slice(b * NT, (b + 1) * NT)
                V.tensor_tensor(v[:, b, :, :], xt, delta[:, row, :], ALU.mult).then_inc(v_ok, 1)

            def xd_in(xt, b):
                V.tensor_tensor(xD[:, b, :, :], xt,
                                Dbc[:, :].rearrange("p (o d) -> p o d", o=1).to_broadcast([128, NT, DI]),
                                ALU.mult).then_inc(xd_ok, 1)

            def inputs(vu, b, nth):
                inverse(vu, b)
                dve.wait_ge(mix_mm, nth)
                xt = mm[:, 0, :].rearrange("p (t d) -> p t d", t=NT)
                v_in(xt, b)
                xd_in(xt, b)

            def stats(w):
                dve.wait_ge(y_t, w + 1)
                for tt in range(NT):
                    V.bn_stats(st[:, tt, :], mm[:, 0, tt * DI:(tt + 1) * DI]).then_inc(l_stat, 1)
                for tt in range(NT):
                    dve.wait_ge(l_stat, w * 2 + 1 + tt)
                    alone(dve)
                    V.bn_aggr(mv[:, tt, :], st[:, tt, :]).then_inc(l_agg, 1)

            def normalise(w):
                dve.wait_ge(l_sd, w + 1)
                V.reciprocal(rs[:, 0:NT], sd[:, 0:NT]).then_inc(l_rs, 1)
                dve.wait_ge(l_rs, w + 1)
                for tt in range(NT):
                    V.tensor_scalar(nrm[:, tt, :], mm[:, 0, tt * DI:(tt + 1) * DI], mv[:, tt, 0:1], rs[:, tt:tt + 1],
                                    ALU.subtract, ALU.mult).then_inc(l_n, 1)

            def update(w, b, i, last=False):
                V.tensor_scalar(yT[:, b, :, 0], ylast[:, i + 1, b, :] if last else ylast[:, bass.ds(i + 1, 1), b, :].rearrange("p o k -> p (o k)"), 1.0, None, ALU.mult).then_inc(y_head, 1)
                dve.wait_ge(gy_ok, w * 2 + 2)
                if last:
                    dve.wait_ge(y_head, w + 1)
                    V.tensor_scalar(ylast[:, i + 1, b, :], yT[:, b, :, T], 1.0, None, ALU.mult).then_inc(y_tail, 1)
                else:
                    V.scalar_tensor_tensor(yT[:, b, :, 1:T + 1], yT[:, b, :, 1:T + 1], 1.0 - STEP, gy[:, :, :],
                                           ALU.mult, ALU.add).then_inc(y_new, 1)

            def keep(w, b, i, nth):
                dve.wait_ge(y_new, nth)
                V.tensor_scalar(ylast[:, bass.ds(i + 1, 1), b, :].rearrange("p o k -> p (o k)"), yT[:, b, :, T], 1.0, None, ALU.mult).then_inc(y_tail, 1)

            def at(**steps):
                return {PLACE[k]: f for k, f in steps.items()}

            def scans(u, b, i, static, first=None, after=None):
                def car(t0, t1):
                    if static:
                        return hcar[:, i, b, t0:t1]
                    return hcar[:, bass.ds(i, 1), b, t0:t1].rearrange("p o k -> p (o k)")

                def carry(g):
                    dve.wait_ge(scanned, u * 16 + 2 * g + 2)
                    V.tensor_scalar(car(4 * g, 4 * g + 4), hring[:, g % 4, :, T - 1], 1.0, None, ALU.mult).then_inc(carried, 1)

                for g in range(NG):
                    if first is not None and g in (0, 1, 4, 5):
                        dve.wait_ge(decay_ok, first + (4, 8, 0, 0, 12, 16)[g])
                    for k in range(2):
                        dve.wait_ge(u_ok, u * 16 + 2 * g + k + 1)
                        if k == 0 and not (first is not None and g < 4):
                            dve.wait_ge(g_ok, u * 8 + g - 3)
                        for j in (2 * k, 2 * k + 1):
                            tile = 4 * g + j
                            last = V.tensor_tensor_scan(
                                hring[:, g % 4, j, :], decay[:, tile, b, :],
                                ups[:, (2 * g + k) % 4, (j % 2) * T:(j % 2 + 1) * T],
                                car(tile, tile + 1), ALU.mult, ALU.add)
                        last.then_inc(scanned, 1)
                        if k == 0:
                            if g >= 1:
                                carry(g - 1)
                            if after and 2 * g in after:
                                after[2 * g]()
                    if after and 2 * g + 1 in after:
                        after[2 * g + 1]()
                carry(NG - 1)

            coef = log1p_coefficients(9)

            def ln1_stats(c, static):
                x = xmid[:, c, :, :] if static else xmid[:, bass.ds(c, 1), :, :].rearrange("p o k d -> p (o k) d")
                for k in range(NTT):
                    V.bn_stats(st1[:, k, :], x[:, k, :]).then_inc(ln1_stat, 1)
                for k in range(NTT):
                    dve.wait_ge(ln1_stat, c * NTT + k + 1)
                    alone(dve)
                    V.bn_aggr(mv1[:, k, :], st1[:, k, :]).then_inc(ln1_agg, 1)

            def ln1_norm(c, static):
                x = xmid[:, c, :, :] if static else xmid[:, bass.ds(c, 1), :, :].rearrange("p o k d -> p (o k) d")
                dve.wait_ge(ln1_sd, c + 1)
                V.reciprocal(rs1[:, :], sd1[:, :]).then_inc(ln1_rs, 1)
                dve.wait_ge(ln1_rs, c + 1)
                for k in range(NTT):
                    V.tensor_scalar(nx[:, k, :], x[:, k, :], mv1[:, k, 0:1], rs1[:, k:k + 1],
                                    ALU.subtract, ALU.mult).then_inc(ln1_n, 1)

            def ln1_mod(c):
                dve.wait_ge(ln1_T, c + 1)
                for b in range(NB):
                    V.tensor_scalar(hTn[:, b * T:(b + 1) * T], mm[:, 1, b * T:(b + 1) * T], modT[:, 1, b:b + 1],
                                    modT[:, 0, b:b + 1], ALU.mult, ALU.add).then_inc(h_T, 1)

            def keep_h(c):
                dve.wait_ge(h_T, c * 2 + 2)
                V.tensor_scalar(hT[:, :], hTn[:, :], 1.0, None, ALU.mult).then_inc(h_kept, 1)

            def softplus(c, k0, k1):
                for k in range(k0, k1):
                    if k == 0:
                        dve.wait_ge(dt_exp, c + 1)
                        V.tensor_scalar(dpoly, dexp_, coef[-1], None, ALU.mult).then_inc(poly, 1)
                        continue
                    dve.wait_ge(poly, c * 10 + k)
                    if k < 10:
                        V.scalar_tensor_tensor(dpoly, dpoly, coef[9 - k], dexp_, ALU.add, ALU.mult).then_inc(poly, 1)
                    else:
                        dve.wait_ge(dt_relu, c + 1)
                        V.tensor_tensor(delta[:, :, :].rearrange("p k d -> p (k d)"), dpoly, drelu,
                                        ALU.add).then_inc(delta_ok, 1)

            def first_inputs(c):
                dve.wait_ge(delta_ok, c + 1)
                for k in range(2):
                    V.tensor_copy(
                        drep(k), delta[:, k, :].rearrange("p (k o d) -> p k o d", k=8, o=1).to_broadcast([128, 8, 4, 32])
                    ).then_inc(drep_d, 1)
                v_in(xm[:, 0:NT, 0:DI], 0)
                dve.wait_ge(v_ok, c * UC + 1)
                dve.wait_ge(bn_ok, c * UC + 1)
                for tt in range(NT):
                    last = v_b_at_once(V, 0, 0, tt)
                last.then_inc(quarter_d, 1)
                xd_in(xm[:, 0:NT, 0:DI], 0)

            def residual(c, static):
                x = xmid[:, c, :, :].rearrange("p k d -> p (k d)") if static else \
                    xmid[:, bass.ds(c, 1), :, :].rearrange("p o k d -> p (o k d)")
                dve.wait_ge(o_t, c + 1)
                V.tensor_tensor(x, yps[:, 1, :], x, ALU.add).then_inc(x_mid, 1)

            def chunk(c, more):
                scans(c * UC, 0, 0, True, first=c * 16,
                      after=at(D_NORMS=lambda: norms(c * UC + 1, 1, c * (UC - 1) + 1), D_INPUTS=lambda: inputs(c * UC + 1, 1, c * (UC - 1) + 1)))
                with dve.Fori(0, EV - 1) as i:
                    u = c * UC + i * 2
                    n = c * (UC - 2) + i * 2
                    m = c * (UC - 1) + i * 2 + 1

                    def upd(w, b, nth):
                        def go():
                            update(w, b, i)
                            keep(w, b, i, nth)
                        return go

                    scans(u + 1, 1, i, False, after=at(
                        D_STATS=lambda: stats(u), D_NORM=lambda: normalise(u), D_UPDATE=upd(u, 0, n + 1),
                        D_NORMS=lambda: norms(u + 2, 0, m + 1), D_INPUTS=lambda: inputs(u + 2, 0, m + 1)))
                    scans(u + 2, 0, i + 1, False, after=at(
                        D_STATS=lambda: stats(u + 1), D_NORM=lambda: normalise(u + 1), D_UPDATE=upd(u + 1, 1, n + 2),
                        D_NORMS=lambda: norms(u + 3, 1, m + 2), D_INPUTS=lambda: inputs(u + 3, 1, m + 2)))
                w = c * UC + UC - 2
                if more:
                    ln1_stats(c + 1, False)
                after = at(D_STATS=lambda: stats(w), D_NORM=lambda: normalise(w),
                           D_UPDATE=lambda: update(w, 0, EV - 1, last=True))
                if more:
                    after[0] = lambda: ln1_norm(c + 1, False)
                    after[2] = lambda: ln1_mod(c + 1)
                scans(w + 1, 1, EV - 1, True, after=after)
                if more:
                    softplus(c + 1, 0, S_STATS)
                stats(w + 1)
                if more:
                    softplus(c + 1, S_STATS, S_NORM)
                normalise(w + 1)
                if more:
                    norms_0(c + 1)
                    softplus(c + 1, S_NORM, S_UPDATE)
                    inverse((c + 1) * UC, 0)
                update(w + 1, 1, EV - 1, last=True)
                if more:
                    softplus(c + 1, S_UPDATE, S_SILU)
                dve.wait_ge(z_silu, c * 2 + 2)
                V.tensor_tensor(sT[:, :, :].rearrange("p k (b t) -> p k b t", b=NB),
                                sT[:, :, :].rearrange("p k (b t) -> p k b t", b=NB),
                                yT[:, :, :, 1:T + 1].rearrange("p b k t -> p k b t"), ALU.mult).then_inc(s_ok, 1)
                if more:
                    keep_h(c + 1)
                    softplus(c + 1, S_SILU, 11)
                dve.wait_ge(o_mm, c + 1)
                for b in range(NB):
                    V.tensor_scalar(gated[:, b * T:(b + 1) * T], yps[:, 0, b * T:(b + 1) * T], modT[:, 2, b:b + 1],
                                    None, ALU.mult).then_inc(o_sc, 1)
                if more:
                    first_inputs(c + 1)
                residual(c, not more)

            ln1_stats(0, True)
            ln1_norm(0, True)
            ln1_mod(0)
            keep_h(0)
            softplus(0, 0, 2)
            norms_0(0)
            softplus(0, 2, 6)
            inverse(0, 0)
            softplus(0, 6, 11)
            first_inputs(0)
            dve.wait_ge(x_in, 16 * NB * (NC - 1))
            with dve.Fori(0, NC - 1) as c:
                chunk(c, True)
            chunk(NC - 1, False)

            with dve.Fori(0, NC) as c:
                xc = xmid[:, bass.ds(c, 1), :, :].rearrange("p o k d -> p (o k) d")
                dve.wait_ge(x_mid, NC + 1)
                for k in range(NTT):
                    V.bn_stats(st[:, k, :], xc[:, k, :]).then_inc(f_stat, 1)
                for k in range(NTT):
                    dve.wait_ge(f_stat, c * NTT + k + 1)
                    alone(dve)
                    V.bn_aggr(mv[:, k, :], st[:, k, :]).then_inc(f_agg, 1)
                dve.wait_ge(f_sd, c + 1)
                V.reciprocal(rs[:, :], sd[:, :]).then_inc(f_rs, 1)
                dve.wait_ge(f_rs, c + 1)
                for k in range(NTT):
                    V.tensor_scalar(nrm[:, :, :].rearrange("p a (x d) -> p (a x) d", d=DM)[:, k, :], xc[:, k, :],
                                    mv[:, k, 0:1], rs[:, k:k + 1],
                                    ALU.subtract, ALU.mult).then_inc(f_n, 1)
                dve.wait_ge(f_T, c + 1)
                for b in range(NB):
                    V.tensor_scalar(hT[:, b * T:(b + 1) * T], mm[:, 0, b * T:(b + 1) * T], modT[:, 4, b:b + 1],
                                    modT[:, 3, b:b + 1], ALU.mult, ALU.add).then_inc(f_h, 1)
                dve.wait_ge(r_mm, c + 1)
                V.tensor_scalar(lg, mm[:, 1, 0:4 * NE].rearrange("p (x e) -> p x e", x=4), 1.0 / TAU, None,
                                ALU.mult).then_inc(r_l, 1)
                dve.wait_ge(r_l, c + 1)
                alone(dve)
                for k in range(NTT):
                    V.max(top[:, k, :], lg[:, k, :]).then_inc(r_top, 1)
                dve.wait_ge(r_top, c * NTT + NTT)
                alone(dve)
                for k in range(NTT):
                    V.max_index(idx[:, k, :].bitcast(U32), top[:, k, :], lg[:, k, :]).then_inc(r_idx, 1)
                V.tensor_tensor(dif, top[:, :, 1], top[:, :, 0], ALU.subtract).then_inc(r_dif, 1)
                dve.wait_ge(r_idx, c * NTT + NTT)
                V.tensor_copy(idf, idx.bitcast(U32)).then_inc(r_p, 1)
                dve.wait_ge(r_e, c + 1)
                V.tensor_scalar(den, er, 1.0, None, ALU.add).then_inc(r_p, 1)
                dve.wait_ge(r_p, c * 4 + 2)
                V.reciprocal(p1, den).then_inc(r_p, 1)
                dve.wait_ge(r_p, c * 4 + 3)
                V.tensor_tensor(p2, er, p1, ALU.mult).then_inc(r_p, 1)
                dve.wait_ge(r_p, c * 4 + 4)
                for k in range(NTT):
                    V.tensor_scalar(wt[:, k, :], iota[:, :], idf[:, k, 0:1], p1[:, k:k + 1], ALU.is_equal,
                                    ALU.mult).then_inc(r_w, 1)
                    V.tensor_scalar(oh[:, k, :], iota[:, :], idf[:, k, 1:2], p2[:, k:k + 1], ALU.is_equal,
                                    ALU.mult).then_inc(r_w, 1)
                dve.wait_ge(r_w, c * 9 + 8)
                V.tensor_tensor(wt, wt, oh, ALU.add).then_inc(r_w, 1)
                for e in range(NE + 1):
                    for k in range(3 if e < NE else 2):
                        n = 3 * e + k
                        dve.wait_ge(gelu, c * (3 * NE + 2) + n + 1)
                        if e >= 2 and e < NE and k == 0:
                            dve.wait_ge(act_ok, c * NE + e - 1)
                        bias = be1s[:, e, k:k + 1] if e < NE else bs1s[:, k:k + 1]
                        dst = geg(e)[:, k, :] if e < NE else shg[:, k, :]
                        V.scalar_tensor_tensor(dst, abank(n), bias, gel[:, k, :], ALU.add, ALU.mult).then_inc(geglu, 1)
                dve.wait_ge(f_mm, c + 1)
                for b in range(NB):
                    V.tensor_scalar(xT[:, 0, b * T:(b + 1) * T], mm[:, 0, b * T:(b + 1) * T], bs2s[:, 0:1],
                                    modT[:, 5, b:b + 1], ALU.add, ALU.mult).then_inc(f_sc, 1)
                dve.wait_ge(f_t, c + 1)
                xo = xmid[:, bass.ds(c, 1), :, :].rearrange("p o k d -> p (o k d)")
                V.tensor_tensor(xo, mm[:, 1, :], xo, ALU.add).then_inc(x_out, 1)

        @block.tensor
        def _(pe):
            MM = nc.tensor.matmul
            TR = nc.tensor.transpose
            pe.wait_ge(w_in, 16 * NW)
            pe.wait_ge(silu_c, 1)
            for k in range(6):
                last = MM(mm[:, 0, NB * k:NB * k + NB], wmods[:, DM * k:DM * k + DM], silc[:, :], start=True, stop=True)
            last.then_inc(mod_mm, 1)

            def mix_x(b):
                for tt in range(NT):
                    MM(mm[:, 0, tt * DI:(tt + 1) * DI], ident[:, :], xm[:, b * NT + tt, 0:DI], start=(tt == 0),
                       stop=False, skip_group_check=True)

            def mix_bc(b):
                for tt in range(NT):
                    MM(mm[:, 1, 2 * NS * tt:2 * NS * (tt + 1)], ident[:, :], xm[:, b * NT + tt, DI:XW],
                       start=(tt == 0), stop=False, skip_group_check=True)

            def mix_y(vu, b):
                for tt in range(NT):
                    for k in range(2):
                        last = MM(mm[:, 1, 2 * NS * tt:2 * NS * (tt + 1)], yT[:, b, k, 128 * tt:128 * tt + 128],
                                  wbc[:, k, :], start=False, stop=(k == 1), skip_group_check=True)
                last.then_inc(bc_mm, 1)
                for tt in range(NT):
                    for k in range(2):
                        last = MM(mm[:, 0, tt * DI:(tt + 1) * DI], yT[:, b, k, 1 + 128 * tt:129 + 128 * tt],
                                  imix[:, k, :], start=False, stop=(k == 1), skip_group_check=True)
                last.then_inc(mix_mm, 1)

            def mix(vu, b):
                mix_x(b)
                mix_bc(b)
                mix_y(vu, b)

            def rep_c(vu, b):
                pe.wait_ge(cexp_ok, vu * 2 + 2)
                pe.wait_ge(v_ok, vu + 1)
                pe.wait_ge(xd_ok, vu + 1)
                for q in range(4):
                    for tt in range(NT):
                        last = TR(mm[:, q // 2, (q % 2) * T + 128 * tt:(q % 2) * T + 128 * tt + 128],
                                  cexp[:, tt, 4 * q:4 * q + 4, :].rearrange("p n d -> p (n d)"), ident[:, :])
                last.then_inc(crep_mm, 1)

            def start_y(u, b, first=None):
                if first is None:
                    pe.wait_ge(y_ev, u * 2)
                else:
                    pe.wait_ge(x_mid, first + 1)
                pe.wait_ge(xd_ok, u + 1)
                for blk in range(2):
                    for tt in range(NT):
                        MM(yps[:, blk, 128 * tt:128 * tt + 128], xD[:, b, tt, 128 * blk:128 * blk + 128], ident[:, :],
                           start=(tt == 0), stop=False, skip_group_check=True)

            def reduce(u, g):
                pe.wait_ge(g_ok, u * 8 + g + 1)
                for j in range(4):
                    last = MM(yps[32 * j:32 * j + 32, g % 2, 0:T], sel[:, :], gring[:, g % 4, j, :],
                              start=False, stop=(g // 2 == 3), skip_group_check=True)
                last.then_inc(summed, 1)

            def inputs(u, g, first=None):
                q, blk = g // 2, g % 2
                for k in range(2):
                    if k == 0 and blk == 0:
                        if first is None or q == 3:
                            pe.wait_ge(quarter, u * 4 + q + 1)
                        elif q == 0:
                            pe.wait_ge(quarter_d, first + 1)
                        else:
                            pe.wait_ge(quarter_p, first * 2 + q)
                    if first is not None and g < 2:
                        pe.wait_ge(decay_ok, first * 16 + 5 + 2 * g + k)
                    else:
                        pe.wait_ge(scanned, u * 16 + 2 * g + k - 3)
                    for j in (2 * k, 2 * k + 1):
                        for tt in range(NT):
                            last = TR(ups[:, (2 * g + k) % 4, (j % 2) * T + 128 * tt:(j % 2) * T + 128 * tt + 128],
                                      U[:, q, tt, 4 * blk + j, :], ident[:, :])
                    last.then_inc(u_ok, 1)

            def back_y(w):
                pe.wait_ge(y_ev, w * 2 + 2)
                for tt in range(NT):
                    for blk in range(2):
                        last = TR(mm[:, 0, tt * DI + 128 * blk:tt * DI + 128 * blk + 128],
                                  yTs[:, blk, 128 * tt:128 * tt + 128], ident[:, :])
                last.then_inc(y_t, 1)

            def forth_n(w):
                pe.wait_ge(l_n, w * 2 + 2)
                for blk in range(2):
                    for tt in range(NT):
                        last = TR(mm[:, 1, blk * T + 128 * tt:blk * T + 128 * tt + 128],
                                  nrm[:, tt, 128 * blk:128 * blk + 128], ident[:, :])
                last.then_inc(n_T, 1)

            def slot(u, b, after, first=None, prev=True):
                for g in range(NG):
                    inputs(u, g, first)
                    for f in after.get((g, 0), ()):
                        f()
                    if g < 2:
                        if prev:
                            reduce(u - 1, 6 + g)
                    else:
                        if g == 2:
                            start_y(u, b, first)
                        reduce(u, g - 2)
                    for f in after.get((g, 1), ()):
                        f()

            def h_in(c):
                pe.wait_ge(ln1_n, c * NTT + NTT)
                for k in range(NTT):
                    last = TR(mm[:, 1, 128 * k:128 * k + 128], nx[:, k, :], ident[:, :])
                last.then_inc(ln1_T, 1)

            def x_in_T(c):
                pe.wait_ge(h_T, c * 2 + 2)
                for k in range(2):
                    MM(mm[:, k, :], winT[:, 128 * k:128 * k + 128], hTn[:, :], start=True, stop=True).then_inc(x_mm, 1)

            def delta_low(c):
                pe.wait_ge(x_T, c * 2 + 2)
                for k in range(2):
                    last = MM(mm[0:RK, 1, :], wxdt[:, k, :], xT[:, k, :], start=(k == 0), stop=(k == 1))
                last.then_inc(dl_mm, 1)

            def delta_up(c):
                pe.wait_ge(dl_sb, c + 1)
                for k in range(NTT):
                    last = MM(mm[:, k // 2, (k % 2) * DI:(k % 2 + 1) * DI], dlow[:, 128 * k:128 * k + 128],
                              wdt9[:, :], start=True, stop=True)
                last.then_inc(dt_mm, 1)

            def x_mixed(c):
                for k in range(NTT):
                    for m in range(2):
                        last = MM(ups[:, k, 0:XW], xT[:, m, 128 * k:128 * k + 128], wxm[:, m, :], start=(m == 0), stop=(m == 1))
                last.then_inc(xm_mm, 1)

            def delta_bank(c, n):
                if n == 0:
                    pe.wait_ge(drep_d, c * 2 + 2)
                    pe.wait_ge(drep_a, c * 2 + 2)
                    pe.wait_ge(xm_sb, c * 2 + 2)
                if n >= 8:
                    pe.wait_ge(decay_ok, c * 16 + n - 1)
                elif n >= 4:
                    pe.wait_ge(decay_ok, c * 16 + n - 3)
                for x in range(NTT):
                    dst = ups[:, n % 4, 128 * x:128 * x + 128] if n < 8 else mm[:, n % 2, 128 * x:128 * x + 128]
                    last = TR(dst, drep(x)[:, n % 8, :, :].rearrange("p n d -> p (n d)"), ident[:, :])
                last.then_inc(dbank, 1)

            def chunk(c, more):
                def delta_banks(*ns):
                    def go():
                        for n in ns:
                            if n == 8:
                                pe.wait_ge(crep_ok, c * UC * 2 + 2)
                            delta_bank(c, n)
                    return go

                def mix1():
                    pe.wait_ge(decay_ok, c * 16 + 16)
                    pe.wait_ge(y_zero, c + 1)
                    pe.wait_ge(setup_dve, 4)
                    mix(c * UC + 1, 1)
                slot(c * UC, 0, {(0, 0): [lambda: rep_c(c * UC, 0)], (0, 1): [delta_banks(8, 9)], (1, 0): [delta_banks(10)],
                                 (1, 1): [delta_banks(11, 12)], (2, 0): [delta_banks(13)], (2, 1): [delta_banks(14)],
                                 (3, 0): [delta_banks(15)], (4, 1): [mix1],
                                 P_REP: [lambda: rep_c(c * UC + 1, 1)]}, first=c, prev=False)
                with pe.Fori(0, EV - 1) as i:
                    u = c * UC + i * 2
                    n = c * (UC - 2) + i * 2

                    def chain(w, b, nth):
                        def back():
                            pe.wait_ge(crep_ok, w * 2 + 4)
                            back_y(w)

                        def forth():
                            forth_n(w)
                            mix_x(b)

                        def again():
                            pe.wait_ge(gy_ok, w * 2 + 2)
                            mix_bc(b)
                            pe.wait_ge(y_new, nth)
                            pe.wait_ge(y_head, w + 1)
                            mix_y(w + 2, b)
                        return {P_BACK: [back], P_FORTH: [forth], P_MIX: [again], P_REP: [lambda: rep_c(w + 2, b)]}

                    slot(u + 1, 1, chain(u, 0, n + 1))
                    slot(u + 2, 0, chain(u + 1, 1, n + 2))
                w = c * UC + UC - 2

                def back_last():
                    pe.wait_ge(crep_ok, w * 2 + 4)
                    back_y(w)
                after = {P_BACK: [back_last], P_FORTH: [lambda: forth_n(w)]}
                if more:
                    n = c + 1

                    def h_first():
                        pe.wait_ge(crep_ok, w * 2 + 4)
                        h_in(n)

                    def forth_after():
                        pe.wait_ge(h_T, n * 2 + 2)
                        forth_n(w)

                    def x_after():
                        pe.wait_ge(gy_ok, w * 2 + 2)
                        x_in_T(n)
                    after = {(0, 1): [h_first], P_BACK: [back_last], P_FORTH: [forth_after], (4, 0): [x_after],
                             (5, 0): [lambda: delta_low(n)], (6, 0): [lambda: delta_up(n)]}
                slot(w + 1, 1, after)
                reduce(w + 1, 6)
                if more:
                    pe.wait_ge(scanned, (w + 1) * 16 + 16)
                    x_mixed(n)
                reduce(w + 1, 7)
                if more:
                    pe.wait_ge(dt_relu, n + 1)
                else:
                    pe.wait_ge(gy_ok, w * 2 + 2)
                back_y(w + 1)
                pe.wait_ge(h_kept, c + 1)
                pe.wait_ge(gy_ok, w * 2 + 2)
                pe.wait_ge(y_head, w + 1)

                def z_part(m, b):
                    for k in range(2):
                        last = MM(yps[:, m, b * T:(b + 1) * T], wzy[:, k, 128 * m:128 * m + 128], yT[:, b, k, 0:T],
                                  start=False, stop=(b == 1 and k == 1), skip_group_check=True)
                    return last
                for m in range(2):
                    MM(yps[:, m, :], winT[:, DI + 128 * m:DI + 128 * m + 128], hT[:, :], start=True, stop=False,
                       skip_group_check=True)
                z_part(0, 0)
                forth_n(w + 1)
                z_part(1, 0)
                pe.wait_ge(gy_ok, w * 2 + 4)
                pe.wait_ge(y_head, w + 2)
                for m in range(2):
                    z_part(m, 1).then_inc(z_mm, 1)
                pe.wait_ge(s_ok, c + 1)
                for m in range(2):
                    last = MM(yps[:, 0, :], wout[:, m, :], sT[:, m, :], start=(m == 0), stop=(m == 1))
                last.then_inc(o_mm, 1)
                pe.wait_ge(o_sc, c * 2 + 2)
                for k in range(NTT):
                    last = TR(yps[:, 1, 128 * k:128 * k + 128], gated[:, 128 * k:128 * k + 128], ident[:, :])
                last.then_inc(o_t, 1)
                if more:
                    for k in range(8):
                        delta_bank(n, k)

            pe.wait_ge(gates, 10)
            h_in(0)
            x_in_T(0)
            delta_low(0)
            delta_up(0)
            x_mixed(0)
            for k in range(8):
                delta_bank(0, k)
            with pe.Fori(0, NC - 1) as c:
                chunk(c, True)
            chunk(NC - 1, False)

            pe.wait_ge(fw_in, 16 * NFW)
            pe.wait_ge(setup_pool, 1)
            pe.wait_ge(x_mid, NC + 1)
            nrmx = nrm[:, :, :].rearrange("p a (x d) -> p (a x) d", d=DM)
            with pe.Fori(0, NC) as c:
                pe.wait_ge(f_n, c * NTT + NTT)
                for k in range(NTT):
                    last = TR(mm[:, 0, 128 * k:128 * k + 128], nrmx[:, k, :], ident[:, :])
                last.then_inc(f_T, 1)
                pe.wait_ge(f_h, c * 2 + 2)
                pe.wait_ge(x_out, c + 1)
                for k in range(NTT):
                    MM(mm[:, 1, NE * k:NE * k + NE], hT[:, 128 * k:128 * k + 128], wr[:, :], start=True, stop=False)
                    last = MM(mm[:, 1, NE * k:NE * k + NE], ones[:, :], brow[:, :], start=False, stop=True)
                last.then_inc(r_mm, 1)
                pe.wait_ge(r_w, c * 9 + 9)
                for k in range(NTT):
                    last = TR(mm[0:NE, 1, 128 * k:128 * k + 128], wt[:, k, :], ident[:, :])
                last.then_inc(w_T, 1)
                pe.wait_ge(w_Ts, c + 1)
                MM(mm[:, 0, :], be2s[:, :], wTs, start=True, stop=False, skip_group_check=True)
                NN = 3 * NE + 2

                def up(e):
                    for k in range(3 if e < NE else 2):
                        n = 3 * e + k
                        if n >= 3:
                            pe.wait_ge(geglu, c * NN + n - 2)
                        wa = we1[:, e, 128 * k:128 * k + 128] if e < NE else ws1[:, 128 * k:128 * k + 128]
                        wg = we1[:, e, HR + 128 * k:HR + 128 * k + 128] if e < NE else \
                            ws1[:, HS + 128 * k:HS + 128 * k + 128]
                        MM(abank(n), wa, hT[:, :], start=True, stop=True)
                        MM(gbank(n), wg, hT[:, :], start=True, stop=True).then_inc(ag_mm, 1)

                def dn(e):
                    if e < NE:
                        pe.wait_ge(act_ok, c * NE + e + 1)
                        for k in range(3):
                            last = MM(mm[:, 0, :], we2[:, e, k, :], actw(e)[:, k, :], start=False, stop=False,
                                      skip_group_check=True)
                    else:
                        pe.wait_ge(geglu, c * NN + NN)
                        for k in range(2):
                            last = MM(mm[:, 0, :], ws2[:, k, :], shg[:, k, :], start=False, stop=(k == 1),
                                      skip_group_check=True)
                    last.then_inc(down, 1)
                    if e == NE:
                        return last

                for e in range(NE + 1):
                    if e < NE:
                        if e >= 1:
                            pe.wait_ge(wb_sb, c * NE + e)
                        for k in range(NTT):
                            last = TR(mm[:, 1, 128 * k:128 * k + 128], wt[:, k, e:e + 1].to_broadcast([128, 128]),
                                      ident[:, :])
                        last.then_inc(wb_mm, 1)
                    up(e)
                    if e >= 1:
                        dn(e - 1)
                dn(NE)
                pe.wait_ge(down, c * (NE + 1) + NE + 1)
                pe.sem_inc(f_mm, 1)
                pe.wait_ge(f_sc, c * 2 + 2)
                for k in range(NTT):
                    last = TR(mm[:, 1, 128 * k:128 * k + 128], xT[:, 0, 128 * k:128 * k + 128], ident[:, :])
                last.then_inc(f_t, 1)


_SHAPE = (NB, L, DM)


def kernel(**inputs):
    import numpy as _np
    import concourse.bacc as _bacc
    from concourse import mybir as _mybir
    from concourse.bass_utils import run_bass_kernel_spmd as _run

    a = {k[3:]: _np.asarray(x) for k, x in inputs.items()}
    eye = _np.eye(128, dtype=_np.float32)
    consts = _np.concatenate([eye, _np.tile(_np.eye(32, dtype=_np.float32), (4, 1)),
                              _np.tile(_np.arange(NE, dtype=_np.float32), (128, 1))], axis=1)
    lay = dict(
        hidden=a["attn_hidden_states"], WinT=a["attn_W_in"].T, WxT=a["attn_W_x"].T,
        Wdt9=_np.concatenate([a["attn_W_dt"].T, a["attn_b_dt"][None, :]], axis=0),
        AlogS=a["attn_A_log"].reshape(2, 4, 32, 4, 4).transpose(4, 2, 3, 0, 1).reshape(128, NTILE),
        WbcT=a["attn_W_bc"].T, WzyT=a["attn_W_zy"].T, WmixT=a["attn_W_mix"].T,
        chanT=_np.stack([a["attn_ln_gamma"], a["attn_ln_beta"], a["attn_D"]], axis=1),
        WoutT=a["attn_W_out"].T,
        Ws1=a["ffn_Ws1"], bs1T=a["ffn_bs1"].reshape(-1, 128).T, Ws2=a["ffn_Ws2"], bs2T=a["ffn_bs2"][:, None],
        We1=a["ffn_We1"], be1T=a["ffn_be1"].reshape(-1, 128).T, We2=a["ffn_We2"], be2=a["ffn_be2"],
        Wr=a["ffn_Wr"], br=a["ffn_br"][None, :], cT=a["c"].T, wmod=a["wmod"], consts=consts)
    nc = _bacc.Bacc("TRN2", target_bir_lowering=False, num_devices=1)
    arrays, args = {}, []
    for name, x in lay.items():
        x = _np.ascontiguousarray(x)
        arrays[f"in_{name}"] = x
        args.append(nc.dram_tensor(f"in_{name}", x.shape, _mybir.dt.from_np(x.dtype), kind="ExternalInput").ap())
    args.append(nc.dram_tensor("out_0", _SHAPE, _mybir.dt.float32, kind="ExternalOutput").ap())
    adaln_block_kernel(nc, *args)
    r = _run(nc, [arrays], core_ids=[0])
    return r.results[0]["out_0"]
```

```python
import concourse.bass as bass
from concourse import mybir
from concourse.alu_op_type import AluOpType as ALU
from contextlib import ExitStack
import numpy as np


F32 = mybir.dt.float32
U32 = mybir.dt.uint32
ACT = mybir.ActivationFunctionType
AX = mybir.AxisListType

NB, L, DM = 2, 1024, 128
DI, NS, RK = 256, 16, 8
T = 256
NC = L // T
NT = T // 128
NTT = NB * NT
EV = 9
STEP = 0.99
EPS = 1e-5
NTILE = DI * NS // 128
NG = 8
UC = EV * NB
XW = DI + 2 * NS
NE, HR, HS = 12, 384, 256
TAU = 1.5
TOK = NB * T


P_BACK, P_FORTH, P_MIX, P_REP = ((1, 2), (3, 1), (4, 1), (7, 0))
D_STATS, D_AGGR, D_NORM, D_UPDATE, D_COPY, D_SQUARE, D_SUM, D_FLOOR, D_INVERSE, D_INPUTS, D_KEEP, D_DX = \
    (7, 8, 8, 13, 17, 18, 18, 18, 19, 19, 17, 23)
A_C, A_END, A_COPY, A_ROOT, A_NORM = (2, 4, 4, 5, 6)
S_STATS, S_NORM, S_UPDATE, S_SILU = 4, 5, 7, 11

OWN = 2


def log1p_coefficients(degree):
    k = np.arange(degree + 1)
    at = 0.5 + 0.5 * np.cos(np.pi * (k + 0.5) / (degree + 1))
    fit = np.polynomial.chebyshev.Chebyshev.fit(at, np.log1p(at) / at, degree, domain=[0, 1])
    return [float(x) for x in fit.convert(kind=np.polynomial.polynomial.Polynomial).coef]


def adaln_block_kernel(nc, hidden, WinT, WxT, Wdt9, AlogS, WbcT, WzyT, WmixT, chanT, WoutT,
                       Ws1, bs1T, Ws2, bs2T, We1, be1T, We2, be2, Wr, br, cT, wmod, consts, out):
    ctx = ExitStack()
    with ctx:
        def sb(name, shape, dt=F32):
            return ctx.enter_context(nc.sbuf_tensor(name, shape, dt))

        def ps(name, shape):
            return ctx.enter_context(nc.psum_tensor(name, shape, F32))

        def sem(name):
            return ctx.enter_context(nc.semaphore(name))

        ident = sb("ident", [128, 128])
        sel = sb("sel", [128, 32])
        iota = sb("iota", [128, NE])
        winT = sb("winT", [DM, 2 * DI])
        wxdt = sb("wxdt", [128, 2, RK])
        wxm = sb("wxm", [128, 2, XW])
        imix = sb("imix", [128, 2, DI])
        wbc = sb("wbc", [128, 2, 2 * NS])
        wzy = sb("wzy", [128, 2, DI])
        wout = sb("wout", [128, 2, DM])
        wdt9 = sb("wdt9", [RK + 1, DI])
        Aneg = sb("Aneg", [128, NTILE])
        chan = sb("chan", [128, 2, 2])
        damp = sb("damp", [128, 2, 2])
        Dbc = sb("Dbc", [128, DI])
        silc = sb("silc", [128, NB])
        modT = sb("modT", [128, 6, NB])
        modsg = sb("modsg", [128, 2, 6 * NB])
        wr = sb("wr", [DM, NE])
        brow = sb("brow", [128, NE])
        be2s = sb("be2s", [NE, DM])
        bs1s = sb("bs1s", [128, 2 * HS // 128])
        bs2s = sb("bs2s", [128, 1])
        be1s = sb("be1s", [128, NE, 2 * HR // 128])
        nx = sb("nx", [128, NTT, DM])
        hT = sb("hT", [128, TOK])
        hTn = sb("hTn", [128, TOK])
        st1 = sb("st1", [128, NTT, 6])
        mv1 = sb("mv1", [128, NTT, 2])
        sd1 = sb("sd1", [128, NTT])
        rs1 = sb("rs1", [128, NTT])
        xT = sb("xT", [128, 2, TOK])
        dlow = sb("dlow", [RK + 1, TOK])
        delta = sb("delta", [128, NTT, DI])
        xm = sb("xm", [128, NTT, XW])
        decay = sb("decay", [128, NTILE, NB, T])
        yT = sb("yT", [128, NB, 2, T + 1])
        ylast = sb("ylast", [128, EV + 1, NB, 2])
        hcar = sb("hcar", [128, EV, NB, NTILE])
        v = sb("v", [128, NB, NT, DI])
        xD = sb("xD", [128, NB, NT, DI])
        bcs = sb("bcs", [128, NT, 2, NS])
        sq = sb("sq", [128, NT, 2, NS])
        ss = sb("ss", [128, NT, 2])
        sdb = sb("sdb", [128, NT, 2])
        rn = sb("rn", [128, NT, 2])
        Bn = sb("Bn", [128, NB, NT, NS])
        U = sb("U", [128, 4, NT, 8, 128])
        cexp = sb("cexp", [128, NT, NS, 32])
        crep = sb("crep", [128, NB, 4, T])
        hring = sb("hring", [128, 4, 4, T])
        gring = sb("gring", [128, 4, 4, T])
        yTs = sb("yTs", [128, 2, T])
        st = sb("st", [128, NTT, 6])
        mv = sb("mv", [128, NTT, 2])
        sd = sb("sd", [128, NTT])
        rs = sb("rs", [128, NTT])
        nrm = sb("nrm", [128, NT, DI])
        gy = sb("gy", [128, 2, T])
        xmid = sb("xmid", [128, NC, NTT, DM])
        ups = ps("ups", [128, 4, 512])
        yps = ps("yps", [128, 2, 512])
        mm = ps("mm", [128, 2, 512])

        w_first = sem("w_first"); w_second = sem("w_second"); w_in = sem("w_in"); silu_c = sem("silu_c"); mod_mm = sem("mod_mm"); mod_sb = sem("mod_sb")
        gates = sem("gates"); setup_dve = sem("setup_dve"); a_exp = sem("a_exp"); a_neg = sem("a_neg")
        setup_pool = sem("setup_pool")
        x_in = sem("x_in"); ln1_stat = sem("ln1_stat"); ln1_agg = sem("ln1_agg"); ln1_sd = sem("ln1_sd")
        ln1_rs = sem("ln1_rs"); ln1_n = sem("ln1_n"); ln1_T = sem("ln1_T"); h_T = sem("h_T")
        x_mm = sem("x_mm"); x_T = sem("x_T"); dl_mm = sem("dl_mm"); dl_sb = sem("dl_sb")
        dt_mm = sem("dt_mm"); xm_mm = sem("xm_mm"); xm_sb = sem("xm_sb"); dt_abs = sem("dt_abs")
        dt_exp = sem("dt_exp"); dt_relu = sem("dt_relu"); poly = sem("poly"); delta_ok = sem("delta_ok")
        drep_d = sem("drep_d"); drep_a = sem("drep_a"); dbank = sem("dbank"); decay_ok = sem("decay_ok")
        y_zero = sem("y_zero"); h_kept = sem("h_kept")
        mix_mm = sem("mix_mm"); bc_mm = sem("bc_mm"); bc_ok = sem("bc_ok"); m_step = sem("m_step"); bc_sd = sem("bc_sd")
        rn_ok = sem("rn_ok"); v_ok = sem("v_ok"); bn_ok = sem("bn_ok"); xd_ok = sem("xd_ok")
        cexp_ok = sem("cexp_ok"); crep_mm = sem("crep_mm"); crep_ok = sem("crep_ok")
        quarter = sem("quarter"); quarter_d = sem("quarter_d"); quarter_p = sem("quarter_p")
        u_ok = sem("u_ok"); scanned = sem("scanned"); carried = sem("carried")
        g_ok = sem("g_ok"); g_own = sem("g_own"); summed = sem("summed"); y_ev = sem("y_ev"); y_t = sem("y_t")
        l_stat = sem("l_stat"); l_agg = sem("l_agg"); l_sd = sem("l_sd"); l_rs = sem("l_rs")
        l_n = sem("l_n"); n_T = sem("n_T"); gy_ok = sem("gy_ok"); y_head = sem("y_head"); y_new = sem("y_new")
        y_tail = sem("y_tail")
        z_mm = sem("z_mm"); z_silu = sem("z_silu"); s_ok = sem("s_ok"); o_mm = sem("o_mm")
        o_sc = sem("o_sc"); o_t = sem("o_t"); x_mid = sem("x_mid")
        fw_in = sem("fw_in"); f_stat = sem("f_stat"); f_agg = sem("f_agg"); f_sd = sem("f_sd")
        f_rs = sem("f_rs"); f_n = sem("f_n"); f_T = sem("f_T"); f_h = sem("f_h"); r_mm = sem("r_mm")
        r_l = sem("r_l"); r_top = sem("r_top"); r_idx = sem("r_idx"); r_dif = sem("r_dif")
        r_e = sem("r_e"); r_p = sem("r_p"); r_w = sem("r_w"); w_c = sem("w_c"); w_T = sem("w_T"); w_Ts = sem("w_Ts")
        wb_mm = sem("wb_mm"); wb_sb = sem("wb_sb"); ag_mm = sem("ag_mm"); gelu = sem("gelu")
        geglu = sem("geglu"); act_ok = sem("act_ok"); down = sem("down"); f_mm = sem("f_mm")
        f_sc = sem("f_sc"); f_t = sem("f_t"); x_out = sem("x_out"); stored = sem("stored")

        def alone(eng):
            eng.nop(nofuse=True)

        def v_b_at_once(eng, b, q, tt):
            return eng.tensor_tensor(
                U[:, q, tt, :, :].rearrange("p k (n d) -> p k n d", n=4),
                v[:, b, tt, :].rearrange("p (k o d) -> p k o d", k=8, o=1).to_broadcast([128, 8, 4, 32]),
                Bn[:, b, tt, 4 * q:4 * q + 4].rearrange("p (o n m) -> p o n m", o=1, m=1).to_broadcast([128, 8, 4, 32]),
                ALU.mult)

        flat = decay[:, :, :, :].rearrange("p a b t -> p (a b t)")
        we1 = flat[:, 0:NE * 2 * HR].rearrange("p (e f) -> p e f", e=NE)
        o1 = NE * 2 * HR
        we2 = flat[:, o1:o1 + NE * HR].rearrange("p (e k f) -> p e k f", e=NE, k=3)
        o2 = o1 + NE * HR
        ws1 = flat[:, o2:o2 + 2 * HS]
        ws2 = flat[:, o2 + 2 * HS:o2 + 3 * HS].rearrange("p (k f) -> p k f", k=2)
        uflat = U[:, :, :, :, :].rearrange("p q t d n -> p (q t d n)")
        hflat = hring[:, :, :, :].rearrange("p s j t -> p (s j t)")
        gflat = gring[:, :, :, :].rearrange("p s j t -> p (s j t)")

        def drep(x):
            flat_x = (xT[:, :, :].rearrange("p k t -> p (k t)"), crep[:, 1, :, :].rearrange("p q t -> p (q t)"),
                      U[:, 3, 0, :, :].rearrange("p k d -> p (k d)"), U[:, 3, 1, :, :].rearrange("p k d -> p (k d)"))[x]
            return flat_x.rearrange("p (k n d) -> p k n d", k=8, n=4)

        sT = hflat[:, 0:2 * TOK].rearrange("p (k t) -> p k t", k=2)
        wmods = hflat[:, 0:6 * DM]
        dabs, dexp_, drelu, dpoly = (uflat[:, 1024 * k:1024 * (k + 1)] for k in range(4))
        N_FIRST, N_SECOND, NW, N_X = 5, 5, 6, 2 + NB * (NC - 1) + 4

        def geg(e):
            return hflat[:, (e % 2) * 1536:(e % 2) * 1536 + 1536].rearrange("p (k t) -> p k t", k=3)

        def actw(e):
            return gflat[:, (e % 2) * 1536:(e % 2) * 1536 + 1536].rearrange("p (k t) -> p k t", k=3)

        gel = uflat[:, 0:3 * TOK].rearrange("p (k t) -> p k t", k=3)
        shg = uflat[:, 3 * TOK:5 * TOK].rearrange("p (k t) -> p k t", k=2)
        wbs = uflat[:, 5 * TOK:7 * TOK].rearrange("p (s t) -> p s t", s=2)
        wTs = uflat[0:NE, 8 * TOK:12 * TOK].rearrange("p (c t) -> p c t", c=NC)
        hTf = crep[:, :, :, :].rearrange("p b q t -> p (b q t)").rearrange("p (c t) -> p c t", c=NC)
        nrmx = hflat[:, 2 * TOK:6 * TOK].rearrange("p (x d) -> p x d", d=DM)
        NRT = NC * NTT
        at_r = [12 * TOK]

        def route(n, shape):
            i = at_r[0]
            at_r[0] += NRT * n
            r = uflat[:, i:at_r[0]]
            return r.rearrange("p (x e) -> p x e", x=NRT) if shape else r

        stf = route(6, True); mvf = route(2, True); sdf = route(1, False); rsf = route(1, False)
        lg = route(NE, True)
        top = route(8, True)
        idx = route(8, True)
        idf = route(8, True)
        dif = route(1, False); er = route(1, False); den = route(1, False); p1 = route(1, False); p2 = route(1, False)
        oh = route(NE, True)
        wt = route(NE, True)
        wtc = oh[:, 0:NTT, :]

        gated = nrm[:, :, :].rearrange("p a d -> p (a d)")

        def abank(n):
            return ups[:, n % 3, :]

        def gbank(n):
            return (ups[:, 3, :], yps[:, 0, :], yps[:, 1, :])[n % 3]

        block = ctx.enter_context(nc.Block())

        @block.sync
        def _(sp):
            def load(dst, src, s=w_in):
                sp.dma_start(dst, src).then_inc(s, 16)

            with nc.allow_non_contiguous_dma(reason="one-off weight loads with short rows"):
                load(silc[:, :], cT, w_first)
                load(wmods, wmod, w_first)
                for b in range(NB):
                    load(xmid[:, 0, b * NT:(b + 1) * NT, :], hidden[b, 0:T, :].rearrange("(u p) d -> p u d", p=128), w_first)
                load(ident[:, :], consts[:, 0:128], w_first)
                load(winT[:, :], WinT, w_second)
                load(wxdt[:, :, :], WxT[:, 0:RK].rearrange("(k p) m -> p k m", p=128), w_second)
                load(wdt9[:, :], Wdt9, w_second)
                load(wxm[:, :, 0:DI], WmixT.rearrange("(k p) m -> p k m", p=128), w_second)
                load(wxm[:, :, DI:XW], WxT[:, RK:RK + 2 * NS].rearrange("(k p) m -> p k m", p=128), w_second)
                load(Aneg[:, :], AlogS)
                load(Dbc[:, :], chanT[:, 2:3].rearrange("d o -> o d").to_broadcast([128, DI]))
                load(sel[:, :], consts[:, 128:160])
                load(wbc[:, :, :], WbcT.rearrange("(k p) m -> p k m", p=128))
                load(chan[:, :, 0:1], chanT[0:2 * 128, 0:1].rearrange("(k p) m -> p k m", p=128))
                load(chan[:, :, 1:2], chanT[0:2 * 128, 1:2].rearrange("(k p) m -> p k m", p=128))
                load(wzy[:, :, :], WzyT.rearrange("(k p) m -> p k m", p=128), x_in)
                load(wout[:, :, :], WoutT.rearrange("(k p) m -> p k m", p=128), x_in)
                for c in range(1, NC):
                    for b in range(NB):
                        load(xmid[:, c, b * NT:(b + 1) * NT, :],
                             hidden[b, c * T:(c + 1) * T, :].rearrange("(u p) d -> p u d", p=128), x_in)
                load(iota[:, :], consts[:, 160:160 + NE], x_in)
                load(wr[:, :], Wr, x_in)
                load(brow[:, :], br.to_broadcast([128, NE]), x_in)
                load(be2s[:, :], be2, x_in)
                load(bs1s[:, :], bs1T, fw_in)
                load(bs2s[:, :], bs2T, fw_in)
                load(be1s[:, :, :], be1T.rearrange("p (e k) -> p e k", e=NE), fw_in)
            sp.wait_ge(scanned, NC * UC * 16)
            for e in range(NE):
                load(we1[:, e, :], We1[e, :, :], fw_in)
                load(we2[:, e, :, :], We2[e, :, :].rearrange("(k p) m -> p k m", p=128), fw_in)
            load(ws1, Ws1, fw_in)
            load(ws2, Ws2.rearrange("(k p) m -> p k m", p=128), fw_in)
            with sp.Fori(0, NC) as c:
                sp.wait_ge(x_out, c + 2)
                for b in range(NB):
                    sp.dma_start(out[b, bass.ds(c * T, T), :].rearrange("(u p) d -> p u d", p=128),
                                 xmid[:, bass.ds(c, 1), b * NT:(b + 1) * NT, :].rearrange("p o k d -> p (o k) d")).then_inc(stored, 16)
            sp.wait_ge(stored, NC * NB * 16)

        NFW = 3 + 2 * NE + 2

        @block.gpsimd
        def _(pool):
            nc.gpsimd.memset(dlow[:, :], 1.0)
            nc.gpsimd.memset(ylast[:, :, :, :], 0.0)
            nc.gpsimd.memset(hcar[:, :, :, :], 0.0).then_inc(setup_pool, 1)

            def multiply(u, b, first=None):
                for g in range(NG):
                    q = g // 2
                    if first is not None and g == 2:
                        pool.wait_ge(x_mid, first + 1)
                        alone(pool)
                        nc.gpsimd.memset(yT[:, :, :, :], 0.0).then_inc(y_zero, 1)
                    if g == 0:
                        pool.wait_ge(crep_ok, u * 2 + 2)
                    pool.wait_ge(scanned, u * 16 + 2 * g + 2)
                    if not (first is not None and g < 4):
                        pool.wait_ge(summed, u * 8 + g - 3)
                    n = 4 - OWN if g == NG - 1 else 4
                    nc.gpsimd.tensor_tensor(
                        gring[:, g % 4, 0:n, :], hring[:, g % 4, 0:n, :],
                        crep[:, b, q:q + 1, :].to_broadcast([128, n, T]), ALU.mult).then_inc(g_ok, 1)

            with pool.Fori(0, NC) as c:
                pool.wait_ge(bn_ok, c * UC + 1)
                pool.wait_ge(v_ok, c * UC + 1)
                for q in (1, 2):
                    for tt in range(NT):
                        last = v_b_at_once(nc.gpsimd, 0, q, tt)
                    last.then_inc(quarter_p, 1)
                multiply(c * UC, 0, first=c)
                with pool.Fori(0, EV - 1) as i:
                    u = c * UC + i * 2
                    multiply(u + 1, 1)
                    multiply(u + 2, 0)
                multiply(c * UC + UC - 1, 1)

            with pool.Fori(0, NC) as c:
                for e in range(NE):
                    n = e + 1
                    pool.wait_ge(wb_sb, c * NE + e + 1)
                    pool.wait_ge(geglu, c * (3 * NE + 2) + 3 * e + 3)
                    if e >= 2:
                        pool.wait_ge(down, c * (NE + 1) + e - 1)
                    nc.gpsimd.tensor_tensor(
                        actw(e), geg(e),
                        wbs[:, e % 2, :].rearrange("p (o t) -> p o t", o=1).to_broadcast([128, 3, TOK]),
                        ALU.mult).then_inc(act_ok, 1)

        @block.scalar
        def _(act):
            A = nc.scalar.activation
            act.wait_ge(w_first, 16 * N_FIRST)
            A(silc[:, :], silc[:, :], ACT.Silu).then_inc(silu_c, 1)

            def v_times_b(vu, b, h):
                q = h // 2
                if h == 0:
                    act.wait_ge(bn_ok, vu + 1)
                    act.wait_ge(v_ok, vu + 1)
                if h % 2 == 0:
                    act.wait_ge(u_ok, vu * 16 + 4 * q - 12)
                for n in (2 * (h % 2), 2 * (h % 2) + 1):
                    for tt in range(NT):
                        last = A(U[:, q, tt, :, 32 * n:32 * n + 32],
                                 v[:, b, tt, :].rearrange("p (k d) -> p k d", k=8),
                                 ACT.Copy, scale=Bn[:, b, tt, 4 * q + n:4 * q + n + 1])
                if h % 2:
                    last.then_inc(quarter, 1)

            def c_tiles(vu):
                act.wait_ge(bc_ok, vu + 1)
                A(sdb[:, :, :], ss[:, :, :], ACT.Sqrt).then_inc(bc_sd, 1)
                act.wait_ge(rn_ok, vu + 1)
                for tt in range(NT):
                    A(cexp[:, tt, :, :], bcs[:, tt, 1, :].rearrange("p (n o) -> p n o", o=1).to_broadcast([128, NS, 32]),
                      ACT.Copy, scale=rn[:, tt, 1:2]).then_inc(cexp_ok, 1)

            def c_out(vu, b):
                act.wait_ge(crep_mm, vu + 1)
                for k in range(2):
                    A(crep[:, b, 2 * k:2 * k + 2, :].rearrange("p q t -> p (q t)"), mm[:, k, :],
                      ACT.Copy).then_inc(crep_ok, 1)

            def form(vu, b):
                c_tiles(vu)
                for h in range(A_C):
                    v_times_b(vu, b, h)
                c_out(vu, b)
                for h in range(A_C, A_END):
                    v_times_b(vu, b, h)

            def decays(c, n):
                act.wait_ge(dbank, c * 16 + n + 1)
                k = n % 8
                src = ups[:, n, :] if n < 4 else mm[:, n % 2, :]
                for q in ((0, 1) if n < 8 else (2, 3)):
                    tile = (2 * q + k // 4) * 4 + k % 4
                    last = A(decay[:, tile, :, :].rearrange("p b t -> p (b t)"), src, ACT.Exp,
                             scale=Aneg[:, tile:tile + 1])
                last.then_inc(decay_ok, 1)

            def slot(u, b, last=False, nxt=True, ahead=None):
                w, o = u - 1, 1 - b
                for blk in range(2):
                    act.wait_ge(summed, w * 8 + 7 + blk)
                    A(yTs[:, blk, :], yps[:, blk, 0:T], ACT.Copy).then_inc(y_ev, 1)
                    if blk == 0:
                        for h in range(A_END, A_COPY):
                            v_times_b(u, b, h)
                for h in range(A_COPY, A_ROOT):
                    v_times_b(u, b, h)
                act.wait_ge(l_agg, w * 2 + 2)
                A(sd[:, 0:NT], mv[:, 0:NT, 1], ACT.Sqrt, bias=EPS).then_inc(l_sd, 1)
                for h in range(A_ROOT, A_NORM):
                    v_times_b(u, b, h)
                evac_norm(w, o, last)
                for h in range(A_NORM, 8):
                    v_times_b(u, b, h)
                if nxt:
                    form(u + 1, o)
                if ahead:
                    ahead()

            def evac_norm(w, b, last=False):
                act.wait_ge(n_T, w + 1)
                for blk in range(2):
                    src = mm[:, 1, blk * T:(blk + 1) * T]
                    if last:
                        A(yT[:, b, blk, 1:T + 1], src, ACT.Identity, bias=chan[:, blk, 1:2],
                          scale=chan[:, blk, 0:1]).then_inc(gy_ok, 1)
                    else:
                        A(gy[:, blk, :], src, ACT.Identity, bias=damp[:, blk, 1:2],
                          scale=damp[:, blk, 0:1]).then_inc(gy_ok, 1)

            def norm_in(c):
                act.wait_ge(ln1_agg, c * NTT + NTT)
                A(sd1[:, :], mv1[:, :, 1], ACT.Sqrt, bias=EPS).then_inc(ln1_sd, 1)

            def delta_in(c):
                for k in range(2):
                    act.wait_ge(x_mm, c * 2 + k + 1)
                    A(xT[:, k, :], mm[:, k, :], ACT.Copy).then_inc(x_T, 1)
                act.wait_ge(dl_mm, c + 1)
                A(dlow[0:RK, :], mm[0:RK, 1, :], ACT.Copy).then_inc(dl_sb, 1)
                act.wait_ge(dt_mm, c + 1)
                A(dabs, mm[:, :, :].rearrange("p k t -> p (k t)"), ACT.Abs).then_inc(dt_abs, 1)
                A(drelu, mm[:, :, :].rearrange("p k t -> p (k t)"), ACT.Relu).then_inc(dt_relu, 1)
                act.wait_ge(dt_abs, c + 1)
                A(dexp_, dabs, ACT.Exp, scale=-1.0).then_inc(dt_exp, 1)

            def xm_out(c):
                act.wait_ge(xm_mm, c + 1)
                for k in range(2):
                    A(xm[:, 2 * k:2 * k + 2, :], ups[:, 2 * k:2 * k + 2, 0:XW], ACT.Copy).then_inc(xm_sb, 1)

            def decay_start(c):
                act.wait_ge(delta_ok, c + 1)
                for k in range(2, 4):
                    A(drep(k), delta[:, k, :].rearrange("p (k o d) -> p k o d", k=8, o=1).to_broadcast([128, 8, 4, 32]),
                      ACT.Copy).then_inc(drep_a, 1)
                for n in range(8):
                    decays(c, n)

            def chunk(c, more):
                for n in range(8, 16):
                    decays(c, n)
                act.wait_ge(v_ok, c * UC + 1)
                act.wait_ge(bn_ok, c * UC + 1)
                for n in range(4):
                    for tt in range(NT):
                        last = A(U[:, 3, tt, :, 32 * n:32 * n + 32], v[:, 0, tt, :].rearrange("p (k d) -> p k d", k=8),
                                 ACT.Copy, scale=Bn[:, 0, tt, 12 + n:13 + n])
                last.then_inc(quarter, 4)

                form(c * UC + 1, 1)
                with act.Fori(0, EV - 1) as i:
                    u = c * UC + i * 2
                    slot(u + 1, 1)
                    slot(u + 2, 0)
                w = c * UC + UC - 2
                if more:
                    norm_in(c + 1)

                def ahead():
                    act.wait_ge(u_ok, (w + 1) * 16 + 8)
                    delta_in(c + 1)
                slot(w + 1, 1, last=True, nxt=False, ahead=ahead if more else None)
                for blk in range(2):
                    act.wait_ge(summed, (w + 1) * 8 + 7 + blk)
                    A(yTs[:, blk, :], yps[:, blk, 0:T], ACT.Copy).then_inc(y_ev, 1)
                if more:
                    xm_out(c + 1)
                act.wait_ge(l_agg, (w + 1) * 2 + 2)
                A(sd[:, 0:NT], mv[:, 0:NT, 1], ACT.Sqrt, bias=EPS).then_inc(l_sd, 1)
                evac_norm(w + 1, 1, last=True)
                if more:
                    c_tiles((c + 1) * UC)
                for m in range(2):
                    act.wait_ge(z_mm, c * 2 + m + 1)
                    A(sT[:, m, :], yps[:, m, :], ACT.Silu).then_inc(z_silu, 1)
                if more:
                    c_out((c + 1) * UC, 0)
                    decay_start(c + 1)

            norm_in(0)
            act.wait_ge(setup_pool, 1)
            delta_in(0)
            act.wait_ge(w_in, 16 * NW)
            A(Aneg[:, :], Aneg[:, :], ACT.Exp).then_inc(a_exp, 1)
            xm_out(0)
            c_tiles(0)
            c_out(0, 0)
            act.wait_ge(a_neg, 1)
            decay_start(0)
            with act.Fori(0, NC - 1) as c:
                chunk(c, True)
            chunk(NC - 1, False)

            for c in range(NC):
                act.wait_ge(f_agg, c * NTT + NTT)
                A(sdf[:, NTT * c:NTT * c + NTT], mvf[:, NTT * c:NTT * c + NTT, 1], ACT.Sqrt, bias=EPS).then_inc(f_sd, 1)
            act.wait_ge(r_dif, 1)
            A(er, dif, ACT.Exp).then_inc(r_e, 1)
            for c in range(NC):
                act.wait_ge(w_T, c + 1)
                A(wTs[:, c, :], ups[0:NE, c, :], ACT.Copy).then_inc(w_Ts, 1)
            act.wait_ge(fw_in, 16 * NFW)
            with act.Fori(0, NC) as c:
                for e in range(NE + 1):
                    for k in range(3 if e < NE else 2):
                        n = 3 * e + k
                        act.wait_ge(ag_mm, c * (3 * NE + 2) + n + 1)
                        if n >= 3:
                            act.wait_ge(geglu, c * (3 * NE + 2) + n - 2)
                        bias = be1s[:, e, 3 + k:4 + k] if e < NE else bs1s[:, 2 + k:3 + k]
                        A(gel[:, k, :], gbank(n), ACT.Gelu, bias=bias).then_inc(gelu, 1)
                    if e < NE:
                        act.wait_ge(wb_mm, c * NE + e + 1)
                        if e >= 2:
                            act.wait_ge(act_ok, c * NE + e - 1)
                        A(wbs[:, e % 2, :], mm[:, 1, :], ACT.Copy).then_inc(wb_sb, 1)

        @block.vector
        def _(dve):
            V = nc.vector
            dve.sem_inc(x_mid, 1)
            dve.sem_inc(x_out, 1)
            dve.wait_ge(mod_mm, 1)
            V.tensor_copy(modT[:, :, :].rearrange("p k b -> p (k b)"), mm[:, 0, 0:6 * NB]).then_inc(mod_sb, 1)
            dve.wait_ge(mod_sb, 1)
            sgn, mag = modsg[:, 0, :], modsg[:, 1, :]
            flatm = modT[:, :, :].rearrange("p k b -> p (k b)")
            V.tensor_scalar(sgn, flatm, 0.0, 2.0, ALU.is_ge, ALU.mult).then_inc(gates, 1)
            V.tensor_scalar(mag, flatm, -1.0, None, ALU.mult).then_inc(gates, 1)
            dve.wait_ge(gates, 2)
            V.tensor_scalar(sgn, sgn, -1.0, None, ALU.add).then_inc(gates, 1)
            V.tensor_tensor(mag, mag, flatm, ALU.max).then_inc(gates, 1)
            dve.wait_ge(gates, 4)
            V.tensor_scalar(mag, mag, 0.25, None, ALU.max).then_inc(gates, 1)
            dve.wait_ge(gates, 5)
            V.tensor_tensor(mag, mag, sgn, ALU.mult).then_inc(gates, 1)
            dve.wait_ge(gates, 6)
            for k in (2, 5):
                V.tensor_copy(modT[:, k, :], mag[:, NB * k:NB * k + NB]).then_inc(gates, 1)
            for k in (1, 4):
                V.tensor_scalar(modT[:, k, :], modT[:, k, :], 1.0, None, ALU.add).then_inc(gates, 1)
            dve.wait_ge(gates, 10)

            def bc_copy(vu, b, nth):
                dve.wait_ge(bc_mm, nth)
                V.tensor_tensor(bcs[:, :, :, :].rearrange("p t k n -> p t (k n)"),
                                mm[:, 1, 0:NT * 2 * NS].rearrange("p (t m) -> p t m", t=NT),
                                xm[:, b * NT:(b + 1) * NT, DI:XW], ALU.add).then_inc(m_step, 1)

            def bc_square(vu):
                dve.wait_ge(m_step, vu * 3 + 1)
                V.tensor_tensor(sq[:, :, :, :], bcs[:, :, :, :], bcs[:, :, :, :], ALU.mult).then_inc(m_step, 1)

            def bc_sum(vu):
                dve.wait_ge(m_step, vu * 3 + 2)
                V.tensor_reduce(ss[:, :, :], sq[:, :, :, :], AX.X, ALU.add).then_inc(m_step, 1)

            def bc_floor(vu):
                dve.wait_ge(m_step, vu * 3 + 3)
                V.tensor_scalar(ss[:, :, :], ss[:, :, :], EPS * EPS, None, ALU.max).then_inc(bc_ok, 1)

            def norms_0(c):
                dve.wait_ge(xm_sb, c * 2 + 1)
                V.tensor_copy(bcs[:, :, :, :].rearrange("p t k n -> p t (k n)"), xm[:, 0:NT, DI:XW]).then_inc(m_step, 1)
                bc_square(c * UC)
                bc_sum(c * UC)
                bc_floor(c * UC)

            def inverse(vu, b):
                dve.wait_ge(bc_sd, vu + 1)
                V.reciprocal(rn[:, :, :], sdb[:, :, :]).then_inc(rn_ok, 1)
                dve.wait_ge(rn_ok, vu + 1)
                V.tensor_tensor(Bn[:, b, :, :], bcs[:, :, 0, :], rn[:, :, 0:1].to_broadcast([128, NT, NS]),
                                ALU.mult).then_inc(bn_ok, 1)

            def v_in(xt, b):
                row = slice(b * NT, (b + 1) * NT)
                V.tensor_tensor(v[:, b, :, :], xt, delta[:, row, :], ALU.mult).then_inc(v_ok, 1)

            def xd_in(xt, b):
                V.tensor_tensor(xD[:, b, :, :], xt,
                                Dbc[:, :].rearrange("p (o d) -> p o d", o=1).to_broadcast([128, NT, DI]),
                                ALU.mult).then_inc(xd_ok, 1)

            mixed_x = mm[:, 0, :].rearrange("p (t d) -> p t d", t=NT)

            def v_mixed(vu, b, nth):
                dve.wait_ge(mix_mm, nth)
                v_in(mixed_x, b)

            def stats(w):
                dve.wait_ge(y_t, w + 1)
                for tt in range(NT):
                    V.bn_stats(st[:, tt, :], mm[:, 0, tt * DI:(tt + 1) * DI]).then_inc(l_stat, 1)

            def aggregate(w):
                for tt in range(NT):
                    dve.wait_ge(l_stat, w * 2 + 1 + tt)
                    alone(dve)
                    V.bn_aggr(mv[:, tt, :], st[:, tt, :]).then_inc(l_agg, 1)

            def normalise(w):
                dve.wait_ge(l_sd, w + 1)
                V.reciprocal(rs[:, 0:NT], sd[:, 0:NT]).then_inc(l_rs, 1)
                dve.wait_ge(l_rs, w + 1)
                for tt in range(NT):
                    V.tensor_scalar(nrm[:, tt, :], mm[:, 0, tt * DI:(tt + 1) * DI], mv[:, tt, 0:1], rs[:, tt:tt + 1],
                                    ALU.subtract, ALU.mult).then_inc(l_n, 1)

            def update(w, b, i, last=False):
                V.tensor_scalar(yT[:, b, :, 0], ylast[:, i + 1, b, :] if last else ylast[:, bass.ds(i + 1, 1), b, :].rearrange("p o k -> p (o k)"), 1.0, None, ALU.mult).then_inc(y_head, 1)
                dve.wait_ge(gy_ok, w * 2 + 2)
                if last:
                    dve.wait_ge(y_head, w + 1)
                    V.tensor_scalar(ylast[:, i + 1, b, :], yT[:, b, :, T], 1.0, None, ALU.mult).then_inc(y_tail, 1)
                else:
                    V.scalar_tensor_tensor(yT[:, b, :, 1:T + 1], yT[:, b, :, 1:T + 1], 1.0 - STEP, gy[:, :, :],
                                           ALU.mult, ALU.add).then_inc(y_new, 1)

            def keep(w, b, i, nth):
                dve.wait_ge(y_new, nth)
                V.tensor_scalar(ylast[:, bass.ds(i + 1, 1), b, :].rearrange("p o k -> p (o k)"), yT[:, b, :, T], 1.0, None, ALU.mult).then_inc(y_tail, 1)

            def chain(w, b, updated, kept=lambda: None):
                return [(D_STATS, lambda: stats(w)), (D_AGGR, lambda: aggregate(w)), (D_NORM, lambda: normalise(w)),
                        (D_UPDATE, updated), (D_KEEP, kept)]

            def mixed(vu, b, nth):
                return [(D_COPY, lambda: bc_copy(vu, b, nth)), (D_SQUARE, lambda: bc_square(vu)),
                        (D_SUM, lambda: bc_sum(vu)), (D_FLOOR, lambda: bc_floor(vu)),
                        (D_INVERSE, lambda: inverse(vu, b)), (D_INPUTS, lambda: v_mixed(vu, b, nth)),
                        (D_DX, lambda: xd_in(mixed_x, b))]

            def scans(u, b, i, static, first=None, after=()):
                def car(t0, t1):
                    if static:
                        return hcar[:, i, b, t0:t1]
                    return hcar[:, bass.ds(i, 1), b, t0:t1].rearrange("p o k -> p (o k)")

                def carry(g):
                    dve.wait_ge(scanned, u * 16 + 2 * g + 4)
                    V.tensor_scalar(car(4 * g, 4 * g + 8).rearrange("p (s j) -> p s j", s=2),
                                    hring[:, g % 4:g % 4 + 2, :, T - 1], 1.0, None, ALU.mult).then_inc(carried, 1)

                for g in range(NG):
                    if first is not None and g in (0, 1, 4, 5):
                        dve.wait_ge(decay_ok, first + (4, 8, 0, 0, 12, 16)[g])
                    for k in range(2):
                        dve.wait_ge(u_ok, u * 16 + 2 * g + k + 1)
                        if k == 0 and not (first is not None and g < 4):
                            dve.wait_ge(g_ok, u * 8 + g - 3)
                        if k == 0 and (g in (4, 6) or (g == 2 and first is None)):
                            dve.wait_ge(carried, u * 4 + g // 2 - 1)
                        if first is None and g == 3 and 2 * k + 2 > 4 - OWN:
                            dve.wait_ge(g_own, u)
                        for j in (2 * k, 2 * k + 1):
                            tile = 4 * g + j
                            last = V.tensor_tensor_scan(
                                hring[:, g % 4, j, :], decay[:, tile, b, :],
                                ups[:, (2 * g + k) % 4, (j % 2) * T:(j % 2 + 1) * T],
                                car(tile, tile + 1), ALU.mult, ALU.add)
                            if j % 2:
                                last.then_inc(scanned, 1)
                            if j == 1 and g >= 2 and g % 2 == 0:
                                carry(g - 2)
                            for place, step in after:
                                if place == tile:
                                    step()
                carry(NG - 2)
                dve.wait_ge(crep_ok, u * 2 + 2)
                dve.wait_ge(summed, u * 8 + 4)
                V.tensor_tensor(
                    gring[:, 3, 4 - OWN:4, :], hring[:, 3, 4 - OWN:4, :],
                    crep[:, b, 3:4, :].to_broadcast([128, OWN, T]), ALU.mult).then_inc(g_own, 1)

            coef = log1p_coefficients(9)

            def ln1_stats(c, static):
                x = xmid[:, c, :, :] if static else xmid[:, bass.ds(c, 1), :, :].rearrange("p o k d -> p (o k) d")
                for k in range(NTT):
                    V.bn_stats(st1[:, k, :], x[:, k, :]).then_inc(ln1_stat, 1)
                for k in range(NTT):
                    dve.wait_ge(ln1_stat, c * NTT + k + 1)
                    alone(dve)
                    V.bn_aggr(mv1[:, k, :], st1[:, k, :]).then_inc(ln1_agg, 1)

            def ln1_norm(c, static):
                x = xmid[:, c, :, :] if static else xmid[:, bass.ds(c, 1), :, :].rearrange("p o k d -> p (o k) d")
                dve.wait_ge(ln1_sd, c + 1)
                V.reciprocal(rs1[:, :], sd1[:, :]).then_inc(ln1_rs, 1)
                dve.wait_ge(ln1_rs, c + 1)
                for k in range(NTT):
                    V.tensor_scalar(nx[:, k, :], x[:, k, :], mv1[:, k, 0:1], rs1[:, k:k + 1],
                                    ALU.subtract, ALU.mult).then_inc(ln1_n, 1)

            def ln1_mod(c):
                dve.wait_ge(ln1_T, c + 1)
                for b in range(NB):
                    V.tensor_scalar(hTn[:, b * T:(b + 1) * T], mm[:, 1, b * T:(b + 1) * T], modT[:, 1, b:b + 1],
                                    modT[:, 0, b:b + 1], ALU.mult, ALU.add).then_inc(h_T, 1)

            def keep_h(c):
                dve.wait_ge(h_T, c * 2 + 2)
                V.tensor_scalar(hT[:, :], hTn[:, :], 1.0, None, ALU.mult).then_inc(h_kept, 1)

            def softplus(c, k0, k1):
                for k in range(k0, k1):
                    if k == 0:
                        dve.wait_ge(dt_exp, c + 1)
                        V.tensor_scalar(dpoly, dexp_, coef[-1], None, ALU.mult).then_inc(poly, 1)
                        continue
                    dve.wait_ge(poly, c * 10 + k)
                    if k < 10:
                        V.scalar_tensor_tensor(dpoly, dpoly, coef[9 - k], dexp_, ALU.add, ALU.mult).then_inc(poly, 1)
                    else:
                        dve.wait_ge(dt_relu, c + 1)
                        V.tensor_tensor(delta[:, :, :].rearrange("p k d -> p (k d)"), dpoly, drelu,
                                        ALU.add).then_inc(delta_ok, 1)

            def first_drep(c):
                dve.wait_ge(delta_ok, c + 1)
                for k in range(2):
                    V.tensor_copy(
                        drep(k), delta[:, k, :].rearrange("p (k o d) -> p k o d", k=8, o=1).to_broadcast([128, 8, 4, 32])
                    ).then_inc(drep_d, 1)

            def first_inputs(c):
                v_in(xm[:, 0:NT, 0:DI], 0)
                dve.wait_ge(v_ok, c * UC + 1)
                dve.wait_ge(bn_ok, c * UC + 1)
                for tt in range(NT):
                    last = v_b_at_once(V, 0, 0, tt)
                last.then_inc(quarter_d, 1)
                xd_in(xm[:, 0:NT, 0:DI], 0)

            def residual(c, static):
                x = xmid[:, c, :, :].rearrange("p k d -> p (k d)") if static else \
                    xmid[:, bass.ds(c, 1), :, :].rearrange("p o k d -> p (o k d)")
                dve.wait_ge(o_t, c + 1)
                V.tensor_tensor(x, yps[:, 1, :], x, ALU.add).then_inc(x_mid, 1)

            def f_stats(c):
                dve.wait_ge(x_mid, c + 2)
                for k in range(NTT):
                    V.bn_stats(stf[:, NTT * c + k, :], xmid[:, c, k, :]).then_inc(f_stat, 1)
                for k in range(NTT):
                    dve.wait_ge(f_stat, c * NTT + k + 1)
                    alone(dve)
                    V.bn_aggr(mvf[:, NTT * c + k, :], stf[:, NTT * c + k, :]).then_inc(f_agg, 1)

            def f_norm(c):
                dve.wait_ge(f_sd, c + 1)
                V.reciprocal(rsf[:, NTT * c:NTT * c + NTT], sdf[:, NTT * c:NTT * c + NTT]).then_inc(f_rs, 1)
                dve.wait_ge(f_rs, c + 1)
                for k in range(NTT * c, NTT * c + NTT):
                    V.tensor_scalar(nrmx[:, k, :], xmid[:, c, k % NTT, :], mvf[:, k, 0:1], rsf[:, k:k + 1],
                                    ALU.subtract, ALU.mult).then_inc(f_n, 1)

            def chunk(c, more):
                scans(c * UC, 0, 0, True, first=c * 16,
                      after=mixed(c * UC + 1, 1, c * (UC - 1) + 1))
                with dve.Fori(0, EV - 1) as i:
                    u = c * UC + i * 2
                    n = c * (UC - 2) + i * 2
                    m = c * (UC - 1) + i * 2 + 1

                    def end(w, b, nth):
                        return chain(w, b, lambda: update(w, b, i), lambda: keep(w, b, i, nth))

                    scans(u + 1, 1, i, False, after=end(u, 0, n + 1) + mixed(u + 2, 0, m + 1))
                    scans(u + 2, 0, i + 1, False, after=end(u + 1, 1, n + 2) + mixed(u + 3, 1, m + 2))
                w = c * UC + UC - 2
                if more:
                    ln1_stats(c + 1, False)
                after = chain(w, 0, lambda: update(w, 0, EV - 1, last=True))
                if more:
                    after = [(1, lambda: ln1_norm(c + 1, False)), (5, lambda: ln1_mod(c + 1))] + after
                scans(w + 1, 1, EV - 1, True, after=after)
                if more:
                    softplus(c + 1, 0, S_STATS)
                stats(w + 1)
                aggregate(w + 1)
                if more:
                    softplus(c + 1, S_STATS, S_NORM)
                normalise(w + 1)
                if more:
                    norms_0(c + 1)
                    softplus(c + 1, S_NORM, S_UPDATE)
                    inverse((c + 1) * UC, 0)
                update(w + 1, 1, EV - 1, last=True)
                if more:
                    softplus(c + 1, S_UPDATE, S_SILU)
                if more:
                    first_drep(c + 1)
                dve.wait_ge(z_silu, c * 2 + 2)
                V.tensor_tensor(sT[:, :, :].rearrange("p k (b t) -> p k b t", b=NB),
                                sT[:, :, :].rearrange("p k (b t) -> p k b t", b=NB),
                                yT[:, :, :, 1:T + 1].rearrange("p b k t -> p k b t"), ALU.mult).then_inc(s_ok, 1)
                if more:
                    keep_h(c + 1)
                    first_inputs(c + 1)
                else:
                    for k in range(NC - 1):
                        f_stats(k)
                dve.wait_ge(o_mm, c + 1)
                for b in range(NB):
                    V.tensor_scalar(gated[:, b * T:(b + 1) * T], yps[:, 0, b * T:(b + 1) * T], modT[:, 2, b:b + 1],
                                    None, ALU.mult).then_inc(o_sc, 1)
                residual(c, not more)
                if not more:
                    for k in range(NC - 1):
                        f_norm(k)

            ln1_stats(0, True)
            ln1_norm(0, True)
            ln1_mod(0)
            keep_h(0)
            dve.wait_ge(w_second, 16 * N_SECOND)
            dve.wait_ge(w_in, 16 * NW)
            V.tensor_scalar(imix[:, :, :], wxm[:, :, 0:DI], -1.0, None, ALU.mult).then_inc(setup_dve, 1)
            dve.wait_ge(setup_dve, 1)
            for k in range(2):
                V.tensor_tensor(imix[:, k, 128 * k:128 * k + 128], imix[:, k, 128 * k:128 * k + 128], ident[:, :],
                                ALU.add).then_inc(setup_dve, 1)
            V.tensor_scalar(damp[:, :, :], chan[:, :, :], STEP, None, ALU.mult).then_inc(setup_dve, 1)
            softplus(0, 0, 2)
            dve.wait_ge(a_exp, 1)
            V.tensor_scalar(Aneg[:, :], Aneg[:, :], -1.0, None, ALU.mult).then_inc(a_neg, 1)
            norms_0(0)
            softplus(0, 2, 6)
            inverse(0, 0)
            softplus(0, 6, 11)
            first_drep(0)
            first_inputs(0)
            dve.wait_ge(x_in, 16 * N_X)
            with dve.Fori(0, NC - 1) as c:
                chunk(c, True)
            chunk(NC - 1, False)

            f_stats(NC - 1)
            f_norm(NC - 1)
            for c in range(NC):
                dve.wait_ge(f_T, c + 1)
                for b in range(NB):
                    V.tensor_scalar(hTf[:, c, b * T:(b + 1) * T], ups[:, c, b * T:(b + 1) * T], modT[:, 4, b:b + 1],
                                    modT[:, 3, b:b + 1], ALU.mult, ALU.add).then_inc(f_h, 1)
            dve.wait_ge(r_mm, 1)
            V.tensor_tensor(lg, mm[:, 0, 0:NRT * NE].rearrange("p (x e) -> p x e", x=NRT),
                            brow[:, :].rearrange("p (o e) -> p o e", o=1).to_broadcast([128, NRT, NE]), ALU.add).then_inc(r_l, 1)
            dve.wait_ge(r_l, 1)
            V.tensor_scalar(lg, lg, 1.0 / TAU, None, ALU.mult).then_inc(r_l, 1)
            dve.wait_ge(r_l, 2)
            alone(dve)
            for k in range(NRT):
                V.max(top[:, k, :], lg[:, k, :]).then_inc(r_top, 1)
            dve.wait_ge(r_top, NRT)
            alone(dve)
            for k in range(NRT):
                V.max_index(idx[:, k, :].bitcast(U32), top[:, k, :], lg[:, k, :]).then_inc(r_idx, 1)
            V.tensor_tensor(dif, top[:, :, 1], top[:, :, 0], ALU.subtract).then_inc(r_dif, 1)
            dve.wait_ge(r_idx, NRT)
            V.tensor_copy(idf, idx.bitcast(U32)).then_inc(r_p, 1)
            dve.wait_ge(r_e, 1)
            V.tensor_scalar(den, er, 1.0, None, ALU.add).then_inc(r_p, 1)
            dve.wait_ge(r_p, 2)
            V.reciprocal(p1, den).then_inc(r_p, 1)
            dve.wait_ge(r_p, 3)
            V.tensor_tensor(p2, er, p1, ALU.mult).then_inc(r_p, 1)
            dve.wait_ge(r_p, 4)
            wide = [128, NRT, NE]
            number = iota[:, :].rearrange("p (o e) -> p o e", o=1).to_broadcast(wide)
            for m, (dst, p) in enumerate(((wt, p1), (oh, p2))):
                V.tensor_tensor(dst, number, idf[:, :, m:m + 1].to_broadcast(wide), ALU.is_equal).then_inc(r_w, 1)
            for m, (dst, p) in enumerate(((wt, p1), (oh, p2))):
                dve.wait_ge(r_w, m + 1)
                V.tensor_tensor(dst, dst, p.rearrange("p (x o) -> p x o", o=1).to_broadcast(wide), ALU.mult).then_inc(r_w, 1)
            dve.wait_ge(r_w, 4)
            V.tensor_tensor(wt, wt, oh, ALU.add).then_inc(r_w, 1)
            dve.wait_ge(r_w, 5)
            with dve.Fori(0, NC) as c:
                dve.wait_ge(x_out, c + 1)
                V.tensor_scalar(wtc, wt[:, bass.ds(c * NTT, NTT), :], 1.0, None, ALU.mult).then_inc(w_c, 1)
                for e in range(NE + 1):
                    for k in range(3 if e < NE else 2):
                        n = 3 * e + k
                        dve.wait_ge(gelu, c * (3 * NE + 2) + n + 1)
                        if e >= 2 and e < NE and k == 0:
                            dve.wait_ge(act_ok, c * NE + e - 1)
                        bias = be1s[:, e, k:k + 1] if e < NE else bs1s[:, k:k + 1]
                        dst = geg(e)[:, k, :] if e < NE else shg[:, k, :]
                        V.scalar_tensor_tensor(dst, abank(n), bias, gel[:, k, :], ALU.add, ALU.mult).then_inc(geglu, 1)
                dve.wait_ge(f_mm, c + 1)
                for b in range(NB):
                    V.tensor_scalar(xT[:, 0, b * T:(b + 1) * T], mm[:, 0, b * T:(b + 1) * T], bs2s[:, 0:1],
                                    modT[:, 5, b:b + 1], ALU.add, ALU.mult).then_inc(f_sc, 1)
                dve.wait_ge(f_t, c + 1)
                xo = xmid[:, bass.ds(c, 1), :, :].rearrange("p o k d -> p (o k d)")
                V.tensor_tensor(xo, mm[:, 1, :], xo, ALU.add).then_inc(x_out, 1)

        @block.tensor
        def _(pe):
            MM = nc.tensor.matmul
            TR = nc.tensor.transpose
            pe.wait_ge(w_first, 16 * N_FIRST)
            pe.wait_ge(silu_c, 1)
            for k in range(6):
                last = MM(mm[:, 0, NB * k:NB * k + NB], wmods[:, DM * k:DM * k + DM], silc[:, :], start=True, stop=True)
            last.then_inc(mod_mm, 1)

            def mix_x(b):
                for tt in range(NT):
                    MM(mm[:, 0, tt * DI:(tt + 1) * DI], ident[:, :], xm[:, b * NT + tt, 0:DI], start=(tt == 0),
                       stop=False, skip_group_check=True)

            def mix_y(vu, b):
                for tt in range(NT):
                    for k in range(2):
                        last = MM(mm[:, 1, 2 * NS * tt:2 * NS * (tt + 1)], yT[:, b, k, 128 * tt:128 * tt + 128],
                                  wbc[:, k, :], start=(tt == 0 and k == 0), stop=(k == 1), skip_group_check=True)
                last.then_inc(bc_mm, 1)
                for tt in range(NT):
                    for k in range(2):
                        last = MM(mm[:, 0, tt * DI:(tt + 1) * DI], yT[:, b, k, 1 + 128 * tt:129 + 128 * tt],
                                  imix[:, k, :], start=False, stop=(k == 1), skip_group_check=True)
                last.then_inc(mix_mm, 1)

            def mix(vu, b):
                mix_x(b)
                mix_y(vu, b)

            def rep_c(vu, b, first=False):
                pe.wait_ge(cexp_ok, vu * 2 + 2)
                if not first:
                    pe.wait_ge(v_ok, vu + 1)
                    pe.wait_ge(xd_ok, vu + 1)
                for q in range(4):
                    for tt in range(NT):
                        last = TR(mm[:, q // 2, (q % 2) * T + 128 * tt:(q % 2) * T + 128 * tt + 128],
                                  cexp[:, tt, 4 * q:4 * q + 4, :].rearrange("p n d -> p (n d)"), ident[:, :])
                last.then_inc(crep_mm, 1)

            def start_y(u, b, first=None):
                if first is None:
                    pe.wait_ge(y_ev, u * 2)
                else:
                    pe.wait_ge(x_mid, first + 1)
                pe.wait_ge(xd_ok, u + 1)
                for blk in range(2):
                    for tt in range(NT):
                        MM(yps[:, blk, 128 * tt:128 * tt + 128], xD[:, b, tt, 128 * blk:128 * blk + 128], ident[:, :],
                           start=(tt == 0), stop=False, skip_group_check=True)

            def reduce(u, g):
                pe.wait_ge(g_ok, u * 8 + g + 1)
                if g == NG - 1:
                    pe.wait_ge(g_own, u + 1)
                for j in range(4):
                    last = MM(yps[32 * j:32 * j + 32, g % 2, 0:T], sel[:, :], gring[:, g % 4, j, :],
                              start=False, stop=(g // 2 == 3), skip_group_check=True)
                last.then_inc(summed, 1)

            def inputs(u, g, first=None, between=()):
                q, blk = g // 2, g % 2
                for k in range(2):
                    if k == 0 and blk == 0:
                        if first is None or q == 3:
                            pe.wait_ge(quarter, u * 4 + q + 1)
                        elif q == 0:
                            pe.wait_ge(quarter_d, first + 1)
                        else:
                            pe.wait_ge(quarter_p, first * 2 + q)
                    if first is not None and g < 2:
                        pe.wait_ge(decay_ok, first * 16 + 1 + 2 * g + k)
                    else:
                        pe.wait_ge(scanned, u * 16 + 2 * g + k - 3)
                    for j in (2 * k, 2 * k + 1):
                        for tt in range(NT):
                            last = TR(ups[:, (2 * g + k) % 4, (j % 2) * T + 128 * tt:(j % 2) * T + 128 * tt + 128],
                                      U[:, q, tt, 4 * blk + j, :], ident[:, :])
                    last.then_inc(u_ok, 1)
                    if k == 0:
                        for f in between:
                            f()

            def back_y(w):
                pe.wait_ge(y_ev, w * 2 + 2)
                for tt in range(NT):
                    for blk in range(2):
                        last = TR(mm[:, 0, tt * DI + 128 * blk:tt * DI + 128 * blk + 128],
                                  yTs[:, blk, 128 * tt:128 * tt + 128], ident[:, :])
                last.then_inc(y_t, 1)

            def forth_n(w):
                pe.wait_ge(l_n, w * 2 + 2)
                for blk in range(2):
                    for tt in range(NT):
                        last = TR(mm[:, 1, blk * T + 128 * tt:blk * T + 128 * tt + 128],
                                  nrm[:, tt, 128 * blk:128 * blk + 128], ident[:, :])
                last.then_inc(n_T, 1)

            def slot(u, b, after, first=None, prev=True):
                for g in range(NG):
                    inputs(u, g, first, after.get((g, 0), ()))
                    for f in after.get((g, 1), ()):
                        f()
                    if g < 2:
                        if prev:
                            reduce(u - 1, 6 + g)
                    else:
                        if g == 2:
                            start_y(u, b, first)
                        reduce(u, g - 2)
                    for f in after.get((g, 2), ()):
                        f()

            def h_in(c):
                pe.wait_ge(ln1_n, c * NTT + NTT)
                for k in range(NTT):
                    last = TR(mm[:, 1, 128 * k:128 * k + 128], nx[:, k, :], ident[:, :])
                last.then_inc(ln1_T, 1)

            def x_in_T(c):
                pe.wait_ge(h_T, c * 2 + 2)
                for k in range(2):
                    MM(mm[:, k, :], winT[:, 128 * k:128 * k + 128], hTn[:, :], start=True, stop=True).then_inc(x_mm, 1)

            def delta_low(c):
                pe.wait_ge(x_T, c * 2 + 2)
                for k in range(2):
                    last = MM(mm[0:RK, 1, :], wxdt[:, k, :], xT[:, k, :], start=(k == 0), stop=(k == 1))
                last.then_inc(dl_mm, 1)

            def delta_up(c):
                pe.wait_ge(dl_sb, c + 1)
                for k in range(NTT):
                    last = MM(mm[:, k // 2, (k % 2) * DI:(k % 2 + 1) * DI], dlow[:, 128 * k:128 * k + 128],
                              wdt9[:, :], start=True, stop=True)
                last.then_inc(dt_mm, 1)

            def x_mixed(c):
                for k in range(NTT):
                    for m in range(2):
                        last = MM(ups[:, k, 0:XW], xT[:, m, 128 * k:128 * k + 128], wxm[:, m, :], start=(m == 0), stop=(m == 1))
                last.then_inc(xm_mm, 1)

            def delta_bank(c, n):
                if n == 0:
                    pe.wait_ge(drep_d, c * 2 + 2)
                    pe.wait_ge(drep_a, c * 2 + 2)
                    pe.wait_ge(xm_sb, c * 2 + 2)
                if n == 4:
                    pe.wait_ge(crep_ok, c * UC * 2 + 2)
                if n >= 6:
                    pe.wait_ge(decay_ok, c * 16 + n - 1)
                for x in range(NTT):
                    dst = ups[:, n, 128 * x:128 * x + 128] if n < 4 else mm[:, n % 2, 128 * x:128 * x + 128]
                    last = TR(dst, drep(x)[:, n % 8, :, :].rearrange("p n d -> p (n d)"), ident[:, :])
                last.then_inc(dbank, 1)

            def chunk(c, more):
                def delta_banks(*ns):
                    def go():
                        for n in ns:
                            delta_bank(c, n)
                    return go

                def mix1():
                    pe.wait_ge(decay_ok, c * 16 + 16)
                    pe.wait_ge(y_zero, c + 1)
                    pe.wait_ge(setup_dve, 4)
                    mix(c * UC + 1, 1)
                slot(c * UC, 0, {(0, 2): [delta_banks(6)], (1, 0): [delta_banks(7)], (1, 2): [delta_banks(8, 9, 10)],
                                 (2, 0): [delta_banks(11)], (3, 0): [delta_banks(12, 13)], (3, 1): [delta_banks(14)],
                                 (3, 2): [delta_banks(15)], (4, 2): [mix1],
                                 P_REP: [lambda: rep_c(c * UC + 1, 1)]}, first=c, prev=False)
                with pe.Fori(0, EV - 1) as i:
                    u = c * UC + i * 2
                    n = c * (UC - 2) + i * 2

                    def chain(w, b, nth):
                        def back():
                            pe.wait_ge(crep_ok, w * 2 + 4)
                            back_y(w)

                        def forth():
                            forth_n(w)
                            mix_x(b)

                        def again():
                            pe.wait_ge(gy_ok, w * 2 + 2)
                            pe.wait_ge(y_new, nth)
                            pe.wait_ge(y_head, w + 1)
                            mix_y(w + 2, b)
                        return {P_BACK: [back], P_FORTH: [forth], P_MIX: [again], P_REP: [lambda: rep_c(w + 2, b)]}

                    slot(u + 1, 1, chain(u, 0, n + 1))
                    slot(u + 2, 0, chain(u + 1, 1, n + 2))
                w = c * UC + UC - 2

                def back_last():
                    pe.wait_ge(crep_ok, w * 2 + 4)
                    back_y(w)
                after = {P_BACK: [back_last], P_FORTH: [lambda: forth_n(w)]}
                if more:
                    n = c + 1

                    def h_first():
                        pe.wait_ge(crep_ok, w * 2 + 4)
                        h_in(n)

                    def forth_after():
                        pe.wait_ge(h_T, n * 2 + 2)
                        forth_n(w)

                    def x_after():
                        pe.wait_ge(gy_ok, w * 2 + 2)
                        x_in_T(n)
                    after = {(0, 2): [h_first], P_BACK: [back_last], P_FORTH: [forth_after], (4, 1): [x_after],
                             (5, 1): [lambda: delta_low(n)], (6, 1): [lambda: delta_up(n)]}
                slot(w + 1, 1, after)
                reduce(w + 1, 6)
                if more:
                    pe.wait_ge(scanned, (w + 1) * 16 + 16)
                    x_mixed(n)
                reduce(w + 1, 7)
                if more:
                    pe.wait_ge(dt_relu, n + 1)
                else:
                    pe.wait_ge(gy_ok, w * 2 + 2)
                back_y(w + 1)
                pe.wait_ge(x_in, 16 * N_X)
                pe.wait_ge(h_kept, c + 1)
                pe.wait_ge(gy_ok, w * 2 + 2)
                pe.wait_ge(y_head, w + 1)

                def z_part(m, b):
                    for k in range(2):
                        last = MM(yps[:, m, b * T:(b + 1) * T], wzy[:, k, 128 * m:128 * m + 128], yT[:, b, k, 0:T],
                                  start=False, stop=(b == 1 and k == 1), skip_group_check=True)
                    return last
                for m in range(2):
                    MM(yps[:, m, :], winT[:, DI + 128 * m:DI + 128 * m + 128], hT[:, :], start=True, stop=False,
                       skip_group_check=True)
                z_part(0, 0)
                forth_n(w + 1)
                z_part(1, 0)
                pe.wait_ge(gy_ok, w * 2 + 4)
                pe.wait_ge(y_head, w + 2)
                for m in range(2):
                    z_part(m, 1).then_inc(z_mm, 1)
                if more:
                    rep_c(n * UC, 0, first=True)
                if more:
                    for k in range(4):
                        delta_bank(n, k)
                pe.wait_ge(s_ok, c + 1)
                for m in range(2):
                    last = MM(yps[:, 0, :], wout[:, m, :], sT[:, m, :], start=(m == 0), stop=(m == 1))
                last.then_inc(o_mm, 1)
                if more:
                    for k in range(4, 6):
                        delta_bank(n, k)
                pe.wait_ge(o_sc, c * 2 + 2)
                for k in range(NTT):
                    last = TR(yps[:, 1, 128 * k:128 * k + 128], gated[:, 128 * k:128 * k + 128], ident[:, :])
                last.then_inc(o_t, 1)

            pe.wait_ge(gates, 10)
            h_in(0)
            pe.wait_ge(w_second, 16 * N_SECOND)
            x_in_T(0)
            delta_low(0)
            delta_up(0)
            x_mixed(0)
            pe.wait_ge(dt_relu, 1)
            rep_c(0, 0, first=True)
            pe.wait_ge(w_in, 16 * NW)
            for k in range(6):
                delta_bank(0, k)
            with pe.Fori(0, NC - 1) as c:
                chunk(c, True)
            chunk(NC - 1, False)

            for c in range(NC):
                pe.wait_ge(f_n, c * NTT + NTT)
                for k in range(NTT):
                    last = TR(ups[:, c, 128 * k:128 * k + 128], nrmx[:, NTT * c + k, :], ident[:, :])
                last.then_inc(f_T, 1)
            for c in range(NC):
                pe.wait_ge(f_h, c * 2 + 2)
                for k in range(NTT):
                    x = NTT * c + k
                    last = MM(mm[:, 0, NE * x:NE * x + NE], hTf[:, c, 128 * k:128 * k + 128], wr[:, :], start=True, stop=True)
            last.then_inc(r_mm, 1)
            pe.wait_ge(r_w, 5)
            for c in range(NC):
                for k in range(NTT):
                    last = TR(ups[0:NE, c, 128 * k:128 * k + 128], wt[:, NTT * c + k, :], ident[:, :])
                last.then_inc(w_T, 1)
            pe.wait_ge(fw_in, 16 * NFW)
            pe.wait_ge(w_Ts, NC)
            pe.wait_ge(x_mid, NC + 1)
            with pe.Fori(0, NC) as c:
                ht = hTf[:, bass.ds(c, 1), :].rearrange("p o t -> p (o t)")
                NN = 3 * NE + 2

                def up(e):
                    for k in range(3 if e < NE else 2):
                        n = 3 * e + k
                        if n >= 3:
                            pe.wait_ge(geglu, c * NN + n - 2)
                        wa = we1[:, e, 128 * k:128 * k + 128] if e < NE else ws1[:, 128 * k:128 * k + 128]
                        wg = we1[:, e, HR + 128 * k:HR + 128 * k + 128] if e < NE else \
                            ws1[:, HS + 128 * k:HS + 128 * k + 128]
                        MM(abank(n), wa, ht, start=True, stop=True)
                        MM(gbank(n), wg, ht, start=True, stop=True).then_inc(ag_mm, 1)

                def dn(e):
                    if e < NE:
                        pe.wait_ge(act_ok, c * NE + e + 1)
                        for k in range(3):
                            last = MM(mm[:, 0, :], we2[:, e, k, :], actw(e)[:, k, :], start=False, stop=False,
                                      skip_group_check=True)
                    else:
                        pe.wait_ge(geglu, c * NN + NN)
                        for k in range(2):
                            last = MM(mm[:, 0, :], ws2[:, k, :], shg[:, k, :], start=False, stop=(k == 1),
                                      skip_group_check=True)
                    last.then_inc(down, 1)
                    if e == NE:
                        return last

                for e in range(NE + 1):
                    up(e)
                    if e < NE:
                        if e == 0:
                            pe.wait_ge(x_out, c + 1)
                            pe.wait_ge(w_c, c + 1)
                        else:
                            pe.wait_ge(wb_sb, c * NE + e)
                        for k in range(NTT):
                            last = TR(mm[:, 1, 128 * k:128 * k + 128], wtc[:, k, e:e + 1].to_broadcast([128, 128]),
                                      ident[:, :])
                        last.then_inc(wb_mm, 1)
                    if e == 0:
                        MM(mm[:, 0, :], be2s[:, :], wTs[:, bass.ds(c, 1), :].rearrange("p o t -> p (o t)"), start=True,
                           stop=False, skip_group_check=True)
                    if e >= 1:
                        dn(e - 1)
                dn(NE)
                pe.wait_ge(down, c * (NE + 1) + NE + 1)
                pe.sem_inc(f_mm, 1)
                pe.wait_ge(f_sc, c * 2 + 2)
                for k in range(NTT):
                    last = TR(mm[:, 1, 128 * k:128 * k + 128], xT[:, 0, 128 * k:128 * k + 128], ident[:, :])
                last.then_inc(f_t, 1)


_SHAPE = (NB, L, DM)


def kernel(**inputs):
    import numpy as _np
    import concourse.bacc as _bacc
    from concourse import mybir as _mybir
    from concourse.bass_utils import run_bass_kernel_spmd as _run

    a = {k[3:]: _np.asarray(x) for k, x in inputs.items()}
    eye = _np.eye(128, dtype=_np.float32)
    consts = _np.concatenate([eye, _np.tile(_np.eye(32, dtype=_np.float32), (4, 1)),
                              _np.tile(_np.arange(NE, dtype=_np.float32), (128, 1))], axis=1)
    lay = dict(
        hidden=a["attn_hidden_states"], WinT=a["attn_W_in"].T, WxT=a["attn_W_x"].T,
        Wdt9=_np.concatenate([a["attn_W_dt"].T, a["attn_b_dt"][None, :]], axis=0),
        AlogS=a["attn_A_log"].reshape(2, 4, 32, 4, 4).transpose(4, 2, 3, 0, 1).reshape(128, NTILE),
        WbcT=a["attn_W_bc"].T, WzyT=a["attn_W_zy"].T, WmixT=a["attn_W_mix"].T,
        chanT=_np.stack([a["attn_ln_gamma"], a["attn_ln_beta"], a["attn_D"]], axis=1),
        WoutT=a["attn_W_out"].T,
        Ws1=a["ffn_Ws1"], bs1T=a["ffn_bs1"].reshape(-1, 128).T, Ws2=a["ffn_Ws2"], bs2T=a["ffn_bs2"][:, None],
        We1=a["ffn_We1"], be1T=a["ffn_be1"].reshape(-1, 128).T, We2=a["ffn_We2"], be2=a["ffn_be2"],
        Wr=a["ffn_Wr"], br=a["ffn_br"][None, :], cT=a["c"].T, wmod=a["wmod"], consts=consts)
    nc = _bacc.Bacc("TRN2", target_bir_lowering=False, num_devices=1)
    arrays, args = {}, []
    for name, x in lay.items():
        x = _np.ascontiguousarray(x)
        arrays[f"in_{name}"] = x
        args.append(nc.dram_tensor(f"in_{name}", x.shape, _mybir.dt.from_np(x.dtype), kind="ExternalInput").ap())
    args.append(nc.dram_tensor("out_0", _SHAPE, _mybir.dt.float32, kind="ExternalOutput").ap())
    adaln_block_kernel(nc, *args)
    r = _run(nc, [arrays], core_ids=[0])
    return r.results[0]["out_0"]
```
